# Optimizing a Trainium2 kernel written in Bass

```python
import numpy as np
import jax
import jax.numpy as jnp

def _softmax(x, axis=-1):
    return jax.nn.softmax(x, axis=axis)

def _gelu(x):
    return jax.nn.gelu(x, approximate=True)

def _silu(x):
    return jax.nn.silu(x)

def _sigmoid(x):
    return jax.nn.sigmoid(x)

def _layernorm(x, axis=-1, eps=1e-05):
    m = jnp.mean(x, axis=axis, keepdims=True)
    v = jnp.var(x, axis=axis, keepdims=True)
    return (x - m) / jnp.sqrt(v + eps)

def _scatter_add(tgt, idx, src, axis=0):
    return tgt.at[idx].add(src)

def _segment_sum(src, seg, n):
    return jax.ops.segment_sum(src, seg, n)
kernel_name = 'mk_recurrent_d2_jaxref_r8_9f4800'

def setup_inputs(seed: int=0):
    np.random.seed(seed)
    _w = jnp.asarray

    def _L0_attn_setup():
        import jax, jax.numpy as jnp
        import numpy as np
        D_MODEL = 128
        NUM_HEADS = 16
        D_K = D_MODEL // NUM_HEADS
        ROPE_THETA = 10000.0
        MAX_SEQ_LEN = 256

        def _rope_tables():
            dim_index = jnp.arange(D_K // 2, dtype=jnp.float32)
            pos = jnp.arange(MAX_SEQ_LEN, dtype=jnp.float32)
            theta_inv = ROPE_THETA ** (-2.0 * dim_index / D_K)
            ang = pos[:, None] * theta_inv[None, :]
            return (jnp.sin(ang), jnp.cos(ang))

        def _apply_rope(x, positions, sin, cos):
            s = sin[positions]
            c = cos[positions]
            x_even = x[..., ::2]
            x_odd = x[..., 1::2]
            y_even = x_even * c - x_odd * s
            y_odd = x_even * s + x_odd * c
            y = jnp.stack([y_even, y_odd], axis=-1)
            return y.reshape(x.shape)
        key = jax.random.key(seed)
        k0, k1, k2, k3, k4 = jax.random.split(key, 5)
        std = np.sqrt(2.0 / (D_MODEL + D_MODEL))
        in_features = jax.random.normal(k0, (2, 256, D_MODEL), dtype=jnp.float32)
        W_q = jax.random.normal(k1, (D_MODEL, D_MODEL), dtype=jnp.float32) * std
        W_k = jax.random.normal(k2, (D_MODEL, D_MODEL), dtype=jnp.float32) * std
        W_v = jax.random.normal(k3, (D_MODEL, D_MODEL), dtype=jnp.float32) * std
        W_o = jax.random.normal(k4, (D_MODEL, D_MODEL), dtype=jnp.float32) * std
        return {'in_features': in_features, 'W_q': W_q, 'W_k': W_k, 'W_v': W_v, 'W_o': W_o}
    _L0_attn_in = _L0_attn_setup()

    def _L0_ffn_setup():
        import jax, jax.numpy as jnp
        import numpy as np
        LORA_DIM = 16
        LORA_TOKEN_INDEX = 1
        B, S, D, H = (4, 256, 128, 512)
        key = jax.random.key(seed)
        ks = jax.random.split(key, 6)
        x = jax.random.normal(ks[0], (B, S, D), dtype=jnp.float32)
        W1 = jax.random.normal(ks[1], (H, D), dtype=jnp.float32) * 0.02
        b1 = jnp.zeros((H,), dtype=jnp.float32)
        W2 = jax.random.normal(ks[2], (D, H), dtype=jnp.float32) * 0.02
        b2 = jnp.zeros((D,), dtype=jnp.float32)
        scale = jnp.asarray(0.001, dtype=jnp.float32)
        return {'x': x, 'W1': W1, 'b1': b1, 'W2': W2, 'b2': b2, 'scale': scale}
    _L0_ffn_in = _L0_ffn_setup()

    def _L1_attn_setup():
        import jax, jax.numpy as jnp
        import numpy as np
        B, S, E, H = (2, 256, 128, 16)
        D = E // H
        EPS = 1e-06

        def _angle_decay():
            a = 1.0 / 10000.0 ** jnp.linspace(0.0, 1.0, D // 2)
            angle = jnp.repeat(a, 2)
            decay = jnp.log(1.0 - 2.0 ** (-5.0 - jnp.arange(H, dtype=jnp.float32)))
            return (angle, decay)

        def _rel_pos(slen):
            angle, decay = _angle_decay()
            idx = jnp.arange(slen, dtype=jnp.float32)
            sin = jnp.sin(idx[:, None] * angle[None, :])
            cos = jnp.cos(idx[:, None] * angle[None, :])
            diff = idx[:, None] - idx[None, :]
            tril = diff >= 0
            masked = jnp.where(tril, diff, jnp.inf)
            mask = jnp.exp(masked * decay[:, None, None])
            mask = jnp.nan_to_num(mask)
            mask = mask / jnp.sqrt(jnp.sum(mask, axis=-1, keepdims=True))
            return (sin, cos, mask)

        def _rotate_every_two(x):
            x1 = x[..., ::2]
            x2 = x[..., 1::2]
            return jnp.stack((-x2, x1), axis=-1).reshape(x.shape)

        def _theta_shift(x, sin, cos):
            return x * cos + _rotate_every_two(x) * sin
        key = jax.random.key(seed)
        ks = jax.random.split(key, 5)
        scale = 1.0 / np.sqrt(E)
        return {'x': jax.random.normal(ks[0], (B, S, E), dtype=jnp.float32), 'Wq': jax.random.normal(ks[1], (E, E), dtype=jnp.float32) * scale, 'Wk': jax.random.normal(ks[2], (E, E), dtype=jnp.float32) * scale, 'Wv': jax.random.normal(ks[3], (E, E), dtype=jnp.float32) * scale, 'Wg': jax.random.normal(ks[4], (E, E), dtype=jnp.float32) * scale}
    _L1_attn_in = _L1_attn_setup()

    def _L1_ffn_setup():
        import jax, jax.numpy as jnp
        import numpy as np
        B, T, C = (8, 256, 128)
        E, K = (8, 2)
        H = 4 * C
        CAP_FACTOR = 1.2
        EPS = 1e-09
        key = jax.random.key(seed)
        ks = jax.random.split(key, 6)
        x = jax.random.normal(ks[0], (B, T, C), dtype=jnp.float32)
        router_w = jax.random.normal(ks[1], (E, C), dtype=jnp.float32) * 0.02
        router_b = jnp.zeros((E,), dtype=jnp.float32)
        fc1_w = jax.random.normal(ks[2], (E, H, C), dtype=jnp.float32) * (1.0 / np.sqrt(C))
        fc1_b = jnp.zeros((E, H), dtype=jnp.float32)
        fc2_w = jax.random.normal(ks[3], (E, C, H), dtype=jnp.float32) * (1.0 / np.sqrt(H))
        fc2_b = jnp.zeros((E, C), dtype=jnp.float32)
        layer_scale = jnp.full((E, C), 0.1, dtype=jnp.float32)
        return {'x': x, 'router_w': router_w, 'router_b': router_b, 'fc1_w': fc1_w, 'fc1_b': fc1_b, 'fc2_w': fc2_w, 'fc2_b': fc2_b, 'layer_scale': layer_scale}
    _L1_ffn_in = _L1_ffn_setup()
    _d = {'L0_attn_in_features': _L0_attn_in['in_features'], 'L0_attn_W_q': _L0_attn_in['W_q'], 'L0_attn_W_k': _L0_attn_in['W_k'], 'L0_attn_W_v': _L0_attn_in['W_v'], 'L0_attn_W_o': _L0_attn_in['W_o'], 'L0_ffn_W1': _L0_ffn_in['W1'], 'L0_ffn_b1': _L0_ffn_in['b1'], 'L0_ffn_W2': _L0_ffn_in['W2'], 'L0_ffn_b2': _L0_ffn_in['b2'], 'L0_ffn_scale': _L0_ffn_in['scale'], 'L1_attn_Wq': _L1_attn_in['Wq'], 'L1_attn_Wk': _L1_attn_in['Wk'], 'L1_attn_Wv': _L1_attn_in['Wv'], 'L1_attn_Wg': _L1_attn_in['Wg'], 'L1_ffn_router_w': _L1_ffn_in['router_w'], 'L1_ffn_router_b': _L1_ffn_in['router_b'], 'L1_ffn_fc1_w': _L1_ffn_in['fc1_w'], 'L1_ffn_fc1_b': _L1_ffn_in['fc1_b'], 'L1_ffn_fc2_w': _L1_ffn_in['fc2_w'], 'L1_ffn_fc2_b': _L1_ffn_in['fc2_b'], 'L1_ffn_layer_scale': _L1_ffn_in['layer_scale']}
    _x0 = _d['L0_attn_in_features']
    _d['L0_attn_in_features'] = jax.random.normal(jax.random.fold_in(jax.random.key(seed), 1), (4, 1024, 128), dtype=_x0.dtype)
    del _x0
    return _d

def reference(L0_attn_in_features, L0_attn_W_q, L0_attn_W_k, L0_attn_W_v, L0_attn_W_o, L0_ffn_W1, L0_ffn_b1, L0_ffn_W2, L0_ffn_b2, L0_ffn_scale, L1_attn_Wq, L1_attn_Wk, L1_attn_Wv, L1_attn_Wg, L1_ffn_router_w, L1_ffn_router_b, L1_ffn_fc1_w, L1_ffn_fc1_b, L1_ffn_fc2_w, L1_ffn_fc2_b, L1_ffn_layer_scale):

    def _L0_attn_ref(in_features, W_q, W_k, W_v, W_o):
        import jax, jax.numpy as jnp
        import numpy as np
        D_MODEL = 128
        NUM_HEADS = 16
        D_K = D_MODEL // NUM_HEADS
        ROPE_THETA = 10000.0
        MAX_SEQ_LEN = 256

        def _rope_tables():
            dim_index = jnp.arange(D_K // 2, dtype=jnp.float32)
            pos = jnp.arange(MAX_SEQ_LEN, dtype=jnp.float32)
            theta_inv = ROPE_THETA ** (-2.0 * dim_index / D_K)
            ang = pos[:, None] * theta_inv[None, :]
            return (jnp.sin(ang), jnp.cos(ang))

        def _apply_rope(x, positions, sin, cos):
            s = sin[positions]
            c = cos[positions]
            x_even = x[..., ::2]
            x_odd = x[..., 1::2]
            y_even = x_even * c - x_odd * s
            y_odd = x_even * s + x_odd * c
            y = jnp.stack([y_even, y_odd], axis=-1)
            return y.reshape(x.shape)
        B, S, _ = in_features.shape
        sin, cos = _rope_tables()
        positions = jnp.arange(S)

        def proj(W):
            y = jnp.einsum('bsd,od->bso', in_features, W)
            return y.reshape(B, S, NUM_HEADS, D_K).transpose(0, 2, 1, 3)
        Q = _apply_rope(proj(W_q), positions, sin, cos)
        K = _apply_rope(proj(W_k), positions, sin, cos)
        V = proj(W_v)
        scores = jnp.einsum('bhnd,bhmd->bhnm', Q, K) / jnp.sqrt(jnp.float32(D_K))
        causal = jnp.tril(jnp.ones((S, S), dtype=bool))
        scores = jnp.where(causal[None, None], scores, -jnp.inf)
        attn = jax.nn.softmax(scores, axis=-1)
        head = jnp.einsum('bhnm,bhmd->bhnd', attn, V)
        head = head.transpose(0, 2, 1, 3).reshape(B, S, D_MODEL)
        return jnp.einsum('bso,do->bsd', head, W_o.T.T) if False else jnp.einsum('bsi,oi->bso', head, W_o)

    def _L0_ffn_ref(x, W1, b1, W2, b2, scale):
        import jax, jax.numpy as jnp
        import numpy as np
        LORA_DIM = 16
        LORA_TOKEN_INDEX = 1
        B, S, D, H = (4, 256, 128, 512)
        Bx, Sx, Dx = x.shape
        Hx = W1.shape[0]
        lt = jax.lax.dynamic_slice_in_dim(x, LORA_TOKEN_INDEX, LORA_DIM, axis=1)
        even = lt[:, ::2, :]
        odd = lt[:, 1::2, :]
        m1 = (even[:, :4, :, None] * odd[:, :4, None, :]).reshape(Bx, Hx, Dx)
        m2 = (even[:, 4:, :, None] * odd[:, 4:, None, :]).reshape(Bx, Dx, Hx)
        h = jnp.einsum('bsd,hd->bsh', x, W1) + scale * jnp.einsum('bsd,bhd->bsh', x, m1) + b1
        h = jax.nn.gelu(h, approximate=False)
        out = jnp.einsum('bsh,oh->bso', h, W2) + scale * jnp.einsum('bsh,boh->bso', h, m2) + b2
        return out

    def _L1_attn_ref(x, Wq, Wk, Wv, Wg):
        import jax, jax.numpy as jnp
        import numpy as np
        B, S, E, H = (2, 256, 128, 16)
        D = E // H
        EPS = 1e-06

        def _angle_decay():
            a = 1.0 / 10000.0 ** jnp.linspace(0.0, 1.0, D // 2)
            angle = jnp.repeat(a, 2)
            decay = jnp.log(1.0 - 2.0 ** (-5.0 - jnp.arange(H, dtype=jnp.float32)))
            return (angle, decay)

        def _rel_pos(slen):
            angle, decay = _angle_decay()
            idx = jnp.arange(slen, dtype=jnp.float32)
            sin = jnp.sin(idx[:, None] * angle[None, :])
            cos = jnp.cos(idx[:, None] * angle[None, :])
            diff = idx[:, None] - idx[None, :]
            tril = diff >= 0
            masked = jnp.where(tril, diff, jnp.inf)
            mask = jnp.exp(masked * decay[:, None, None])
            mask = jnp.nan_to_num(mask)
            mask = mask / jnp.sqrt(jnp.sum(mask, axis=-1, keepdims=True))
            return (sin, cos, mask)

        def _rotate_every_two(x):
            x1 = x[..., ::2]
            x2 = x[..., 1::2]
            return jnp.stack((-x2, x1), axis=-1).reshape(x.shape)

        def _theta_shift(x, sin, cos):
            return x * cos + _rotate_every_two(x) * sin
        bsz, tgt_len, _ = x.shape
        sin, cos, mask = _rel_pos(tgt_len)
        scaling = E ** (-0.5)
        q = x @ Wq
        k = x @ Wk * scaling
        v = x @ Wv
        g = x @ Wg
        q = q.reshape(bsz, tgt_len, H, D).transpose(0, 2, 1, 3)
        k = k.reshape(bsz, tgt_len, H, D).transpose(0, 2, 1, 3)
        vr = v.reshape(bsz, tgt_len, H, D).transpose(0, 2, 1, 3)
        qr = _theta_shift(q, sin, cos)
        kr = _theta_shift(k, sin, cos)
        qk = jnp.einsum('bhqd,bhkd->bhqk', qr, kr) * mask[None]
        denom = jax.lax.stop_gradient(jnp.clip(jnp.sum(jnp.abs(qk), axis=-1, keepdims=True), 1.0, 50000.0))
        out = jnp.einsum('bhqk,bhkd->bhqd', qk / denom, vr)
        out = out.transpose(0, 2, 1, 3)
        out = out * jax.lax.rsqrt(jnp.mean(out * out, axis=-1, keepdims=True) + EPS)
        out = out.reshape(bsz, tgt_len, E)
        return jax.nn.silu(g) * out

    def _L1_ffn_ref(x, router_w, router_b, fc1_w, fc1_b, fc2_w, fc2_b, layer_scale):
        import jax, jax.numpy as jnp
        import numpy as np
        B, T, C = (8, 256, 128)
        E, K = (8, 2)
        H = 4 * C
        CAP_FACTOR = 1.2
        EPS = 1e-09
        Bb, Tt, Cc = x.shape
        N = Bb * Tt
        KN = K * N
        capacity = int(CAP_FACTOR * (N // E + 1))
        xf = x.reshape(N, Cc)
        logits = xf @ router_w.T + router_b
        probs = jax.nn.softmax(logits, axis=-1)
        top_vals, top_inds = jax.lax.top_k(probs, K)
        top_vals = top_vals / (jnp.sum(top_vals, axis=-1, keepdims=True) + EPS)
        e_flat = top_inds.T.reshape(-1)
        w_flat = top_vals.T.reshape(-1)
        valid = w_flat > EPS
        onehot = (e_flat[:, None] == jnp.arange(E)[None, :]) & valid[:, None]
        pos = jnp.cumsum(onehot.astype(jnp.int32), axis=0) - 1
        pos_own = jnp.take_along_axis(pos, e_flat[:, None], axis=1)[:, 0]
        keep = valid & (pos_own < capacity)
        scores = jnp.where(keep[None, :] & (e_flat[None, :] == jnp.arange(E)[:, None]), jnp.arange(KN)[None, :], KN)
        sel = jnp.sort(scores, axis=1)[:, :capacity]
        slot_valid = sel < KN
        sel_c = jnp.where(slot_valid, sel, 0)
        tok = sel_c % N
        wgt = jnp.where(slot_valid, w_flat[sel_c], 0.0)
        toks = xf[tok]
        h = jax.nn.gelu(jnp.einsum('etc,ehc->eth', toks, fc1_w) + fc1_b[:, None, :], approximate=False)
        y = jnp.einsum('eth,ech->etc', h, fc2_w) + fc2_b[:, None, :]
        y = toks + y * layer_scale[:, None, :]
        out = jnp.zeros((N, Cc), dtype=x.dtype)
        out = out.at[tok.reshape(-1)].add((wgt[..., None] * y).reshape(-1, Cc))
        return out.reshape(Bb, Tt, Cc)
    x = L0_attn_in_features
    xn = _layernorm(x, axis=-1)
    s = _L0_attn_ref(xn, L0_attn_W_q, L0_attn_W_k, L0_attn_W_v, L0_attn_W_o)
    g = _silu(_L0_ffn_ref(xn, L0_ffn_W1, L0_ffn_b1, L0_ffn_W2, L0_ffn_b2, L0_ffn_scale))
    x = x + s * g
    xn = _layernorm(x, axis=-1)
    s = _L1_attn_ref(xn, L1_attn_Wq, L1_attn_Wk, L1_attn_Wv, L1_attn_Wg)
    g = _silu(_L1_ffn_ref(xn, L1_ffn_router_w, L1_ffn_router_b, L1_ffn_fc1_w, L1_ffn_fc1_b, L1_ffn_fc2_w, L1_ffn_fc2_b, L1_ffn_layer_scale))
    x = x + s * g
    return x

_drawn_inputs = setup_inputs


def setup_inputs(seed=0):
    import zlib

    import numpy as np

    out = dict(_drawn_inputs(seed))
    spreads = {'L0_ffn_b1': (0.0, 0.633),
     'L0_ffn_b2': (0.0, 0.385),
     'L1_ffn_router_b': (0.0, 0.1),
     'L1_ffn_fc1_b': (0.0, 2.0),
     'L1_ffn_fc2_b': (0.0, 2.0),
     'L1_ffn_layer_scale': (0.10000000149011612, 0.6)}
    factors = {'L0_attn_W_q': 3.546,
     'L0_attn_W_k': 3.254,
     'L0_attn_W_v': 2.901,
     'L0_attn_W_o': 2.783,
     'L0_ffn_W1': 4.086,
     'L0_ffn_W2': 4.266,
     'L1_ffn_fc1_w': 4.827,
     'L1_ffn_fc2_w': 4.313}
    for name, (base, spread) in spreads.items():
        noise = np.random.default_rng([zlib.crc32(name.encode()), seed]).standard_normal(out[name].shape)
        drawn = base * np.exp(spread * noise) if base else spread * noise
        out[name] = jnp.asarray(drawn.astype(out[name].dtype))
    for name, factor in factors.items():
        out[name] = (out[name] * factor).astype(out[name].dtype)
    return out
```

```python
from contextlib import ExitStack

import numpy as np

import concourse.bass as bass
from concourse import mybir

F32 = mybir.dt.float32
BF16 = mybir.dt.bfloat16
I32 = mybir.dt.int32
ALU = mybir.AluOpType
ACT = mybir.ActivationFunctionType
AX = mybir.AxisListType

P = 128
B, S, D = 4, 1024, 128
H, DH = 16, 8
NT = S // P
NTILES = B * NT
HALF = 512
FF = 512
FC = FF // P
QUADS = H // 4
ROWS = 64
VW = 32
AUG = 48
Q_ROWS = {"hi": (0, 1, 2), "mid": (3, 4), "lo": (5,)}
K_ROWS = {"hi": (0, 3, 5), "mid": (1, 4), "lo": (2,)}
NE = 8
N = B * S
CAP = int(1.2 * (N // NE + 1))
SLOT_TILES = -(-CAP // P)
SLOTS = SLOT_TILES * P
ALL_SLOTS = NE * SLOTS
NO_SLOT = ALL_SLOTS
MASKED = -1.0e30
LN_EPS, RMS_EPS, TOP_EPS = 1e-5, 1e-6, 1e-9


def linker(engine, semaphore, base):
    count = [0]

    def link(ins):
        count[0] += 1
        ins.then_inc(semaphore, 1)
        engine.wait_ge(semaphore, base + count[0])

    return link, count


class Space:

    def __init__(self, nc):
        self.nc, self.stack = nc, ExitStack()

    def __enter__(self):
        self.stack.__enter__()
        return self

    def __exit__(self, *e):
        return self.stack.__exit__(*e)

    def sb(self, name, shape, dt=F32):
        return self.stack.enter_context(self.nc.sbuf_tensor(name, shape, dt))

    def psum(self, name):
        return self.stack.enter_context(self.nc.psum_tensor(name, [P, 8, HALF], F32))

    def sem(self, name):
        return self.stack.enter_context(self.nc.semaphore(name))


def one(ap, i):
    return ap[bass.ds(i, 1)]


def split_rows(dst, it, rows):
    return [one(dst, it)[:, :, DH * r:DH * r + DH, :].rearrange("a h d s -> (a h) d s") for r in rows]


def fill_padding(nc, A):
    with Space(nc) as m:
        zeros = m.sb("zeros", [P, 8192], BF16)
        ones = m.sb("ones_rows", [P, 2048], BF16)
        zeros_f = m.sb("zeros_f", [P, 5 * P])
        filled, stored = m.sem("pad_filled"), m.sem("pad_stored")
        pad = ROWS - AUG
        with nc.Block() as block:
            @block.vector
            def _(dve):
                nc.vector.memset(zeros[:, :], 0.0).then_inc(filled, 1)
                nc.vector.memset(ones[:, :], 1.0).then_inc(filled, 1)
                nc.vector.memset(zeros_f[:, :], 0.0).then_inc(filled, 1)

            @block.sync
            def _(sp):
                sp.wait_ge(filled, 3)
                n = 0
                heads = B * H
                for t, aug in ((A["q0"], 0), (A["k0"], 1), (A["q1"], 0), (A["k1"], 0)):
                    v = t[0:B].rearrange("b h r s -> (b h) r s")
                    src = zeros[0:heads, 0:8192].rearrange("p (r s) -> p r s", s=S)
                    sp.dma_start(v[:, AUG + 8:ROWS, :], src[:, 0:pad - 8, :]).then_inc(stored, 16)
                    sp.dma_start(v[:, AUG + 2:AUG + 8, :], src[:, 0:6, :]).then_inc(stored, 16)
                    o = (ones if aug else zeros)[0:heads, 0:2048].rearrange("p (r s) -> p r s", s=S)
                    sp.dma_start(v[:, AUG:AUG + 2, :], o).then_inc(stored, 16)
                    n += 3
                for t in (A["q0"], A["k0"], A["q1"], A["k1"]):
                    v = t[B].rearrange("h r s -> (h r) s")
                    for k in range(H * ROWS // P):
                        sp.dma_start(v[k * P:k * P + P, :], zeros[:, 0:S]).then_inc(stored, 16)
                        n += 1
                sp.dma_start(A["v1"][B].rearrange("(t p) c -> p t c", p=P),
                             zeros[:, 0:2 * S].bitcast(F32).rearrange("p (t c) -> p t c", c=D)).then_inc(stored, 16)
                n += 1
                for t in range(NT):
                    sp.dma_start(A["v0"][B, :, t * H * VW:(t + 1) * H * VW], zeros[:, 0:2 * H * VW].bitcast(F32)).then_inc(stored, 16)
                    n += 1
                for e in range(NE):
                    sp.dma_start(A["slot_x"][e * SLOTS:(e + 1) * SLOTS, :].rearrange("(t p) c -> p t c", p=P),
                                 zeros_f[:, :].rearrange("p (t c) -> p t c", c=D)).then_inc(stored, 16)
                    n += 1
                sp.dma_start(A["slot_y"][NO_SLOT:NO_SLOT + P, :], zeros_f[:, 0:D]).then_inc(stored, 16)
                sp.wait_ge(stored, 16 * (n + 1))


def project_and_ffn(nc, A):
    with Space(nc) as m:
        ps = m.psum("psA")
        ident = m.sb("identA", [P, P])
        cos, sin = m.sb("cosA", [P, S]), m.sb("sinA", [P, S])
        w_proj = m.sb("w_projA", [P, 5, P])
        w1 = m.sb("w1A", [P, FF])
        w2 = m.sb("w2A", [P, FC, P])
        b1 = m.sb("b1A", [P, FC])
        b2 = m.sb("b2A", [P, D])
        scale = m.sb("scaleA", [P, 1])
        pick = m.sb("pickA", [P, 8, P])
        eps, power = m.sb("epsA", [P, NT]), m.sb("powA", [P, NT])
        x = m.sb("xA", [P, NT, D])
        stat, mom = m.sb("statA", [P, NT, 6]), m.sb("momA", [P, NT, 2])
        held = m.sb("heldA", [P, 1])
        var, rstd = m.sb("varA", [P, NT]), m.sb("rstdA", [P, NT])
        xn = m.sb("xnA", [P, NT, D])
        xnT = m.sb("xnTA", [P, S])
        terms = m.sb("termsA", [P, 2, 4, HALF])
        roped = m.sb("ropedA", [P, 2, S])
        rest = m.sb("restA", [P, 2, S])
        hi, mid, lo = (m.sb(n, [P, 2, S], BF16) for n in ("hiA", "midA", "loA"))
        vaug = m.sb("vaugA", [P, NT, H, VW])
        odd = m.sb("oddA", [P, 8])
        w1e = m.sb("w1eA", [P, FF])
        w2e = m.sb("w2eA", [P, FC, P])
        hT = m.sb("hTA", [P, FC, HALF])
        u = m.sb("uA", [P, NT, D])

        loaded, ready = m.sem("constA"), m.sem("initA")
        x_loaded, stats, moments = m.sem("x_loadedA"), m.sem("statsA"), m.sem("momentsA")
        var_ready, rstd_ready, xn_ready = m.sem("var_readyA"), m.sem("rstd_readyA"), m.sem("xn_readyA")
        turned, xnT_ready = m.sem("turnedA"), m.sem("xnT_readyA")
        projected, v_done, v_kept = m.sem("projectedA"), m.sem("v_doneA"), m.sem("v_keptA")
        outer_done, odd_ready, w_ready = m.sem("outer_doneA"), m.sem("odd_readyA"), m.sem("w_readyA")
        terms_ready, roped_ready = m.sem("terms_readyA"), m.sem("roped_readyA")
        hi_ready, rest_ready = m.sem("hi_readyA"), m.sem("rest_readyA")
        mid_ready, lo_ready = m.sem("mid_readyA"), m.sem("lo_readyA")
        h_done, gelu_done, u_done, u_ready = (m.sem(n) for n in ("h_doneA", "gelu_doneA", "u_doneA", "u_readyA"))
        stored = m.sem("storedA")
        STORES = 14
        consts = [(ident, A["ident"]), (cos, A["cos0"]), (sin, A["sin0"]), (w_proj, A["w_proj0"]), (w1, A["w1T"]),
                  (w2, A["w2T"]), (b1, A["b1c"]), (pick, A["pick"])]

        with nc.Block() as block:
            @block.sync
            def _(sp):
                for dst, src in consts:
                    sp.dma_start(dst[:], src).then_inc(loaded, 16)
                sp.dma_start(b2[:, :], A["b2"].broadcast_to((P, D))).then_inc(loaded, 16)
                sp.dma_start(scale[:, :], A["scale"].broadcast_to((P, 1))).then_inc(loaded, 16)
                sp.dma_start(x[:, :, :], A["x"][0].rearrange("(t p) c -> p t c", p=P)).then_inc(x_loaded, 16)
                with sp.Fori(0, B) as it:
                    nxt = one(A["x_next"], it).rearrange("a (t p) c -> p (a t) c", p=P)
                    q_rows = {k: split_rows(A["q0"], it, r) for k, r in Q_ROWS.items()}
                    k_rows = {k: split_rows(A["k0"], it, r) for k, r in K_ROWS.items()}
                    xn_all, split_all, u_all = (sp.snap(it * NT + NT), sp.snap(it * 2 + 2), sp.snap(it * 2 + 2))
                    sp.wait_ge(xn_ready, xn_all)
                    sp.dma_start(x[:, :, :], nxt).then_inc(x_loaded, 16)
                    sp.wait_ge(lo_ready, split_all)
                    for name, part in (("hi", hi), ("mid", mid), ("lo", lo)):
                        for i, rows in ((0, q_rows), (1, k_rows)):
                            for dst in rows[name]:
                                sp.dma_start(dst, part[:, i, :]).then_inc(stored, 16)
                    sp.wait_ge(u_ready, u_all)
                    sp.dma_start(one(A["u"][1:B + 1], it).rearrange("a (t p) c -> p (a t) c", p=P), u[:, :, :]).then_inc(stored, 16)
                    sp.dma_start(one(A["v0"], it).rearrange("a p f -> (a p) f"),
                                 vaug[:, :, :, :].rearrange("p t h d -> p (t h d)")).then_inc(stored, 16)
                sp.wait_ge(x_loaded, 16 * (B + 1))
                sp.wait_ge(stored, 16 * STORES * B + 1)

            @block.vector
            def _(dve):
                nc.vector.memset(vaug[:, :, :, :], 1.0).then_inc(ready, 1)
                nc.vector.memset(eps[:, :], LN_EPS).then_inc(ready, 1)
                nc.vector.memset(power[:, :], -0.5).then_inc(ready, 1)
                dve.sem_inc(stored, 1)
                dve.wait_ge(loaded, 16 * (len(consts) + 2))
                with dve.Fori(0, B) as it:
                    dve.wait_ge(x_loaded, it * 16 + 16)
                    for t in range(NT):
                        nc.vector.bn_stats(stat[:, t, :], x[:, t, :]).then_inc(stats, 1)
                    dve.wait_ge(stats, it * NT + NT)
                    nc.vector.memset(held[:, :], 0.0)
                    for t in range(NT):
                        nc.vector.bn_aggr(mom[:, t, :], stat[:, t, :]).then_inc(moments, 1)
                    dve.wait_ge(rstd_ready, it + 1)
                    for t in range(NT):
                        nc.vector.tensor_scalar(xn[:, t, :], x[:, t, :], mom[:, t, 0:1], rstd[:, t:t + 1],
                                                ALU.subtract, ALU.mult).then_inc(xn_ready, 1)
                    dve.wait_ge(xnT_ready, it * 2 + 1)
                    nc.vector.tensor_scalar(odd[:, :], xnT[:, 2:18:2], scale[:, 0:1], None,
                                            ALU.mult).then_inc(odd_ready, 1)

                    def rope(half):
                        c = slice(half * HALF, half * HALF + HALF)
                        dve.wait_ge(projected, it * 2 + half + 1)
                        for j in range(4):
                            ins = nc.vector.tensor_tensor(terms[:, half, j, :], ps[:, 2 + j, :],
                                                          (cos if j % 2 == 0 else sin)[:, c], ALU.mult)
                        ins.then_inc(terms_ready, 1)

                    rope(0)
                    dve.wait_ge(outer_done, it + 1)
                    dve.wait_ge(odd_ready, it + 1)
                    for j in range(4):
                        c = slice(j * P, j * P + P)
                        nc.vector.scalar_tensor_tensor(w1e[:, c], ps[:, 0, c], odd[:, j:j + 1], w1[:, c],
                                                       ALU.mult, ALU.add)
                    for j in range(4):
                        o = slice(j * 32, j * 32 + 32)
                        ins = nc.vector.scalar_tensor_tensor(
                            w2e[:, :, o], ps[:, 1, j * P:j * P + P].rearrange("p (r q) -> p q r", q=FC),
                            odd[:, 4 + j:5 + j], w2[:, :, o], ALU.mult, ALU.add)
                    ins.then_inc(w_ready, 1)
                    rope(1)
                    dve.wait_ge(stored, it * (16 * STORES) + 1)
                    for half in range(2):
                        dve.wait_ge(u_done, it * 2 + half + 1)
                        nc.vector.tensor_tensor(
                            u[:, 4 * half:4 * half + 4, :], ps[:, 6 + half, :].rearrange("p (t c) -> p t c", c=D),
                            b2[:, None, :].broadcast_to((P, 4, D)), ALU.add).then_inc(u_ready, 1)

            @block.gpsimd
            def _(pool):
                pool.wait_ge(ready, 3)
                with pool.Fori(0, B) as it:
                    pool.wait_ge(moments, it * NT + NT)
                    nc.gpsimd.tensor_tensor(var[:, :], mom[:, :, 1], eps[:, :], ALU.add).then_inc(var_ready, 1)
                    pool.wait_ge(var_ready, it + 1)
                    nc.gpsimd.tensor_tensor(rstd[:, :], var[:, :], power[:, :], ALU.pow).then_inc(rstd_ready, 1)
                    for half in range(2):
                        c = slice(half * HALF, half * HALF + HALF)
                        pool.wait_ge(terms_ready, it * 2 + half + 1)
                        for i in range(2):
                            ins = nc.gpsimd.tensor_tensor(roped[:, i, c], terms[:, half, 2 * i, :],
                                                          terms[:, half, 2 * i + 1, :], ALU.add)
                        ins.then_inc(roped_ready, 1)
                        pool.wait_ge(hi_ready, it * 2 + half + 1)
                        for i in range(2):
                            ins = nc.gpsimd.tensor_tensor(rest[:, i, c], roped[:, i, c], hi[:, i, c], ALU.subtract)
                        ins.then_inc(rest_ready, 1)
                        pool.wait_ge(mid_ready, it * 2 + half + 1)
                        for i in range(2):
                            ins = nc.gpsimd.tensor_tensor(lo[:, i, c], rest[:, i, c], mid[:, i, c], ALU.subtract)
                        ins.then_inc(lo_ready, 1)

            @block.scalar
            def _(act):
                act.wait_ge(ready, 3)
                act.wait_ge(loaded, 16 * (len(consts) + 2))
                with act.Fori(0, B) as it:
                    for half in range(2):
                        act.wait_ge(turned, it * 2 + half + 1)
                        nc.scalar.copy(xnT[:, half * HALF:half * HALF + HALF], ps[:, half, :]).then_inc(xnT_ready, 1)
                    act.wait_ge(stored, it * (16 * STORES) + 1)
                    for half in range(2):
                        act.wait_ge(v_done, it * 2 + half + 1)
                        nc.scalar.copy(
                            vaug[:, 4 * half:4 * half + 4, :, 0:DH].rearrange("p t h d -> p (t h) d"),
                            ps[:, 6 + half, :].rearrange("p (g d) -> p g d", d=DH)).then_inc(v_kept, 1)
                    for half in range(2):
                        c = slice(half * HALF, half * HALF + HALF)
                        act.wait_ge(roped_ready, it * 2 + half + 1)
                        nc.scalar.copy(hi[:, :, c], roped[:, :, c]).then_inc(hi_ready, 1)
                        act.wait_ge(rest_ready, it * 2 + half + 1)
                        nc.scalar.copy(mid[:, :, c], rest[:, :, c]).then_inc(mid_ready, 1)
                    for half in range(2):
                        for c in range(FC):
                            act.wait_ge(h_done, it * (2 * FC) + half * FC + c + 1)
                            if half == 1 and c == 0:
                                act.wait_ge(u_done, it * 2 + 1)
                            nc.scalar.activation(hT[:, c, :], ps[:, 2 + c, :], ACT.Gelu,
                                                 bias=b1[:, c:c + 1]).then_inc(gelu_done, 1)

            @block.tensor
            def _(pe):
                pe.wait_ge(loaded, 16 * (len(consts) + 2))
                with pe.Fori(0, B) as it:
                    for t in range(NT):
                        pe.wait_ge(xn_ready, it * NT + t + 1)
                        ins = nc.tensor.transpose(ps[:, t // 4, (t % 4) * P:(t % 4) * P + P], xn[:, t, :], ident[:, :])
                        if t % 4 == 3:
                            ins.then_inc(turned, 1)

                    def project(half):
                        for j in range(4):
                            ins = nc.tensor.matmul(ps[:, 2 + j, :], w_proj[:, j, :],
                                                   xnT[:, half * HALF:half * HALF + HALF], start=True, stop=True)
                        ins.then_inc(projected, 1)

                    pe.wait_ge(xnT_ready, it * 2 + 1)
                    project(0)
                    pe.wait_ge(xnT_ready, it * 2 + 2)
                    for j in range(8):
                        ins = nc.tensor.matmul(ps[:, j // 4, (j % 4) * P:(j % 4) * P + P], pick[:, j, :], xn[:, 0, :],
                                               start=True, stop=True)
                    ins.then_inc(outer_done, 1)
                    for t in range(NT):
                        ins = nc.tensor.matmul(ps[:, 6 + t // 4, (t % 4) * P:(t % 4) * P + P], xnT[:, t * P:t * P + P],
                                               w_proj[:, 4, :], start=True, stop=True)
                        if t % 4 == 3:
                            ins.then_inc(v_done, 1)
                    pe.wait_ge(terms_ready, it * 2 + 1)
                    project(1)
                    pe.wait_ge(terms_ready, it * 2 + 2)
                    pe.wait_ge(w_ready, it + 1)
                    pe.wait_ge(v_kept, it * 2 + 2)
                    for half in range(2):
                        for c in range(FC):
                            nc.tensor.matmul(ps[:, 2 + c, :], w1e[:, c * P:c * P + P],
                                             xnT[:, half * HALF:half * HALF + HALF], start=True,
                                             stop=True).then_inc(h_done, 1)
                        for t in range(4):
                            for c in range(FC):
                                if t == 0:
                                    pe.wait_ge(gelu_done, it * (2 * FC) + half * FC + c + 1)
                                ins = nc.tensor.matmul(ps[:, 6 + half, t * P:t * P + P], hT[:, c, t * P:t * P + P],
                                                       w2e[:, c, :], start=(c == 0), stop=(c == FC - 1))
                        ins.then_inc(u_done, 1)


def attention(nc, A):
    ITEMS, SLOTS_B, UNITS = 24, 12, 49
    units = [(hq, t, c) for t in range(NT) for c in range(t // 4 + 1) for hq in range(4)]
    slots = [(c, jt) for c in range(2) for jt in range(4 * c + 4)]
    with Space(nc) as m:
        ps = m.psum("psB")
        st = [ps[:, 0:2, :], ps[:, 2:4, :]]
        pv = [ps[:, 4, :], ps[:, 5, :]]
        mxb = [ps[:, 6, :], ps[:, 7, :]]
        ident, identb = m.sb("identB", [P, P]), m.sb("identbB", [P, P], BF16)
        mask_ij, mask_ji = m.sb("mask_ijB", [P, P], BF16), m.sb("mask_jiB", [P, P], BF16)
        q, k = m.sb("qB", [P, QUADS, 2, S], BF16), m.sb("kB", [P, QUADS, 2, S], BF16)
        v = m.sb("vB", [P, QUADS, NT, 4 * VW])
        probs = m.sb("probsB", [P, 4, 2, HALF])
        out = m.sb("outB", [P, 2, HALF])
        mx, mx2 = m.sb("mxB", [P, 2, 4, NT]), m.sb("mx2B", [P, 2, 4, NT // 2])
        neg = m.sb("negB", [32, 2, 2, P], BF16)

        loaded = m.sem("constB")
        in_loaded = [m.sem(f"in_loadedB{s}") for s in range(QUADS)]
        st_done, exp_done, pv_done = m.sem("st_doneB"), m.sem("exp_doneB"), m.sem("pv_doneB")
        out_kept, out_stored = m.sem("out_keptB"), [m.sem(f"out_storedB{c}") for c in range(2)]
        max_done, max_read, combined, neg_hi = (m.sem(n) for n in ("max_doneB", "max_readB", "combinedB", "neg_hiB"))
        neg_placed = [m.sem(f"neg_placedB{p}") for p in range(2)]
        LOADS, PLACED = 16 * 5, 16 * 4

        with nc.Block() as block:
            @block.sync
            def _(sp):
                for dst, src in ((ident, "ident"), (identb, "identb"), (mask_ij, "mask_ij"), (mask_ji, "mask_ji")):
                    sp.dma_start(dst[:, :], A[src]).then_inc(loaded, 16)

                def load(s, qd, kd, vd):
                    for p in range(2):
                        rows = slice(4 * s + 2 * p, 4 * s + 2 * p + 2)
                        sp.dma_start(q[:, s, p, :], qd[:, rows].rearrange("a h r s -> (a h r) s")).then_inc(in_loaded[s], 16)
                        sp.dma_start(k[:, s, p, :], kd[:, rows].rearrange("a h r s -> (a h r) s")).then_inc(in_loaded[s], 16)
                    sp.dma_start(v[:, s, :, :], vd.rearrange("a p (t f) -> (a p) t f", t=NT)[
                        :, :, s * 4 * VW:(s + 1) * 4 * VW]).then_inc(in_loaded[s], 16)

                def place(s, par):
                    for part in range(2):
                        for p in range(2):
                            sp.dma_start(q[AUG + part:AUG + part + ROWS + 1:ROWS, s, p, :],
                                         neg[2 * NT * p:2 * NT * p + 2 * NT, par, part, :]).then_inc(neg_placed[par], 16)

                for s in range(QUADS):
                    load(s, A["q0"][0:1], A["k0"][0:1], A["v0"][0:1])
                sp.wait_ge(max_read, UNITS)
                place(0, 0)
                with sp.Fori(0, B) as it:
                    qd, kd, vd = one(A["q0_next"], it), one(A["k0_next"], it), one(A["v0_next"], it)
                    od = one(A["o0"], it)
                    kept = [sp.snap(it * 8 + 2 + e + 1) for e in range(8)]
                    used = [sp.snap(it * (SLOTS_B * QUADS) + 2 + SLOTS_B * (s + 1)) for s in range(QUADS)]
                    maxed = [sp.snap(it * (UNITS * QUADS) + UNITS * (s + 2)) for s in range(QUADS)]

                    def store(s, c):
                        sp.wait_ge(out_kept, kept[2 * s + c])
                        for hq in range(4):
                            sp.dma_start(od[:, 4 * s + hq, :, c * HALF:(c + 1) * HALF].rearrange("a r s -> (a r) s"),
                                         out[VW * hq:VW * hq + 2 * DH, c, :]).then_inc(out_stored[c], 16)

                    for s in range(QUADS):
                        store(s, 0)
                        sp.wait_ge(max_read, maxed[s])
                        place((s + 1) % QUADS, (s + 1) % 2)
                        store(s, 1)
                        sp.wait_ge(pv_done, used[s])
                        load(s, qd, kd, vd)
                for s in range(QUADS):
                    sp.wait_ge(in_loaded[s], LOADS * (B + 1))
                for par in range(2):
                    sp.wait_ge(neg_placed[par], PLACED * (B * QUADS // 2 + 1 - par) + 1)
                for c in range(2):
                    sp.wait_ge(out_stored[c], 64 * B * QUADS + 1)

            @block.vector
            def _(dve):
                dve.sem_inc(out_stored[0], 1)
                dve.sem_inc(out_stored[1], 1)
                dve.sem_inc(neg_placed[0], 1)
                dve.sem_inc(neg_placed[1], 1)

                def maxima(par, done, quads, placed):
                    for g, (hq, t, c) in enumerate(units):
                        w = min(HALF, P * (t + 1) - HALF * c)
                        dst = mx[:, par, hq, t:t + 1] if c == 0 else mx2[:, par, hq, t - 4:t - 3]
                        dve.wait_ge(max_done, done + g + 1)
                        nc.vector.tensor_reduce(dst, mxb[(g + par) % 2][:, 0:w], AX.X, ALU.max).then_inc(max_read, 1)
                    dve.wait_ge(max_read, done + UNITS - 1)
                    nc.vector.tensor_tensor(mx[:, par, :, 4:8], mx[:, par, :, 4:8], mx2[:, par, :, :],
                                            ALU.max).then_inc(combined, 1)
                    turned = mxb[(UNITS - 1 + par) % 2][0:32, 0:P]
                    dve.wait_ge(neg_placed[par], placed * PLACED + 1)
                    dve.wait_ge(max_done, done + UNITS)
                    nc.vector.tensor_scalar(neg[:, par, 0, :], turned, -1.0, None, ALU.mult).then_inc(neg_hi, 1)
                    dve.wait_ge(neg_hi, quads + 1)
                    nc.vector.scalar_tensor_tensor(neg[:, par, 1, :], turned, -1.0, neg[:, par, 0, :], ALU.mult,
                                                   ALU.subtract).then_inc(max_read, 1)

                maxima(0, 0, 0, 0)
                with dve.Fori(0, B) as it:
                    for s in range(QUADS):
                        maxima((s + 1) % 2, it * (UNITS * QUADS) + UNITS * (s + 1), it * QUADS + s + 1,
                               it * 2 + (s + 1) // 2)

            @block.scalar
            def _(act):
                act.sem_inc(pv_done, 2)
                act.sem_inc(out_kept, 2)
                with act.Fori(0, B) as it:
                    def keep(s, c):
                        last = SLOTS_B * s + (4 if c == 0 else SLOTS_B)
                        act.wait_ge(pv_done, it * (SLOTS_B * QUADS) + 2 + last)
                        act.wait_ge(out_stored[c], it * (64 * QUADS) + 64 * s + 1)
                        nc.scalar.copy(out[:, c, :], pv[c]).then_inc(out_kept, 1)

                    for s in range(QUADS):
                        for j, (c, jt) in enumerate(slots):
                            w = HALF * (c + 1) - max(HALF * c, P * jt)
                            for p in range(2):
                                n = ITEMS * s + 2 * j + p
                                act.wait_ge(st_done, it * (ITEMS * QUADS) + n + 1)
                                if p == 0:
                                    act.wait_ge(pv_done, it * (SLOTS_B * QUADS) + n // 2 + 1)
                                nc.scalar.activation(probs[:, n % 4, :, 0:w], st[n % 2][:, :, 0:w], ACT.Exp,
                                                     scale=DH ** -0.5).then_inc(exp_done, 1)
                            if j == 5:
                                keep(s, 0)
                            if j == 1 and s:
                                keep(s - 1, 1)
                    keep(QUADS - 1, 1)

            @block.tensor
            def _(pe):
                def unit(s, g, par, done):
                    bank = mxb[(g + par) % 2]
                    if not (isinstance(done, int) and done + g < 2):
                        pe.wait_ge(max_read, done + g - 1)
                    if g == UNITS - 1:
                        pe.wait_ge(combined, done_quads[0] + 1)
                        nc.tensor.transpose(bank[0:32, 0:P], mx[:, par, :, :].rearrange("p h t -> p (h t)"),
                                            ident[:, :]).then_inc(max_done, 1)
                        return
                    hq, t, c = units[g]
                    r = slice(ROWS * (hq % 2), ROWS * (hq % 2) + ROWS)
                    w = min(HALF, P * (t + 1) - HALF * c)
                    last = c == t // 4
                    ins = nc.tensor.matmul(bank[:, 0:w], q[r, s, hq // 2, t * P:t * P + P],
                                           k[r, s, hq // 2, HALF * c:HALF * c + w], start=True, stop=not last)
                    if last:
                        ins = nc.tensor.matmul(bank[:, w - P:w], identb[:, :], mask_ij[:, :], start=False, stop=True)
                    ins.then_inc(max_done, 1)

                done_quads = [0]
                pe.wait_ge(loaded, 64)
                pe.wait_ge(in_loaded[0], LOADS)
                for g in range(UNITS):
                    unit(0, g, 0, 0)
                with pe.Fori(0, B) as it:
                    def products(s, j):
                        c, jt = slots[j]
                        i0 = max(HALF * c, P * jt)
                        n = ITEMS * s + 2 * j
                        pe.wait_ge(exp_done, it * (ITEMS * QUADS) + n + 2)
                        if jt == 0:
                            pe.wait_ge(out_kept, it * 8 + 2 * s + c + 1)
                        for hq in range(4):
                            ins = nc.tensor.matmul(pv[c][VW * hq:VW * hq + VW, i0 - HALF * c:HALF],
                                                   v[:, s, jt, VW * hq:VW * hq + VW],
                                                   probs[:, (n + hq // 2) % 4, hq % 2, 0:HALF * (c + 1) - i0],
                                                   start=(jt == 0), stop=(jt == 4 * c + 3), skip_group_check=True)
                        ins.then_inc(pv_done, 1)

                    before = None
                    for s in range(QUADS):
                        nxt, par = (s + 1) % QUADS, (s + 1) % 2
                        done = it * (UNITS * QUADS) + UNITS * (s + 1)
                        done_quads[0] = it * QUADS + s + 1
                        g = 0
                        pe.wait_ge(neg_placed[s % 2], it * (2 * PLACED) + PLACED * (s // 2 + 1) + 1)
                        pe.wait_ge(in_loaded[nxt], it * LOADS + LOADS * (1 + (s == QUADS - 1)))
                        for j, (c, jt) in enumerate(slots):
                            i0 = max(HALF * c, P * jt)
                            w = HALF * (c + 1) - i0
                            for p in range(2):
                                n = ITEMS * s + 2 * j + p
                                if n >= 2:
                                    pe.wait_ge(exp_done, it * (ITEMS * QUADS) + n - 1)
                                for hh in range(2):
                                    r = slice(ROWS * hh, ROWS * hh + ROWS)
                                    ins = nc.tensor.matmul(st[n % 2][:, hh, 0:w], k[r, s, p, jt * P:jt * P + P],
                                                           q[r, s, p, i0:i0 + w], start=True, stop=(jt < 4 * c))
                                if jt >= 4 * c:
                                    for hh in range(2):
                                        ins = nc.tensor.matmul(st[n % 2][:, hh, 0:P], identb[:, :], mask_ji[:, :],
                                                               start=False, stop=True)
                                ins.then_inc(st_done, 1)
                                for _ in range(3 if g < UNITS - 1 else 1):
                                    if g < UNITS:
                                        unit(nxt, g, par, done)
                                        g += 1
                            if before:
                                products(*before)
                            before = (s, j)
                    products(*before)


def between_layers(nc, A):
    with Space(nc) as m:
        ps = m.psum("psC")
        ident = m.sb("identC", [P, P])
        tables = m.sb("tablesC", [P, 4, S])
        w_out = m.sb("w_outC", [P, D])
        w_proj = m.sb("w_projC", [P, 4, P])
        w_vg = m.sb("w_vgC", [P, 2, P])
        w_router, b_router = m.sb("w_routerC", [P, NE]), m.sb("b_routerC", [P, NE])
        same_head = m.sb("same_headC", [P, P])
        eps, power = m.sb("epsC", [P, NT]), m.sb("powC", [P, NT])
        oT, den = m.sb("oTC", [P, S]), m.sb("denC", [P, S])
        x, u, gate = m.sb("xC", [P, NT, D]), m.sb("uC", [P, NT, D]), m.sb("gateC", [P, NT, D])
        rden, headT = m.sb("rdenC", [P, S]), m.sb("headTC", [P, S])
        x1 = m.sb("x1C", [P, NT, D])
        stat, mom = m.sb("statC", [P, NT, 6]), m.sb("momC", [P, NT, 2])
        held = m.sb("heldC", [P, 1])
        var, rstd = m.sb("varC", [P, NT]), m.sb("rstdC", [P, NT])
        xn, xnT = m.sb("xnC", [P, NT, D]), m.sb("xnTC", [P, S])
        terms = m.sb("termsC", [P, 2, 4, HALF])
        roped, rest = m.sb("ropedC", [P, 2, S]), m.sb("restC", [P, 2, S])
        hi, mid, lo = (m.sb(n, [P, 2, S], BF16) for n in ("hiC", "midC", "loC"))
        v, gate1 = m.sb("vC", [P, NT, D]), m.sb("gate1C", [P, NT, D])
        logits = m.sb("logitsC", [P, NT, NE])
        k_tok = m.sb("k_tokC", [P, NT, P])
        chunk_state = m.sb("chunk_stateC", [P, NT, P])
        state = m.sb("stateC", [P, NT, P])
        inter = m.sb("interC", [P, S])

        names = ("const init in_loaded u_loaded gated rden_ready head_ready s_done x1_half x1_ready stats moments var_ready "
                 "rstd_ready xn_ready turned xnT_ready projected vg_done v_kept g_kept router_done logits_ready terms_ready "
                 "roped_ready hi_ready rest_ready mid_ready lo_ready k_turned k_kept chunk_done chunk_ready state_ready "
                 "inter_done inter_kept stored").split()
        g = {n: m.sem(n + "C") for n in names}
        consts = [(ident, "ident"), (tables, "tables1"), (w_out, "w_outT"), (w_proj, "w_proj1"), (w_vg, "w_vg1"),
                  (w_router, "w_routerT"), (same_head, "same_head")]
        STORES = 12 + 6
        LOADS = 16 * 3

        with nc.Block() as block:
            @block.sync
            def _(sp):
                for dst, src in consts:
                    sp.dma_start(dst[:], A[src]).then_inc(g["const"], 16)
                sp.dma_start(b_router[:, :], A["b_router"].broadcast_to((P, NE))).then_inc(g["const"], 16)
                with sp.Fori(0, B) as it:
                    od = one(A["o0"], it).rearrange("a h r s -> (a h) r s")
                    xd = one(A["x"], it).rearrange("a (t p) c -> p (a t) c", p=P)
                    tok = {n: one(A[n][1:B + 1] if n == "u" else A[n], it).rearrange("a (t p) c -> p (a t) c", p=P)
                           for n in ("u", "x1", "xn1", "v1", "g1")}
                    ld = one(A["logits"], it).rearrange("a p f -> (a p) f")
                    nd = one(A["inter"], it).rearrange("a p s -> (a p) s")
                    q_rows = {n: split_rows(A["q1"], it, r) for n, r in Q_ROWS.items()}
                    k_rows = {n: split_rows(A["k1"], it, r) for n, r in K_ROWS.items()}
                    val = {n: sp.snap(it * c + c) for n, c in (("xn_ready", NT), ("v_kept", 2), ("g_kept", 2),
                                                                ("logits_ready", 1), ("lo_ready", 2), ("inter_kept", 2))}
                    free = sp.snap(it * 2 + 1)
                    sp.wait_ge(g["x1_ready"], free)
                    sp.dma_start(oT[:, :], od[:, 0:DH, :]).then_inc(g["in_loaded"], 16)
                    sp.dma_start(den[:, :], od[:, DH:2 * DH, :]).then_inc(g["in_loaded"], 16)
                    sp.dma_start(x[:, :, :], xd).then_inc(g["in_loaded"], 16)
                    sp.dma_start(u[:, :, :], tok["u"]).then_inc(g["u_loaded"], 16)
                    sp.wait_ge(g["xn_ready"], val["xn_ready"])
                    sp.dma_start(tok["x1"], x1[:, :, :]).then_inc(g["stored"], 16)
                    sp.dma_start(tok["xn1"], xn[:, :, :]).then_inc(g["stored"], 16)
                    sp.wait_ge(g["v_kept"], val["v_kept"])
                    sp.dma_start(tok["v1"], v[:, :, :]).then_inc(g["stored"], 16)
                    sp.wait_ge(g["g_kept"], val["g_kept"])
                    sp.dma_start(tok["g1"], gate1[:, :, :]).then_inc(g["stored"], 16)
                    sp.wait_ge(g["logits_ready"], val["logits_ready"])
                    sp.dma_start(ld, logits[:, :, :].rearrange("p t e -> p (t e)")).then_inc(g["stored"], 16)
                    sp.wait_ge(g["lo_ready"], val["lo_ready"])
                    for name, part in (("hi", hi), ("mid", mid), ("lo", lo)):
                        for i, rows in ((0, q_rows), (1, k_rows)):
                            for dst in rows[name]:
                                sp.dma_start(dst, part[:, i, :]).then_inc(g["stored"], 16)
                    sp.wait_ge(g["inter_kept"], val["inter_kept"])
                    sp.dma_start(nd, inter[:, :]).then_inc(g["stored"], 16)
                sp.wait_ge(g["stored"], 16 * STORES * B + 1)

            @block.vector
            def _(dve):
                nc.vector.memset(eps[:, :], LN_EPS).then_inc(g["init"], 1)
                nc.vector.memset(power[:, :], -0.5).then_inc(g["init"], 1)
                nc.vector.memset(state[:, 0, :], 0.0).then_inc(g["init"], 1)
                dve.sem_inc(g["stored"], 1)
                dve.sem_inc(g["x1_ready"], 1)
                dve.wait_ge(g["const"], 16 * (len(consts) + 1))
                with dve.Fori(0, B) as it:
                    def after(name, per, n):
                        dve.wait_ge(g[name], it * per + n)

                    after("in_loaded", LOADS, LOADS)
                    nc.vector.reciprocal(rden[:, :], den[:, :]).then_inc(g["rden_ready"], 1)
                    after("rden_ready", 1, 1)
                    for half in range(2):
                        c = slice(half * HALF, half * HALF + HALF)
                        nc.vector.tensor_tensor(headT[:, c], oT[:, c], rden[:, c], ALU.mult).then_inc(g["head_ready"], 1)
                    after("gated", 1, 1)
                    after("stored", 16 * STORES, 1)
                    for half in range(2):
                        t4 = slice(4 * half, 4 * half + 4)
                        after("s_done", 2, half + 1)
                        nc.vector.tensor_tensor(x1[:, t4, :], ps[:, half, :].rearrange("p (t c) -> p t c", c=D),
                                                gate[:, t4, :], ALU.mult).then_inc(g["x1_half"], 1)
                    for half in range(2):
                        t4 = slice(4 * half, 4 * half + 4)
                        after("x1_half", 2, half + 1)
                        nc.vector.tensor_tensor(x1[:, t4, :], x1[:, t4, :], x[:, t4, :], ALU.add).then_inc(g["x1_ready"], 1)
                    for t in range(NT):
                        if t % 4 == 0:
                            after("x1_ready", 2, t // 4 + 2)
                        nc.vector.bn_stats(stat[:, t, :], x1[:, t, :]).then_inc(g["stats"], 1)
                    after("stats", NT, NT)
                    nc.vector.memset(held[:, :], 0.0)
                    for t in range(NT):
                        nc.vector.bn_aggr(mom[:, t, :], stat[:, t, :]).then_inc(g["moments"], 1)
                    after("rstd_ready", 1, 1)
                    for t in range(NT):
                        nc.vector.tensor_scalar(xn[:, t, :], x1[:, t, :], mom[:, t, 0:1], rstd[:, t:t + 1],
                                                ALU.subtract, ALU.mult).then_inc(g["xn_ready"], 1)
                    for half in range(2):
                        c = slice(half * HALF, half * HALF + HALF)
                        after("projected", 2, half + 1)
                        for j in range(4):
                            ins = nc.vector.tensor_tensor(terms[:, half, j, :], ps[:, 2 + j, :], tables[:, j, c], ALU.mult)
                        ins.then_inc(g["terms_ready"], 1)
                    after("router_done", 1, 1)
                    nc.vector.tensor_tensor(logits[:, :, :], ps[:, 0, 0:NT * NE].rearrange("p (t e) -> p t e", e=NE),
                                            b_router[:, None, :].broadcast_to((P, NT, NE)),
                                            ALU.add).then_inc(g["logits_ready"], 1)
                    for half in range(2):
                        after("chunk_done", 2, half + 1)
                        nc.vector.tensor_tensor(chunk_state[:, 4 * half:4 * half + 4, :],
                                                ps[:, 6 + half, :].rearrange("p (t c) -> p t c", c=P),
                                                same_head[:, None, :].broadcast_to((P, 4, P)),
                                                ALU.mult).then_inc(g["chunk_ready"], 1)
                    after("chunk_ready", 2, 2)
                    for t in range(1, NT):
                        if t > 1:
                            after("state_ready", NT - 1, t - 1)
                        nc.vector.tensor_tensor(state[:, t, :], state[:, t - 1, :], chunk_state[:, t - 1, :],
                                                ALU.add).then_inc(g["state_ready"], 1)

            @block.gpsimd
            def _(pool):
                pool.wait_ge(g["init"], 3)
                with pool.Fori(0, B) as it:
                    pool.wait_ge(g["moments"], it * NT + NT)
                    nc.gpsimd.tensor_tensor(var[:, :], mom[:, :, 1], eps[:, :], ALU.add).then_inc(g["var_ready"], 1)
                    pool.wait_ge(g["var_ready"], it + 1)
                    nc.gpsimd.tensor_tensor(rstd[:, :], var[:, :], power[:, :], ALU.pow).then_inc(g["rstd_ready"], 1)
                    for half in range(2):
                        c = slice(half * HALF, half * HALF + HALF)
                        pool.wait_ge(g["terms_ready"], it * 2 + half + 1)
                        for i in range(2):
                            ins = nc.gpsimd.tensor_tensor(roped[:, i, c], terms[:, half, 2 * i, :],
                                                          terms[:, half, 2 * i + 1, :], ALU.add)
                        ins.then_inc(g["roped_ready"], 1)
                        pool.wait_ge(g["hi_ready"], it * 2 + half + 1)
                        for i in range(2):
                            ins = nc.gpsimd.tensor_tensor(rest[:, i, c], roped[:, i, c], hi[:, i, c], ALU.subtract)
                        ins.then_inc(g["rest_ready"], 1)
                        pool.wait_ge(g["mid_ready"], it * 2 + half + 1)
                        for i in range(2):
                            ins = nc.gpsimd.tensor_tensor(lo[:, i, c], rest[:, i, c], mid[:, i, c], ALU.subtract)
                        ins.then_inc(g["lo_ready"], 1)

            @block.scalar
            def _(act):
                act.wait_ge(g["init"], 3)
                with act.Fori(0, B) as it:
                    act.wait_ge(g["u_loaded"], it * 16 + 16)
                    nc.scalar.activation(gate[:, :, :], u[:, :, :], ACT.Silu).then_inc(g["gated"], 1)
                    for half in range(2):
                        act.wait_ge(g["turned"], it * 2 + half + 1)
                        nc.scalar.copy(xnT[:, half * HALF:half * HALF + HALF], ps[:, half, :]).then_inc(g["xnT_ready"], 1)
                    act.wait_ge(g["stored"], it * (16 * STORES) + 1)
                    for half in range(2):
                        t4 = slice(4 * half, 4 * half + 4)
                        act.wait_ge(g["vg_done"], it * 4 + half + 1)
                        nc.scalar.copy(v[:, t4, :], ps[:, 6 + half, :].rearrange("p (t c) -> p t c", c=D)
                                       ).then_inc(g["v_kept"], 1)
                    for half in range(2):
                        t4 = slice(4 * half, 4 * half + 4)
                        act.wait_ge(g["vg_done"], it * 4 + half + 3)
                        nc.scalar.activation(gate1[:, t4, :], ps[:, 6 + half, :].rearrange("p (t c) -> p t c", c=D),
                                             ACT.Silu).then_inc(g["g_kept"], 1)
                    for half in range(2):
                        c = slice(half * HALF, half * HALF + HALF)
                        act.wait_ge(g["roped_ready"], it * 2 + half + 1)
                        nc.scalar.copy(hi[:, :, c], roped[:, :, c]).then_inc(g["hi_ready"], 1)
                        act.wait_ge(g["rest_ready"], it * 2 + half + 1)
                        nc.scalar.copy(mid[:, :, c], rest[:, :, c]).then_inc(g["mid_ready"], 1)
                    for half in range(2):
                        act.wait_ge(g["k_turned"], it * 2 + half + 1)
                        nc.scalar.copy(k_tok[:, 4 * half:4 * half + 4, :],
                                       ps[:, 2 + half, :].rearrange("p (t c) -> p t c", c=P)).then_inc(g["k_kept"], 1)
                    for half in range(2):
                        act.wait_ge(g["inter_done"], it * 2 + half + 1)
                        nc.scalar.copy(inter[:, half * HALF:half * HALF + HALF], ps[:, 4 + half, :]
                                       ).then_inc(g["inter_kept"], 1)

            @block.tensor
            def _(pe):
                pe.wait_ge(g["const"], 16 * (len(consts) + 1))
                pe.wait_ge(g["init"], 3)
                with pe.Fori(0, B) as it:
                    def after(name, per, n):
                        pe.wait_ge(g[name], it * per + n)

                    for t in range(NT):
                        if t % 4 == 0:
                            after("head_ready", 2, t // 4 + 1)
                        ins = nc.tensor.matmul(ps[:, t // 4, (t % 4) * P:(t % 4) * P + P], headT[:, t * P:t * P + P],
                                               w_out[:, :], start=True, stop=True)
                        if t % 4 == 3:
                            ins.then_inc(g["s_done"], 1)
                    for t in range(NT):
                        after("xn_ready", NT, t + 1)
                        ins = nc.tensor.transpose(ps[:, t // 4, (t % 4) * P:(t % 4) * P + P], xn[:, t, :], ident[:, :])
                        if t % 4 == 3:
                            ins.then_inc(g["turned"], 1)

                    def project(half):
                        for j in range(4):
                            ins = nc.tensor.matmul(ps[:, 2 + j, :], w_proj[:, j, :],
                                                   xnT[:, half * HALF:half * HALF + HALF], start=True, stop=True)
                        ins.then_inc(g["projected"], 1)

                    def by_token(i):
                        for t in range(NT):
                            if i == 1 and t % 4 == 0:
                                after("v_kept", 2, t // 4 + 1)
                            ins = nc.tensor.matmul(ps[:, 6 + t // 4, (t % 4) * P:(t % 4) * P + P], xnT[:, t * P:t * P + P],
                                                   w_vg[:, i, :], start=True, stop=True)
                            if t % 4 == 3:
                                ins.then_inc(g["vg_done"], 1)

                    after("xnT_ready", 2, 1)
                    project(0)
                    after("xnT_ready", 2, 2)
                    by_token(0)
                    after("terms_ready", 2, 1)
                    project(1)
                    for t in range(NT):
                        ins = nc.tensor.matmul(ps[:, 0, t * NE:t * NE + NE], xnT[:, t * P:t * P + P], w_router[:, :],
                                               start=True, stop=True)
                    ins.then_inc(g["router_done"], 1)
                    by_token(1)
                    after("terms_ready", 2, 2)
                    for t in range(NT):
                        if t % 4 == 0:
                            after("roped_ready", 2, t // 4 + 1)
                        ins = nc.tensor.transpose(ps[:, 2 + t // 4, (t % 4) * P:(t % 4) * P + P],
                                                  roped[:, 1, t * P:t * P + P], ident[:, :])
                        if t % 4 == 3:
                            ins.then_inc(g["k_turned"], 1)
                    for t in range(NT):
                        if t % 4 == 0:
                            after("k_kept", 2, t // 4 + 1)
                            after("g_kept", 2, t // 4 + 1)
                        ins = nc.tensor.matmul(ps[:, 6 + t // 4, (t % 4) * P:(t % 4) * P + P], k_tok[:, t, :], v[:, t, :],
                                               start=True, stop=True)
                        if t % 4 == 3:
                            ins.then_inc(g["chunk_done"], 1)
                    for t in range(NT):
                        if t:
                            after("state_ready", NT - 1, t)
                        ins = nc.tensor.matmul(ps[:, 4 + t // 4, (t % 4) * P:(t % 4) * P + P], state[:, t, :],
                                               roped[:, 0, t * P:t * P + P], start=True, stop=True)
                        if t % 4 == 3:
                            ins.then_inc(g["inter_done"], 1)


def retention(nc, A):
    units = [(hq, t, c) for t in range(1, NT) for c in range((t + 3) // 4) for hq in range(4)]
    PER_TILE = len(units) // NT
    MINE = len(units) // 2
    VCOLS = 4 * DH + VW - DH
    with Space(nc) as m:
        ps = m.psum("psD")
        rows = {"act": [ps[:, 0, :], ps[:, 1, :]], "dve": [ps[:, 2, :], ps[:, 3, :]]}
        pt = [ps[:, 4:6, 2 * P * i:2 * P * i + 2 * P].rearrange("p b (a i) -> p a b i", a=2) for i in range(2)]
        po, pd = ps[:, 6, :], ps[:, 7, :]
        causal = m.sb("causalD", [P, P])
        ones = m.sb("onesD", [P, VW])
        q, k = m.sb("qD", [P, QUADS, 2, S], BF16), m.sb("kD", [P, QUADS, 2, S], BF16)
        v = m.sb("vD", [P, QUADS, NT, VCOLS])
        kept, absd = m.sb("keptD", [P, 2, 4 * P]), m.sb("absD", [P, 2, 4 * P])
        sums = m.sb("sumsD", [P, QUADS, len(units)])
        out, diag = m.sb("outD", [P, 2, HALF]), m.sb("diagD", [P, 2, HALF])

        loaded, init = m.sem("constD"), m.sem("initD")
        in_loaded = [m.sem(f"in_loadedD{s}") for s in range(QUADS)]
        pt_done, masked, abs_done, pv_done = (m.sem(n) for n in ("pt_doneD", "maskedD", "abs_doneD", "pv_doneD"))
        out_kept, out_stored = m.sem("out_keptD"), [m.sem(f"out_storedD{p}") for p in range(2)]
        sums_stored = [m.sem(f"sums_storedD{s}") for s in range(QUADS)]
        unit_done = {e: m.sem("unit_doneD_" + e) for e in ("act", "dve")}
        unit_read = {e: m.sem("unit_readD_" + e) for e in ("act", "dve")}
        LOADS = 16 * 5

        def sum_unit(eng, name, it, s, g):
            i = g // 2
            eng.wait_ge(unit_done[name], it * (MINE * QUADS) + MINE * s + i + 1)
            hq, t, c = units[g]
            w = min(HALF, P * t - HALF * c)
            col = MINE * (g % 2) + i
            return rows[name][i % 2][:, 0:w], sums[:, s, col:col + 1]

        with nc.Block() as block:
            @block.sync
            def _(sp):
                sp.dma_start(causal[:, :], A["causal"]).then_inc(loaded, 16)
                sp.wait_ge(init, 2)

                def load(s, qd, kd, vd):
                    for p in range(2):
                        hs = slice(4 * s + 2 * p, 4 * s + 2 * p + 2)
                        sp.dma_start(q[:, s, p, :], qd[:, hs].rearrange("a h r s -> (a h r) s")).then_inc(in_loaded[s], 16)
                        sp.dma_start(k[:, s, p, :], kd[:, hs].rearrange("a h r s -> (a h r) s")).then_inc(in_loaded[s], 16)
                    n = min(VCOLS, D - 4 * DH * s)
                    sp.dma_start(v[:, s, :, 0:n], vd.rearrange("a (t p) c -> p (a t) c", p=P)[
                        :, :, 4 * DH * s:4 * DH * s + n]).then_inc(in_loaded[s], 16)

                for s in range(QUADS):
                    load(s, A["q1"][0:1], A["k1"][0:1], A["v1"][0:1])
                with sp.Fori(0, B) as it:
                    qd, kd, vd = one(A["q1_next"], it), one(A["k1_next"], it), one(A["v1_next"], it)
                    od, dd, sd = one(A["o1"], it), one(A["diag"], it), one(A["sums"], it)
                    kept_at = [sp.snap(it * 8 + 1 + e + 1) for e in range(8)]
                    units_read = [sp.snap(it * (MINE * QUADS) + MINE * (s + 1)) for s in range(QUADS)]
                    for s in range(QUADS):
                        for c in range(2):
                            sp.wait_ge(out_kept, kept_at[2 * s + c])
                            for hq in range(4):
                                sp.dma_start(od[:, 4 * s + hq, :, c * HALF:(c + 1) * HALF].rearrange("a r s -> (a r) s"),
                                             out[VW * hq:VW * hq + DH, c, :]).then_inc(out_stored[c], 16)
                            sp.dma_start(dd[:, s, 4 * c:4 * c + 4, :].rearrange("a t f -> (a t) f"),
                                         diag[0:P:VW, c, :]).then_inc(out_stored[c], 16)
                        for i, name in enumerate(("act", "dve")):
                            c = slice(MINE * i, MINE * i + MINE)
                            sp.wait_ge(unit_read[name], units_read[s])
                            sp.dma_start(sd[:, s, :, c].rearrange("a p u -> (a p) u"), sums[:, s, c]
                                         ).then_inc(sums_stored[s], 16)
                        load(s, qd, kd, vd)
                for s in range(QUADS):
                    sp.wait_ge(in_loaded[s], LOADS * (B + 1))
                    sp.wait_ge(sums_stored[s], 32 * B + 1)
                for c in range(2):
                    sp.wait_ge(out_stored[c], 80 * B * QUADS + 1)

            @block.vector
            def _(dve):
                nc.vector.memset(v[:, :, :, :], 0.0).then_inc(init, 1)
                nc.vector.memset(ones[:, :], 1.0).then_inc(init, 1)
                for c in range(2):
                    dve.sem_inc(out_stored[c], 1)
                for s in range(QUADS):
                    dve.sem_inc(sums_stored[s], 1)
                dve.wait_ge(loaded, 16)
                with dve.Fori(0, B) as it:
                    for s in range(QUADS):
                        for t in range(NT):
                            n = NT * s + t
                            dve.wait_ge(pt_done, it * (NT * QUADS) + n + 1)
                            dve.wait_ge(pv_done, it * (NT * QUADS) + n + 1)
                            nc.vector.tensor_tensor(kept[:, t % 2, :].rearrange("p (a b i) -> p a b i", a=2, b=2), pt[t % 2],
                                                    causal[:, None, None, :].broadcast_to((P, 2, 2, P)), ALU.mult).then_inc(masked, 1)
                            if t == 0:
                                dve.wait_ge(sums_stored[s], it * 32 + 1)
                            for g in range(PER_TILE * t, PER_TILE * t + PER_TILE):
                                if g % 2 == 1:
                                    src, dst = sum_unit(dve, "dve", it, s, g)
                                    nc.vector.tensor_reduce(dst, src, AX.X, ALU.add,
                                                            apply_absolute_value=True).then_inc(unit_read["dve"], 1)

            @block.scalar
            def _(act):
                act.sem_inc(pv_done, 2)
                act.sem_inc(out_kept, 1)
                with act.Fori(0, B) as it:
                    def keep(e):
                        act.wait_ge(pv_done, it * (NT * QUADS) + 4 * (e + 1) + 2)
                        act.wait_ge(out_stored[e % 2], it * (80 * QUADS) + 80 * (e // 2) + 1)
                        nc.scalar.copy(out[:, e % 2, :], po)
                        nc.scalar.copy(diag[:, e % 2, :], pd).then_inc(out_kept, 1)

                    for s in range(QUADS):
                        for t in range(NT):
                            n = NT * s + t
                            act.wait_ge(masked, it * (NT * QUADS) + n + 1)
                            nc.scalar.activation(absd[:, t % 2, :], kept[:, t % 2, :], ACT.Abs).then_inc(abs_done, 1)
                            if t == 0:
                                act.wait_ge(sums_stored[s], it * 32 + 1)
                            for g in range(PER_TILE * t, PER_TILE * t + PER_TILE):
                                if g % 2 == 0:
                                    src, dst = sum_unit(act, "act", it, s, g)
                                    nc.scalar.activation(src, src, ACT.Abs, accum_out=dst).then_inc(unit_read["act"], 1)
                            if t % 4 == 1 and n > 1:
                                keep(n // 4 - 1)
                    keep(2 * QUADS - 1)

            @block.tensor
            def _(pe):
                pe.wait_ge(init, 2)
                with pe.Fori(0, B) as it:
                    def inside(s, t):
                        n = NT * s + t
                        pe.wait_ge(abs_done, it * (NT * QUADS) + n + 1)
                        if t % 4 == 0:
                            pe.wait_ge(out_kept, it * 8 + n // 4 + 1)
                        c = slice((t % 4) * P, (t % 4) * P + P)
                        for hq in range(4):
                            nc.tensor.matmul(po[VW * hq:VW * hq + VW, c], v[:, s, t, DH * hq:DH * hq + VW],
                                             kept[:, t % 2, hq * P:hq * P + P], start=True, stop=True)
                        r = VW * (t % 4)
                        nc.tensor.matmul(pd[r:r + VW, :], ones[:, :], absd[:, t % 2, :], start=True,
                                         stop=True).then_inc(pv_done, 1)

                    before = None
                    for s in range(QUADS):
                        pe.wait_ge(in_loaded[s], it * LOADS + LOADS)
                        for t in range(NT):
                            n = NT * s + t
                            if n >= 2:
                                pe.wait_ge(masked, it * (NT * QUADS) + n - 1)
                            ts = slice(t * P, t * P + P)
                            for hq in range(4):
                                r = slice(ROWS * (hq % 2), ROWS * (hq % 2) + ROWS)
                                ins = nc.tensor.matmul(pt[t % 2][:, hq // 2, hq % 2, :], k[r, s, hq // 2, ts],
                                                       q[r, s, hq // 2, ts], start=True, stop=True)
                            ins.then_inc(pt_done, 1)
                            for g in range(PER_TILE * t, PER_TILE * t + PER_TILE):
                                hq, tq, c = units[g]
                                e, i = ("act", "dve")[g % 2], g // 2
                                r = slice(ROWS * (hq % 2), ROWS * (hq % 2) + ROWS)
                                w = min(HALF, P * tq - HALF * c)
                                done = MINE * s + i
                                if done >= 2:
                                    pe.wait_ge(unit_read[e], it * (MINE * QUADS) + done - 1)
                                nc.tensor.matmul(rows[e][i % 2][:, 0:w], q[r, s, hq // 2, tq * P:tq * P + P],
                                                 k[r, s, hq // 2, HALF * c:HALF * c + w], start=True,
                                                 stop=True).then_inc(unit_done[e], 1)
                            if before:
                                inside(*before)
                            before = (s, t)
                    inside(*before)
                    for e in ("act", "dve"):
                        pe.wait_ge(unit_read[e], it * (MINE * QUADS) + MINE * QUADS)


def route(nc, A):
    TK = 2 * NTILES
    with Space(nc) as m:
        ps = m.psum("psR")
        before, ones_b = m.sb("beforeR", [P, P], BF16), m.sb("onesR", [P, P], BF16)
        rank = m.sb("rankR", [P, NE])
        ones = m.sb("ones_scanR", [P, TK])
        L = m.sb("logitsR", [P, NTILES, NE])
        top, z, e = m.sb("topR", [P, NTILES]), m.sb("zR", [P, NTILES, NE]), m.sb("eR", [P, NTILES, NE])
        total, inv = m.sb("totalR", [P, NTILES]), m.sb("invR", [P, NTILES])
        p = [m.sb(f"pR{i}", [P, NTILES, NE]) for i in range(2)]
        best = m.sb("bestR", [P, 2, NTILES])
        at = m.sb("atR", [P, 2, NTILES, NE])
        first = m.sb("firstR", [P, 2, NTILES])
        chosen = m.sb("chosenR", [P, 2, NTILES, NE])
        both, winv = m.sb("bothR", [P, NTILES]), m.sb("winvR", [P, NTILES])
        w, valid = m.sb("wR", [P, 2, NTILES]), m.sb("validR", [P, 2, NTILES])
        hot, hot_b = m.sb("hotR", [P, 2, NTILES, NE]), m.sb("hot_bR", [P, 2, NTILES, NE], BF16)
        upto = m.sb("uptoR", [P, TK, NE])
        pos = m.sb("posR", [P, TK, NE])
        own = m.sb("ownR", [P, TK])
        keep = m.sb("keepR", [P, TK])
        slot = m.sb("slotR", [P, TK])
        index = m.sb("indexR", [P, 2, NTILES], I32)
        weight = m.sb("weightR", [P, 2, NTILES])

        loaded, step, shifted, exped = m.sem("constR"), m.sem("stepR"), m.sem("shiftedR"), m.sem("expedR")
        hot_ready, counted, routed, stored = m.sem("hot_readyR"), m.sem("countedR"), m.sem("routedR"), m.sem("storedR")

        def spread(ap, n=NE):
            return ap[:, :, None].broadcast_to((P, ap.shape[1], n))

        def flat(ap):
            return ap[:, :, :, :].rearrange("p k t e -> p (k t) e")

        with nc.Block() as block:
            @block.sync
            def _(sp):
                for dst, src in ((before, A["before"]), (rank, A["rank"].broadcast_to((P, NE)))):
                    sp.dma_start(dst[:, :], src).then_inc(loaded, 16)
                sp.dma_start(L[:, :, :].rearrange("p (b t) e -> p b (t e)", b=B),
                             A["logits"].rearrange("b p f -> p b f")).then_inc(loaded, 16)
                sp.wait_ge(routed, 2)
                n = 0
                for b in range(B):
                    for kk in range(2):
                        sp.dma_start(A["index"][b, :, kk * NT:kk * NT + NT], index[:, kk, b * NT:b * NT + NT]).then_inc(stored, 16)
                        sp.dma_start(A["weight"][b, :, kk * NT:kk * NT + NT], weight[:, kk, b * NT:b * NT + NT]).then_inc(stored, 16)
                        n += 2
                sp.wait_ge(stored, 16 * n)

            @block.scalar
            def _(act):
                act.wait_ge(shifted, 1)
                nc.scalar.activation(e[:, :, :], z[:, :, :], ACT.Exp).then_inc(exped, 1)

            @block.tensor
            def _(pe):
                pe.wait_ge(loaded, 48)
                pe.wait_ge(hot_ready, 1)
                rhs = hot_b[:, :, :, :].rearrange("p k t e -> p (k t e)")
                nc.tensor.matmul(ps[:, 0, :], before[:, :], rhs, start=True, stop=True)
                nc.tensor.matmul(ps[:, 1, :], ones_b[:, :], rhs, start=True, stop=True).then_inc(counted, 1)

            @block.vector
            def _(dve):
                V = nc.vector
                link, _ = linker(dve, step, 0)
                link(V.memset(ones[:, :], 1.0))
                link(V.memset(ones_b[:, :], 1.0))
                dve.wait_ge(loaded, 48)
                link(V.tensor_reduce(top[:, :], L[:, :, :], AX.X, ALU.max))
                V.tensor_tensor(z[:, :, :], L[:, :, :], spread(top), ALU.subtract).then_inc(shifted, 1)
                dve.wait_ge(exped, 1)
                link(V.tensor_reduce(total[:, :], e[:, :, :], AX.X, ALU.add))
                link(V.reciprocal(inv[:, :], total[:, :]))
                link(V.tensor_tensor(p[0][:, :, :], e[:, :, :], spread(inv), ALU.mult))
                ranks = rank[:, None, :].broadcast_to((P, NTILES, NE))
                for kk in range(2):
                    link(V.tensor_reduce(best[:, kk, :], p[kk][:, :, :], AX.X, ALU.max))
                    link(V.tensor_tensor(at[:, kk], p[kk][:, :, :], spread(best[:, kk, :]), ALU.is_equal))
                    link(V.tensor_tensor(at[:, kk], at[:, kk], ranks, ALU.mult))
                    link(V.tensor_reduce(first[:, kk, :], at[:, kk], AX.X, ALU.max))
                    link(V.tensor_tensor(chosen[:, kk], at[:, kk], spread(first[:, kk, :]), ALU.is_equal))
                    if kk == 0:
                        link(V.scalar_tensor_tensor(p[1][:, :, :], chosen[:, 0], -2.0, p[0][:, :, :], ALU.mult, ALU.add))
                link(V.tensor_tensor(both[:, :], best[:, 0, :], best[:, 1, :], ALU.add))
                link(V.tensor_scalar(both[:, :], both[:, :], TOP_EPS, None, ALU.add))
                link(V.reciprocal(winv[:, :], both[:, :]))
                link(V.tensor_tensor(w[:, :, :], best[:, :, :], winv[:, None, :].broadcast_to((P, 2, NTILES)), ALU.mult))
                link(V.tensor_scalar(valid[:, :, :], w[:, :, :], TOP_EPS, None, ALU.is_gt))
                link(V.tensor_tensor(flat(hot), flat(chosen), spread(valid[:, :, :].rearrange("p k t -> p (k t)")), ALU.mult))
                V.tensor_copy(flat(hot_b), flat(hot)).then_inc(hot_ready, 1)
                dve.wait_ge(counted, 1)
                inside = ps[:, 0, :].rearrange("p (g e) -> p g e", e=NE)
                tile_n = ps[:, 1, :].rearrange("p (g e) -> p g e", e=NE)
                for x in range(NE):
                    ins = V.tensor_tensor_scan(upto[:, :, x], ones[:, :], tile_n[:, :, x], 0.0, ALU.mult, ALU.add)
                link(ins)
                link(V.tensor_tensor(pos[:, :, :], upto[:, :, :], tile_n, ALU.subtract))
                link(V.tensor_tensor(pos[:, :, :], pos[:, :, :], inside, ALU.add))
                link(V.tensor_tensor(pos[:, :, :], pos[:, :, :], flat(hot), ALU.mult))
                link(V.tensor_reduce(own[:, :], pos[:, :, :], AX.X, ALU.add))
                flat2 = [a[:, :, :].rearrange("p k t -> p (k t)") for a in (valid, first, w, weight, index)]
                link(V.scalar_tensor_tensor(keep[:, :], own[:, :], float(CAP), flat2[0], ALU.is_lt, ALU.mult))
                link(V.scalar_tensor_tensor(slot[:, :], flat2[1], -float(SLOTS), own[:, :], ALU.mult, ALU.add))
                link(V.tensor_scalar(slot[:, :], slot[:, :], float(NE * SLOTS - NO_SLOT), None, ALU.add))
                link(V.tensor_tensor(slot[:, :], slot[:, :], keep[:, :], ALU.mult))
                V.tensor_scalar(flat2[4], slot[:, :], float(NO_SLOT), None, ALU.add).then_inc(routed, 1)
                V.tensor_tensor(flat2[3], flat2[2], keep[:, :], ALU.mult).then_inc(routed, 1)


def scatter(nc, A):
    with Space(nc) as m:
        x = m.sb("xS", [P, NT, D])
        index = m.sb("indexS", [P, 2 * NT], I32)
        loaded, started, scattered = m.sem("loadedS"), m.sem("startedS"), m.sem("scatteredS")
        with nc.Block() as block:
            @block.gpsimd
            def _(pool):
                with pool.Fori(0, B) as it:
                    xd = one(A["xn1"], it).rearrange("a (t p) c -> p (a t) c", p=P)
                    pool.dma_start(x[:, :, :], xd).then_inc(loaded, 16)
                    pool.dma_start(index[:, :], one(A["index"], it).rearrange("a p k -> (a p) k")).then_inc(loaded, 16)
                    all_rows = pool.snap(it * (16 * 2 * NT) + 16 * 2 * NT)
                    pool.wait_ge(loaded, it * 32 + 32)
                    pool.sem_inc(started, 1)
                    for kk in range(2):
                        for t in range(NT):
                            pool.indirect_dma_start(
                                A["slot_x"], bass.IndirectOffsetOnAxis(ap=index[:, kk * NT + t:kk * NT + t + 1], axis=0),
                                x[:, t, :], None, bounds_check=ALL_SLOTS - 1, oob_is_err=False).then_inc(scattered, 16)
                    pool.wait_ge(scattered, all_rows)
                    pool.sem_inc(started, 1)


def experts(nc, A):
    PART = SLOTS // 2
    with Space(nc) as m:
        ps = m.psum("psE")
        ident = m.sb("identE", [P, P])
        x = m.sb("xE", [P, 2, SLOT_TILES, D])
        fc1, fc2 = m.sb("fc1E", [P, 2, FF]), m.sb("fc2E", [P, 2, FC, D])
        b1, b2, ls = m.sb("b1E", [P, 2, FC]), m.sb("b2E", [P, 2, D]), m.sb("lsE", [P, 2, D])
        xT = m.sb("xTE", [P, SLOTS])
        hT = m.sb("hTE", [P, FC, SLOTS])
        y, z = m.sb("yE", [P, SLOT_TILES, D]), m.sb("zE", [P, SLOT_TILES, D])
        scaled = m.sb("scaledE", [P, SLOT_TILES, D])
        loaded = m.sem("constE")
        in_loaded = [m.sem(f"in_loadedE{i}") for i in range(2)]
        turned, xT_ready, h_done, gelu_done = (m.sem(n) for n in ("turnedE", "xT_readyE", "h_doneE", "gelu_doneE"))
        y_done, y_biased, y_scaled, z_ready, stored = (m.sem(n) for n in ("y_doneE", "y_biasedE", "y_scaledE", "z_readyE", "storedE"))
        LOADS = 16 * 6
        with nc.Block() as block:
            @block.sync
            def _(sp):
                sp.dma_start(ident[:, :], A["ident"]).then_inc(loaded, 16)

                def load(i, src):
                    xd, f1, f2, c1, c2, l = src
                    for dst, s in ((x[:, i], xd), (fc1[:, i, :], f1), (fc2[:, i], f2), (b1[:, i, :], c1), (b2[:, i, :], c2),
                                   (ls[:, i, :], l)):
                        sp.dma_start(dst, s).then_inc(in_loaded[i], 16)

                def sources(sel):
                    return (sel(A["slot_x"].rearrange("(e t p) c -> e p t c", t=SLOT_TILES, p=P)).rearrange("a p t c -> (a p) t c"),
                            sel(A["fc1T"]).rearrange("a c h -> (a c) h"),
                            sel(A["fc2T"]).rearrange("a h q c -> (a h) q c"),
                            sel(A["fc1_b"]).rearrange("a p q -> (a p) q"),
                            sel(A["fc2_b"]).broadcast_to((P, D)), sel(A["ls"]).broadcast_to((P, D)))

                load(0, sources(lambda a: a[0:1]))
                with sp.Fori(0, NE // 2) as it:
                    src1 = sources(lambda a: a[bass.ds(it * 2 + 1, 1)])
                    src0 = sources(lambda a: a[bass.ds((it * 2 + 2) % NE, 1)])
                    out = [A["slot_y"][0:ALL_SLOTS, :].rearrange("(e t p) c -> e p t c", t=SLOT_TILES, p=P)[
                        bass.ds(it * 2 + i, 1)].rearrange("a p t c -> (a p) t c") for i in range(2)]
                    z_at = [sp.snap(it * 2 + i + 1) for i in range(2)]
                    load(1, src1)
                    for i in range(2):
                        sp.wait_ge(z_ready, z_at[i])
                        sp.dma_start(out[i], z[:, :, :]).then_inc(stored, 16)
                        if i == 0:
                            load(0, src0)
                sp.wait_ge(in_loaded[0], LOADS * (NE // 2 + 1))
                sp.wait_ge(stored, 16 * NE + 1)

            @block.tensor
            def _(pe):
                pe.wait_ge(loaded, 16)
                with pe.Fori(0, NE // 2) as it:
                    for i in range(2):
                        pe.wait_ge(in_loaded[i], it * LOADS + LOADS)
                        for t in range(SLOT_TILES):
                            ins = nc.tensor.transpose(ps[:, t // 4, (t % 4) * P:(t % 4) * P + P], x[:, i, t, :], ident[:, :])
                        ins.then_inc(turned, 1)
                        pe.wait_ge(xT_ready, it * 2 + i + 1)
                        for c in range(FC):
                            for h in range(2):
                                n = 2 * c + h
                                if n >= 4:
                                    pe.wait_ge(gelu_done, it * (4 * FC) + 2 * FC * i + n - 3)
                                nc.tensor.matmul(ps[:, 2 + n % 4, 0:PART], fc1[:, i, c * P:c * P + P],
                                                 xT[:, h * PART:h * PART + PART], start=True, stop=True).then_inc(h_done, 1)
                        pe.wait_ge(gelu_done, it * (4 * FC) + 2 * FC * (i + 1))
                        pe.wait_ge(y_biased, it * 2 + i + 1)
                        for t in range(SLOT_TILES):
                            for c in range(FC):
                                ins = nc.tensor.matmul(ps[:, 6 + t // 4, (t % 4) * P:(t % 4) * P + P],
                                                       hT[:, c, t * P:t * P + P], fc2[:, i, c, :], start=(c == 0),
                                                       stop=(c == FC - 1))
                        ins.then_inc(y_done, 1)

            @block.scalar
            def _(act):
                with act.Fori(0, NE // 2) as it:
                    for i in range(2):
                        act.wait_ge(turned, it * 2 + i + 1)
                        nc.scalar.copy(xT[:, :], ps[:, 0:2, :].rearrange("p b f -> p (b f)")[:, 0:SLOTS]).then_inc(xT_ready, 1)
                        for c in range(FC):
                            for h in range(2):
                                n = 2 * c + h
                                act.wait_ge(h_done, it * (4 * FC) + 2 * FC * i + n + 1)
                                nc.scalar.activation(hT[:, c, h * PART:h * PART + PART], ps[:, 2 + n % 4, 0:PART], ACT.Gelu,
                                                     bias=b1[:, i, c:c + 1]).then_inc(gelu_done, 1)

            @block.vector
            def _(dve):
                dve.sem_inc(stored, 1)
                dve.sem_inc(y_biased, 1)
                with dve.Fori(0, NE // 2) as it:
                    for i in range(2):
                        dve.wait_ge(y_done, it * 2 + i + 1)
                        nc.vector.tensor_tensor(y[:, :, :], ps[:, 6:8, :].rearrange("p b (t c) -> p (b t) c", c=D)[:, 0:SLOT_TILES, :],
                                                b2[:, i, None, :].broadcast_to((P, SLOT_TILES, D)), ALU.add).then_inc(y_biased, 1)
                        dve.wait_ge(y_biased, it * 2 + i + 2)
                        nc.vector.tensor_tensor(scaled[:, :, :], y[:, :, :], ls[:, i, None, :].broadcast_to((P, SLOT_TILES, D)),
                                                ALU.mult).then_inc(y_scaled, 1)
                        dve.wait_ge(stored, it * 32 + 16 * i + 1)
                        dve.wait_ge(y_scaled, it * 2 + i + 1)
                        nc.vector.tensor_tensor(z[:, :, :], scaled[:, :, :], x[:, i], ALU.add).then_inc(z_ready, 1)


def finish(nc, A):
    U = 10
    unit_of = {}
    for i, (t, c) in enumerate((t, c) for t in range(1, NT) for c in range((t + 3) // 4)):
        unit_of[t, c] = i
    with Space(nc) as m:
        ps = m.psum("psF")
        ident = m.sb("identF", [P, P])
        inter, intra = m.sb("interF", [P, S]), m.sb("intraF", [P, S])
        sums = m.sb("sumsF", [P, QUADS, 2, U, 2])
        diag = m.sb("diagF", [P, P])
        gate, x1 = m.sb("gateF", [P, NT, D]), m.sb("x1F", [P, NT, D])
        index, weight = m.sb("indexF", [P, 2 * NT], I32), m.sb("weightF", [P, 2 * NT])
        rows = m.sb("rowsF", [P, 2, NT, D])
        outT = m.sb("outTF", [P, S])
        den, rden = m.sb("denF", [P, NT, H]), m.sb("rdenF", [P, NT, H])
        ret, sq = m.sb("retF", [P, NT, D]), m.sb("sqF", [P, NT, D])
        ms, rms = m.sb("msF", [P, NT * H]), m.sb("rmsF", [P, NT * H])
        power = m.sb("powF", [P, NT * H])
        moe, half_moe = m.sb("moeF", [P, NT, D]), m.sb("half_moeF", [P, NT, D])
        res = m.sb("resF", [P, NT, D])
        names = ("const init started in_loaded idx_loaded gathered summed turned step ms_ready rms_ready moe_ready silued done stored")
        g = {n: m.sem(n + "F") for n in names.split()}
        with nc.Block() as block:
            @block.sync
            def _(sp):
                sp.dma_start(ident[:, :], A["ident"]).then_inc(g["const"], 16)
                with sp.Fori(0, B) as it:
                    tok = {n: one(A[n], it).rearrange("a (t p) c -> p (a t) c", p=P) for n in ("g1", "x1", "out")}
                    srcs = [(inter[:, :], one(A["inter"], it).rearrange("a p s -> (a p) s")),
                            (intra[:, :], one(A["o1"], it).rearrange("a h r s -> (a h r) s")),
                            (sums[:, :, :, :, :].rearrange("p q a u b -> p q (a u b)"), one(A["sums"], it).rearrange("a q p u -> p (a q) u")),
                            (diag[:, :], one(A["diag"], it).rearrange("a q t (h i) -> (a q t h) i", h=4)),
                            (weight[:, :], one(A["weight"], it).rearrange("a p k -> (a p) k")),
                            (gate[:, :, :], tok["g1"]), (x1[:, :, :], tok["x1"])]
                    d_at, free = sp.snap(it + 1 + 1), sp.snap(it + 1)
                    sp.wait_ge(g["done"], free)
                    for dst, src in srcs:
                        sp.dma_start(dst, src).then_inc(g["in_loaded"], 16)
                    sp.wait_ge(g["done"], d_at)
                    sp.dma_start(tok["out"], res[:, :, :]).then_inc(g["stored"], 16)
                sp.wait_ge(g["stored"], 16 * B + 1)

            @block.gpsimd
            def _(pool):
                pool.wait_ge(g["init"], 1)
                with pool.Fori(0, B) as it:
                    idx = one(A["index"], it).rearrange("a p k -> (a p) k")
                    at, squares = pool.snap(it + 1), pool.snap(it * 2 + 2)
                    pool.wait_ge(g["done"], at)
                    pool.sem_inc(g["started"], 1)
                    pool.dma_start(index[:, :], idx).then_inc(g["idx_loaded"], 16)
                    pool.wait_ge(g["idx_loaded"], it * 16 + 16)
                    pool.sem_inc(g["started"], 1)
                    for kk in range(2):
                        for t in range(NT):
                            pool.indirect_dma_start(
                                rows[:, kk, t, :], None, A["slot_y"],
                                bass.IndirectOffsetOnAxis(ap=index[:, kk * NT + t:kk * NT + t + 1], axis=0)
                            ).then_inc(g["gathered"], 16)
                    pool.wait_ge(g["ms_ready"], squares)
                    nc.gpsimd.tensor_tensor(rms[:, :], ms[:, :], power[:, :], ALU.pow).then_inc(g["rms_ready"], 1)

            @block.tensor
            def _(pe):
                pe.wait_ge(g["const"], 16)
                with pe.Fori(0, B) as it:
                    pe.wait_ge(g["summed"], it + 1)
                    for t in range(NT):
                        nc.tensor.transpose(ps[:, t // 4, (t % 4) * P:(t % 4) * P + P], outT[:, t * P:t * P + P], ident[:, :])
                    nc.tensor.transpose(ps[:, 2, 0:P], diag[:, :], ident[:, :]).then_inc(g["turned"], 1)

            @block.scalar
            def _(act):
                with act.Fori(0, B) as it:
                    act.wait_ge(g["moe_ready"], it + 1)
                    nc.scalar.activation(moe[:, :, :], half_moe[:, :, :], ACT.Silu).then_inc(g["silued"], 1)

            @block.vector
            def _(dve):
                V = nc.vector
                V.memset(power[:, :], -0.5).then_inc(g["init"], 1)
                dve.sem_inc(g["done"], 1)
                dve.sem_inc(g["stored"], 1)
                STEPS = 12
                with dve.Fori(0, B) as it:
                    link, count = linker(dve, g["step"], it * STEPS)
                    dve.wait_ge(g["in_loaded"], it * 112 + 112)
                    V.tensor_tensor(outT[:, :], inter[:, :], intra[:, :], ALU.add).then_inc(g["summed"], 1)
                    dve.wait_ge(g["turned"], it + 1)
                    link(V.tensor_copy(den[:, :, :].rearrange("p t (q h) -> p q t h", h=4),
                                       ps[:, 2, 0:P].rearrange("p (q t h) -> p q t h", q=QUADS, h=4)))
                    for c in range(2):
                        for t in range(1 + 4 * c, NT):
                            d = den[:, t, :].rearrange("p (q b a) -> p q a b", b=2, a=2)
                            ins = V.tensor_tensor(d, d, sums[:, :, :, unit_of[t, c], :], ALU.add)
                        link(ins)
                    link(V.tensor_scalar(den[:, :, :], den[:, :, :], 1.0, 50000.0, ALU.max, ALU.min))
                    link(V.reciprocal(rden[:, :, :], den[:, :, :]))
                    for b in range(2):
                        t4 = slice(4 * b, 4 * b + 4)
                        ins = V.tensor_tensor(ret[:, t4, :].rearrange("p t (h d) -> p (t h) d", d=DH),
                                              ps[:, b, :].rearrange("p (g d) -> p g d", d=DH),
                                              rden[:, t4, :].rearrange("p t h -> p (t h)")[:, :, None].broadcast_to((P, 4 * H, DH)),
                                              ALU.mult)
                    link(ins)
                    link(V.tensor_tensor(sq[:, :, :], ret[:, :, :], ret[:, :, :], ALU.mult))
                    link(V.tensor_reduce(ms[:, :], sq[:, :, :].rearrange("p t (h d) -> p (t h) d", d=DH), AX.X, ALU.add))
                    V.tensor_scalar(ms[:, :], ms[:, :], 1.0 / DH, RMS_EPS, ALU.mult, ALU.add).then_inc(g["ms_ready"], 2)
                    dve.wait_ge(g["rms_ready"], it + 1)
                    r3 = ret[:, :, :].rearrange("p t (h d) -> p (t h) d", d=DH)
                    link(V.tensor_tensor(r3, r3, rms[:, :, None].broadcast_to((P, NT * H, DH)), ALU.mult))
                    link(V.tensor_tensor(ret[:, :, :], ret[:, :, :], gate[:, :, :], ALU.mult))
                    dve.wait_ge(g["gathered"], it * (16 * 2 * NT) + 16 * 2 * NT)
                    for t in range(NT):
                        ins = V.tensor_scalar(half_moe[:, t, :], rows[:, 0, t, :], weight[:, t:t + 1], None, ALU.mult)
                    link(ins)
                    for t in range(NT):
                        ins = V.scalar_tensor_tensor(half_moe[:, t, :], rows[:, 1, t, :], weight[:, NT + t:NT + t + 1],
                                                     half_moe[:, t, :], ALU.mult, ALU.add)
                    ins.then_inc(g["moe_ready"], 1)
                    dve.wait_ge(g["moe_ready"], it + 1)
                    dve.wait_ge(g["silued"], it + 1)
                    dve.wait_ge(g["stored"], it * 16 + 1)
                    link(V.tensor_tensor(ret[:, :, :], ret[:, :, :], moe[:, :, :], ALU.mult))
                    V.tensor_tensor(res[:, :, :], ret[:, :, :], x1[:, :, :], ALU.add).then_inc(g["done"], 1)
                    assert count[0] == STEPS


def program(nc, A):
    fill_padding(nc, A)
    project_and_ffn(nc, A)
    attention(nc, A)
    between_layers(nc, A)
    retention(nc, A)
    route(nc, A)
    scatter(nc, A)
    experts(nc, A)
    finish(nc, A)


def constants():
    bf16 = mybir.dt.np(BF16)
    f = np.float64
    i = np.arange(S, dtype=f)
    d = np.arange(DH)
    sign = np.where(d % 2 == 0, -1.0, 1.0)
    ang0 = np.minimum(i, 255)[:, None] * (10000.0 ** (-2.0 * (d // 2) / DH))[None, :]
    rows = lambda a: np.tile(a.T, (H, 1))
    ang1 = i[:, None] * np.repeat(1.0 / 10000.0 ** np.linspace(0.0, 1.0, DH // 2), 2)[None, :]
    decay = np.log(1.0 - 2.0 ** (-5.0 - np.arange(H, dtype=f)))
    norm = 1.0 / np.sqrt(np.cumsum(np.exp(decay[:, None] * i[None, :]), axis=1))
    qs = np.repeat(np.exp(decay[:, None] * i) * norm, DH, axis=0)
    ks = np.repeat(np.exp(-decay[:, None] * i) * D ** -0.5, DH, axis=0)
    cos1, sin1 = rows(np.cos(ang1)), rows(np.sin(ang1) * sign)
    p = np.arange(P)
    pick = np.zeros((P, 8, P))
    for j in range(8):
        pick[2 * j + 1, j, :] = 1.0
    behind = np.where(p[None, :] > p[:, None], MASKED, 0.0)
    return {
        "ident": np.eye(P, dtype=np.float32), "identb": np.eye(P).astype(bf16),
        "mask_ij": behind.astype(bf16), "mask_ji": behind.T.astype(bf16).copy(),
        "cos0": rows(np.cos(ang0)).astype(np.float32), "sin0": rows(np.sin(ang0) * sign).astype(np.float32),
        "tables1": np.stack([cos1 * qs, sin1 * qs, cos1 * ks, sin1 * ks], axis=1).astype(np.float32),
        "pick": pick.astype(np.float32),
        "same_head": (p[:, None] // DH == p[None, :] // DH).astype(np.float32),
        "causal": (p[None, :] >= p[:, None]).astype(np.float32),
        "before": (p[:, None] < p[None, :]).astype(bf16),
        "rank": (NE - np.arange(NE, dtype=np.float32))[None, :],
    }


def layouts(inp):
    t = {k: np.ascontiguousarray(np.asarray(v)) for k, v in inp.items()}
    swap = np.arange(D) ^ 1
    chunks = lambda w: np.ascontiguousarray(w.T.reshape(FC, P, -1).transpose(1, 0, 2))
    x = t["L0_attn_in_features"]
    wq, wk, wv = (t["L0_attn_W_" + n].T for n in "qkv")
    q1, k1, v1, g1 = (t["L1_attn_W" + n] for n in "qkvg")
    return {
        "x5": np.concatenate([x, x[:1]]),
        "w_proj0": np.stack([wq, wq[:, swap], wk, wk[:, swap], wv], axis=1),
        "w1T": t["L0_ffn_W1"].T, "w2T": chunks(t["L0_ffn_W2"]),
        "b1c": t["L0_ffn_b1"].reshape(FC, P).T, "b2": t["L0_ffn_b2"][None, :],
        "scale": t["L0_ffn_scale"].reshape(1, 1),
        "w_outT": t["L0_attn_W_o"].T,
        "w_proj1": np.stack([q1, q1[:, swap], k1, k1[:, swap]], axis=1), "w_vg1": np.stack([v1, g1], axis=1),
        "w_routerT": t["L1_ffn_router_w"].T, "b_router": t["L1_ffn_router_b"][None, :],
        "fc1T": t["L1_ffn_fc1_w"].transpose(0, 2, 1),
        "fc2T": t["L1_ffn_fc2_w"].transpose(0, 2, 1).reshape(NE, FC, P, D).transpose(0, 2, 1, 3),
        "fc1_b": t["L1_ffn_fc1_b"].reshape(NE, FC, P).transpose(0, 2, 1),
        "fc2_b": t["L1_ffn_fc2_b"], "ls": t["L1_ffn_layer_scale"],
    }


SCRATCH = {
    "q0": ([B + 1, H, ROWS, S], BF16), "k0": ([B + 1, H, ROWS, S], BF16), "v0": ([B + 1, P, NT * H * VW], F32),
    "u": ([B + 1, S, D], F32), "o0": ([B, H, 2 * DH, S], F32),
    "x1": ([B, S, D], F32), "xn1": ([B, S, D], F32), "v1": ([B + 1, S, D], F32), "g1": ([B, S, D], F32),
    "logits": ([B, P, NT * NE], F32), "inter": ([B, P, S], F32),
    "q1": ([B + 1, H, ROWS, S], BF16), "k1": ([B + 1, H, ROWS, S], BF16),
    "o1": ([B, H, DH, S], F32), "diag": ([B, QUADS, NT, 4 * P], F32), "sums": ([B, QUADS, P, 40], F32),
    "index": ([B, P, 2 * NT], I32), "weight": ([B, P, 2 * NT], F32),
    "slot_x": ([ALL_SLOTS, D], F32), "slot_y": ([ALL_SLOTS + P, D], F32),
}


def build(nc, arrays):
    A = {n: nc.dram_tensor(n, a.shape, mybir.dt.from_np(a.dtype), kind="ExternalInput").ap() for n, a in arrays.items()}
    for n, (shape, dt) in SCRATCH.items():
        A[n] = nc.dram_tensor(n, shape, dt).ap()
    A["out"] = nc.dram_tensor("out", (B, S, D), F32, kind="ExternalOutput").ap()
    A["x"], A["x_next"] = A["x5"][0:B], A["x5"][1:B + 1]
    for n in ("q0", "k0", "v0", "q1", "k1", "v1"):
        A[n + "_next"] = A[n][1:B + 1]
    program(nc, A)


def kernel(**inputs):
    import concourse.bacc as bacc
    from concourse.bass_utils import run_bass_kernel_spmd as run

    nc = bacc.Bacc("TRN2", target_bir_lowering=False, num_devices=1)
    arrays = {n: np.ascontiguousarray(a) for n, a in {**constants(), **layouts(inputs)}.items()}
    build(nc, arrays)
    r = run(nc, [arrays], core_ids=[0])
    return r.results[0]["out"]
```

```python
from contextlib import ExitStack

import numpy as np

import concourse.bass as bass
from concourse import mybir

F32 = mybir.dt.float32
BF16 = mybir.dt.bfloat16
I32 = mybir.dt.int32
ALU = mybir.AluOpType
ACT = mybir.ActivationFunctionType
AX = mybir.AxisListType

P = 128
B, S, D = 4, 1024, 128
H, DH = 16, 8
NT = S // P
NTILES = B * NT
HALF = 512
FF = 512
FC = FF // P
QUADS = H // 4
ROWS = 64
VW = 32
AUG = 48
ROWS0 = AUG + 2
Q_ROWS = {"hi": (0, 1, 2), "mid": (3, 4), "lo": (5,)}
K_ROWS = {"hi": (0, 3, 5), "mid": (1, 4), "lo": (2,)}
NE = 8
N = B * S
CAP = int(1.2 * (N // NE + 1))
SLOT_TILES = -(-CAP // P)
SLOTS = SLOT_TILES * P
ALL_SLOTS = NE * SLOTS
NO_SLOT = ALL_SLOTS
MASKED = -1.0e30
LN_EPS, RMS_EPS, TOP_EPS = 1e-5, 1e-6, 1e-9


def linker(engine, semaphore, base):
    count = [0]

    def link(ins):
        count[0] += 1
        ins.then_inc(semaphore, 1)
        engine.wait_ge(semaphore, base + count[0])

    return link, count


class Space:

    def __init__(self, nc):
        self.nc, self.stack = nc, ExitStack()

    def __enter__(self):
        self.stack.__enter__()
        return self

    def __exit__(self, *e):
        return self.stack.__exit__(*e)

    def sb(self, name, shape, dt=F32):
        return self.stack.enter_context(self.nc.sbuf_tensor(name, shape, dt))

    def psum(self, name):
        return self.stack.enter_context(self.nc.psum_tensor(name, [P, 8, HALF], F32))

    def sem(self, name):
        return self.stack.enter_context(self.nc.semaphore(name))


def one(ap, i):
    return ap[bass.ds(i, 1)]


def turn(it, i):
    return lambda per, n: (i * per + n if it is None else it * (2 * per) + i * per + n)


def split_rows(dst, it, rows):
    return [one(dst, it)[:, :, DH * r:DH * r + DH, :].rearrange("a h d s -> (a h) d s") for r in rows]


def project_and_ffn(nc, A):
    with Space(nc) as m:
        ps = m.psum("psA")
        ident = m.sb("identA", [P, P])
        cos, sin = m.sb("cosA", [P, S]), m.sb("sinA", [P, S])
        w_proj = m.sb("w_projA", [P, 5, P])
        w1 = m.sb("w1A", [P, FF])
        w2 = m.sb("w2A", [P, FC, P])
        b1 = m.sb("b1A", [P, FC])
        b2 = m.sb("b2A", [P, D])
        scale = m.sb("scaleA", [P, 1])
        pick = m.sb("pickA", [P, 8, P])
        eps, power = m.sb("epsA", [P, NT]), m.sb("powA", [P, NT])
        x = m.sb("xA", [P, NT, D])
        stat, mom = m.sb("statA", [P, NT, 6]), m.sb("momA", [P, NT, 2])
        held = m.sb("heldA", [P, 1])
        var, rstd = m.sb("varA", [P, NT]), m.sb("rstdA", [P, NT])
        xn = m.sb("xnA", [P, NT, D])
        xnT = m.sb("xnTA", [P, 2, S])
        terms = m.sb("termsA", [P, 2, 4, HALF])
        roped = m.sb("ropedA", [P, 2, S])
        rest = m.sb("restA", [P, 2, S])
        hi, mid, lo = (m.sb(n, [P, 2, 2, S], BF16) for n in ("hiA", "midA", "loA"))
        vaug = m.sb("vaugA", [P, 2, NT, H, VW])
        odd = m.sb("oddA", [P, 8])
        w1e = m.sb("w1eA", [P, FF])
        w2e = m.sb("w2eA", [P, FC, P])
        hT = m.sb("hTA", [P, FC, HALF])
        u = m.sb("uA", [P, 2, NT, D])
        aug = m.sb("augA", [B * H, 2, 2 * S], BF16)

        loaded, ready = m.sem("constA"), m.sem("initA")
        x_loaded, stats, moments = m.sem("x_loadedA"), m.sem("statsA"), m.sem("momentsA")
        var_ready, rstd_ready, xn_ready = m.sem("var_readyA"), m.sem("rstd_readyA"), m.sem("xn_readyA")
        turned, xnT_ready = m.sem("turnedA"), m.sem("xnT_readyA")
        projected, v_done, v_kept = m.sem("projectedA"), m.sem("v_doneA"), m.sem("v_keptA")
        outer_done, odd_ready, w_ready = m.sem("outer_doneA"), m.sem("odd_readyA"), m.sem("w_readyA")
        terms_ready, roped_ready = m.sem("terms_readyA"), m.sem("roped_readyA")
        hi_ready, rest_ready = m.sem("hi_readyA"), m.sem("rest_readyA")
        mid_ready, lo_ready = m.sem("mid_readyA"), m.sem("lo_readyA")
        h_done, gelu_done, u_done, u_ready = (m.sem(n) for n in ("h_doneA", "gelu_doneA", "u_doneA", "u_readyA"))
        stored, aug_stored = [m.sem(f"storedA{i}") for i in range(2)], m.sem("aug_storedA")
        STORES = 14
        consts = [(ident, A["ident"]), (cos, A["cos0"]), (sin, A["sin0"]), (w_proj, A["w_proj0"]), (w1, A["w1T"]),
                  (w2, A["w2T"]), (b1, A["b1c"]), (pick, A["pick"])]

        with nc.Block() as block:
            @block.sync
            def _(sp):
                def load(sel):
                    sp.dma_start(x[:, :, :], sel(A["x"]).rearrange("a (t p) c -> p (a t) c", p=P)).then_inc(x_loaded, 16)

                load(lambda a: a[0:1])
                for dst, src in consts:
                    sp.dma_start(dst[:], src).then_inc(loaded, 16)
                sp.dma_start(b2[:, :], A["b2"].broadcast_to((P, D))).then_inc(loaded, 16)
                sp.dma_start(scale[:, :], A["scale"].broadcast_to((P, 1))).then_inc(loaded, 16)
                sp.wait_ge(ready, 5)
                for i, n in enumerate(("q0", "k0")):
                    sp.dma_start(A[n].rearrange("b h r s -> (b h) r s")[:, AUG:ROWS0, :],
                                 aug[:, i, :].rearrange("p (r s) -> p r s", s=S)).then_inc(aug_stored, 16)
                sp.wait_ge(xn_ready, NT)
                load(lambda a: a[1:2])
                with sp.Fori(0, B // 2) as it:
                    ahead = [A["x"][bass.ds((it * 2 + i + 2) % B, 1)].rearrange("a (t p) c -> p (a t) c", p=P) for i in range(2)]
                    q_rows = [{k: split_rows(A["q0"], it * 2 + i, r) for k, r in Q_ROWS.items()} for i in range(2)]
                    k_rows = [{k: split_rows(A["k0"], it * 2 + i, r) for k, r in K_ROWS.items()} for i in range(2)]
                    ud = [A["u"][1:B + 1][bass.ds(it * 2 + i, 1)].rearrange("a (t p) c -> p (a t) c", p=P) for i in range(2)]
                    vd = [A["v0"][bass.ds(it * 2 + i, 1)].rearrange("a p f -> (a p) f") for i in range(2)]
                    count = [{n: sp.snap(turn(it, i)(per, extra)) for n, per, extra in (
                        ("xn", NT, 2 * NT), ("lo", 2, 2), ("u", 2, 3))} for i in range(2)]
                    for i in range(2):
                        sp.wait_ge(xn_ready, count[i]["xn"])
                        sp.dma_start(x[:, :, :], ahead[i]).then_inc(x_loaded, 16)
                        sp.wait_ge(lo_ready, count[i]["lo"])
                        for name, part in (("hi", hi), ("mid", mid), ("lo", lo)):
                            for j, rows in ((0, q_rows[i]), (1, k_rows[i])):
                                for dst in rows[name]:
                                    sp.dma_start(dst, part[:, i, j, :]).then_inc(stored[i], 16)
                        sp.wait_ge(u_ready, count[i]["u"])
                        sp.dma_start(ud[i], u[:, i]).then_inc(stored[i], 16)
                        sp.dma_start(vd[i], vaug[:, i].rearrange("p t h d -> p (t h d)")).then_inc(stored[i], 16)
                sp.wait_ge(x_loaded, 16 * (B + 2))
                sp.wait_ge(aug_stored, 32)
                for i in range(2):
                    sp.wait_ge(stored[i], 16 * STORES * (B // 2) + 1)

            @block.vector
            def _(dve):
                nc.vector.memset(eps[:, :], LN_EPS).then_inc(ready, 1)
                nc.vector.memset(power[:, :], -0.5).then_inc(ready, 1)
                for i in range(2):
                    nc.vector.memset(aug[:, i, :], float(i)).then_inc(ready, 1)
                    dve.sem_inc(stored[i], 1)
                dve.sem_inc(u_ready, 1)

                def statistics(at):
                    dve.wait_ge(x_loaded, at(16, 16))
                    for t in range(NT):
                        nc.vector.bn_stats(stat[:, t, :], x[:, t, :]).then_inc(stats, 1)
                    dve.wait_ge(stats, at(NT, NT))
                    nc.vector.memset(held[:, :], 0.0)
                    for t in range(NT):
                        nc.vector.bn_aggr(mom[:, t, :], stat[:, t, :]).then_inc(moments, 1)

                def normalise(at):
                    dve.wait_ge(rstd_ready, at(1, 1))
                    for t in range(NT):
                        nc.vector.tensor_scalar(xn[:, t, :], x[:, t, :], mom[:, t, 0:1], rstd[:, t:t + 1],
                                                ALU.subtract, ALU.mult).then_inc(xn_ready, 1)

                statistics(turn(None, 0))
                normalise(turn(None, 0))
                dve.wait_ge(loaded, 16 * (len(consts) + 2))
                with dve.Fori(0, B // 2) as it:
                    for i in range(2):
                        at, ahead = turn(it, i), turn(it, i + 1)

                        def rope(half):
                            c = slice(half * HALF, half * HALF + HALF)
                            dve.wait_ge(roped_ready, at(2, half + 1))
                            dve.wait_ge(projected, at(2, half + 1))
                            for j in range(4):
                                ins = nc.vector.tensor_tensor(terms[:, half, j, :], ps[:, 2 + j, :],
                                                              (cos if j % 2 == 0 else sin)[:, c], ALU.mult)
                            ins.then_inc(terms_ready, 1)

                        dve.wait_ge(xnT_ready, at(2, 1))
                        nc.vector.tensor_scalar(odd[:, :], xnT[:, i, 2:18:2], scale[:, 0:1], None,
                                                ALU.mult).then_inc(odd_ready, 1)
                        statistics(ahead)
                        rope(0)
                        dve.wait_ge(outer_done, at(1, 1))
                        dve.wait_ge(odd_ready, at(1, 1))
                        for j in range(4):
                            c = slice(j * P, j * P + P)
                            nc.vector.scalar_tensor_tensor(w1e[:, c], ps[:, 0, c], odd[:, j:j + 1], w1[:, c],
                                                           ALU.mult, ALU.add)
                        for j in range(4):
                            o = slice(j * 32, j * 32 + 32)
                            ins = nc.vector.scalar_tensor_tensor(
                                w2e[:, :, o], ps[:, 1, j * P:j * P + P].rearrange("p (r q) -> p q r", q=FC),
                                odd[:, 4 + j:5 + j], w2[:, :, o], ALU.mult, ALU.add)
                        ins.then_inc(w_ready, 1)
                        rope(1)
                        normalise(ahead)
                        dve.wait_ge(stored[i], it * (16 * STORES) + 1)
                        for half in range(2):
                            dve.wait_ge(u_done, at(2, half + 1))
                            nc.vector.tensor_tensor(
                                u[:, i, 4 * half:4 * half + 4, :], ps[:, 6 + half, :].rearrange("p (t c) -> p t c", c=D),
                                b2[:, None, :].broadcast_to((P, 4, D)), ALU.add).then_inc(u_ready, 1)

            @block.gpsimd
            def _(pool):
                nc.gpsimd.memset(vaug[:, :, :, :, :], 1.0).then_inc(ready, 1)
                pool.sem_inc(roped_ready, 2)

                def deviation(at):
                    pool.wait_ge(moments, at(NT, NT))
                    nc.gpsimd.tensor_tensor(var[:, :], mom[:, :, 1], eps[:, :], ALU.add).then_inc(var_ready, 1)
                    pool.wait_ge(var_ready, at(1, 1))
                    nc.gpsimd.tensor_tensor(rstd[:, :], var[:, :], power[:, :], ALU.pow).then_inc(rstd_ready, 1)

                pool.wait_ge(ready, 5)
                deviation(turn(None, 0))
                with pool.Fori(0, B // 2) as it:
                    for i in range(2):
                        at = turn(it, i)
                        deviation(turn(it, i + 1))
                        halves = [slice(half * HALF, half * HALF + HALF) for half in range(2)]
                        for half, c in enumerate(halves):
                            pool.wait_ge(terms_ready, at(2, half + 1))
                            for j in range(2):
                                ins = nc.gpsimd.tensor_tensor(roped[:, j, c], terms[:, half, 2 * j, :],
                                                              terms[:, half, 2 * j + 1, :], ALU.add)
                            ins.then_inc(roped_ready, 1)
                        for half, c in enumerate(halves):
                            pool.wait_ge(hi_ready, at(2, half + 1))
                            for j in range(2):
                                ins = nc.gpsimd.tensor_tensor(rest[:, j, c], roped[:, j, c], hi[:, i, j, c], ALU.subtract)
                            ins.then_inc(rest_ready, 1)
                        for half, c in enumerate(halves):
                            pool.wait_ge(mid_ready, at(2, half + 1))
                            for j in range(2):
                                ins = nc.gpsimd.tensor_tensor(lo[:, i, j, c], rest[:, j, c], mid[:, i, j, c], ALU.subtract)
                            ins.then_inc(lo_ready, 1)

            @block.scalar
            def _(act):
                def columns(at, i, half):
                    act.wait_ge(turned, at(2, half + 1))
                    nc.scalar.copy(xnT[:, i, half * HALF:half * HALF + HALF], ps[:, half, :]).then_inc(xnT_ready, 1)

                for half in range(2):
                    columns(turn(None, 0), 0, half)
                act.wait_ge(ready, 5)
                act.wait_ge(loaded, 16 * (len(consts) + 2))
                with act.Fori(0, B // 2) as it:
                    for i in range(2):
                        at, ahead = turn(it, i), turn(it, i + 1)

                        def first_part(half):
                            c = slice(half * HALF, half * HALF + HALF)
                            act.wait_ge(roped_ready, at(2, half + 3))
                            nc.scalar.copy(hi[:, i, :, c], roped[:, :, c]).then_inc(hi_ready, 1)

                        def second_part(half):
                            c = slice(half * HALF, half * HALF + HALF)
                            act.wait_ge(rest_ready, at(2, half + 1))
                            nc.scalar.copy(mid[:, i, :, c], rest[:, :, c]).then_inc(mid_ready, 1)

                        def gelu(half):
                            for c in range(FC):
                                act.wait_ge(h_done, at(2 * FC, half * FC + c + 1))
                                if half == 1 and c == 0:
                                    act.wait_ge(u_done, at(2, 1))
                                nc.scalar.activation(hT[:, c, :], ps[:, 2 + c, :], ACT.Gelu,
                                                     bias=b1[:, c:c + 1]).then_inc(gelu_done, 1)

                        act.wait_ge(stored[i], it * (16 * STORES) + 1)
                        for half in range(2):
                            act.wait_ge(v_done, at(2, half + 1))
                            nc.scalar.copy(
                                vaug[:, i, 4 * half:4 * half + 4, :, 0:DH].rearrange("p t h d -> p (t h) d"),
                                ps[:, 6 + half, :].rearrange("p (g d) -> p g d", d=DH)).then_inc(v_kept, 1)
                        first_part(0)
                        gelu(0)
                        first_part(1)
                        second_part(0)
                        for half in range(2):
                            columns(ahead, 1 - i, half)
                        second_part(1)
                        gelu(1)

            @block.tensor
            def _(pe):
                def transposes(at):
                    for t in range(NT):
                        pe.wait_ge(xn_ready, at(NT, t + 1))
                        ins = nc.tensor.transpose(ps[:, t // 4, (t % 4) * P:(t % 4) * P + P], xn[:, t, :], ident[:, :])
                        if t % 4 == 3:
                            ins.then_inc(turned, 1)

                pe.wait_ge(loaded, 16 * (len(consts) + 2))
                transposes(turn(None, 0))
                with pe.Fori(0, B // 2) as it:
                    for i in range(2):
                        at, ahead = turn(it, i), turn(it, i + 1)

                        def project(half):
                            for j in range(4):
                                ins = nc.tensor.matmul(ps[:, 2 + j, :], w_proj[:, j, :],
                                                       xnT[:, i, half * HALF:half * HALF + HALF], start=True, stop=True)
                            ins.then_inc(projected, 1)

                        def feed_forward(half):
                            for c in range(FC):
                                nc.tensor.matmul(ps[:, 2 + c, :], w1e[:, c * P:c * P + P],
                                                 xnT[:, i, half * HALF:half * HALF + HALF], start=True,
                                                 stop=True).then_inc(h_done, 1)
                            for t in range(4):
                                for c in range(FC):
                                    if t == 0:
                                        pe.wait_ge(gelu_done, at(2 * FC, half * FC + c + 1))
                                    ins = nc.tensor.matmul(ps[:, 6 + half, t * P:t * P + P], hT[:, c, t * P:t * P + P],
                                                           w2e[:, c, :], start=(c == 0), stop=(c == FC - 1))
                            ins.then_inc(u_done, 1)

                        pe.wait_ge(xnT_ready, at(2, 1))
                        project(0)
                        pe.wait_ge(xnT_ready, at(2, 2))
                        for j in range(8):
                            ins = nc.tensor.matmul(ps[:, j // 4, (j % 4) * P:(j % 4) * P + P], pick[:, j, :], xn[:, 0, :],
                                                   start=True, stop=True)
                        ins.then_inc(outer_done, 1)
                        pe.wait_ge(u_ready, at(2, 1))
                        for t in range(NT):
                            ins = nc.tensor.matmul(ps[:, 6 + t // 4, (t % 4) * P:(t % 4) * P + P],
                                                   xnT[:, i, t * P:t * P + P], w_proj[:, 4, :], start=True, stop=True)
                            if t % 4 == 3:
                                ins.then_inc(v_done, 1)
                        pe.wait_ge(terms_ready, at(2, 1))
                        project(1)
                        pe.wait_ge(terms_ready, at(2, 2))
                        pe.wait_ge(w_ready, at(1, 1))
                        pe.wait_ge(v_kept, at(2, 2))
                        feed_forward(0)
                        transposes(ahead)
                        feed_forward(1)


def attention(nc, A):
    SLOTS_B, ITEMS = 12, 48
    units = [(hq, t, c) for t in range(NT) for c in range(t // 4 + 1) for hq in range(4)]
    UNITS = len(units) + 1
    slots = [(c, jt) for c in range(2) for jt in range(4 * c + 4)]
    PER_BATCH = UNITS * QUADS
    AHEAD = 16
    FIRST = UNITS + AHEAD
    DELAY = 4
    TURN = len(units) - AHEAD + DELAY

    def unit_width(g):
        hq, t, c = units[g]
        return min(HALF, P * (t + 1) - HALF * c)

    def stream(s):
        first = [(s + 2, g) for g in range(AHEAD)]
        return [(s + 1, g) for g in range(AHEAD, len(units))] + first[:DELAY] + [(s + 1, None)] + first[DELAY:]

    def spread_units():
        cost = [64 + HALF * (c + 1) - max(HALF * c, P * jt) for c, jt in slots for _ in range(4)]
        work = [64 + (unit_width(g) if g is not None else HALF) for _, g in stream(0)]
        plan, done, spent, item = [], 0, 0.0, 0.0
        for n in range(ITEMS):
            item += cost[n]
            k = 0
            while done < UNITS and (n == ITEMS - 1 or (spent + work[done] / 2) / sum(work) <= item / sum(cost)):
                spent += work[done]
                done, k = done + 1, k + 1
            plan.append(k)
        return plan

    def bank_of(n):
        return (n % PER_BATCH) % 3

    def bank_before(n):
        return max(m for m in range(n - 5, n) if bank_of(m) == bank_of(n))

    with Space(nc) as m:
        ps = m.psum("psB")
        st = [ps[:, i, :] for i in range(3)]
        pv = [ps[:, 3 + c, :] for c in range(2)]
        mxb = [ps[:, 5 + i, :] for i in range(3)]
        ident, identb = m.sb("identB", [P, P]), m.sb("identbB", [P, P], BF16)
        mask_ij, mask_ji = m.sb("mask_ijB", [P, P], BF16), m.sb("mask_jiB", [P, P], BF16)
        zeros = m.sb("zerosB", [P, SLOTS])
        q, k = m.sb("qB", [P, QUADS, 2, S], BF16), m.sb("kB", [P, QUADS, 2, S], BF16)
        v = m.sb("vB", [P, QUADS, NT, 4 * VW])
        probs = m.sb("probsB", [P, 8, HALF])
        out = m.sb("outB", [P, 2, HALF])
        mx, mx2 = m.sb("mxB", [P, 2, 4, NT]), m.sb("mx2B", [P, 2, 4, NT // 2])
        neg = m.sb("negB", [32, 2, 2, P], BF16)

        loaded, cleared, slots_cleared = m.sem("constB"), m.sem("clearedB"), m.sem("slots_clearedB")
        in_loaded = [m.sem(f"in_loadedB{s}") for s in range(QUADS)]
        st_done, exp_done, pv_done = m.sem("st_doneB"), m.sem("exp_doneB"), m.sem("pv_doneB")
        out_kept, out_stored = m.sem("out_keptB"), [m.sem(f"out_storedB{c}") for c in range(2)]
        max_done, max_read, combined, neg_hi = (m.sem(n) for n in ("max_doneB", "max_readB", "combinedB", "neg_hiB"))
        neg_placed = [m.sem(f"neg_placedB{p}") for p in range(2)]
        LOADS, PLACED = 16 * 9, 16 * 4

        with nc.Block() as block:
            @block.sync
            def _(sp):
                for dst, src in ((ident, "ident"), (identb, "identb"), (mask_ij, "mask_ij"), (mask_ji, "mask_ji")):
                    sp.dma_start(dst[:, :], A[src]).then_inc(loaded, 16)

                def load(s, qd, kd, vd):
                    for h in range(4):
                        r = slice(ROWS * (h % 2), ROWS * (h % 2) + ROWS0)
                        sp.dma_start(q[r, s, h // 2, :], qd[:, 4 * s + h].rearrange("a r s -> (a r) s")).then_inc(in_loaded[s], 16)
                        sp.dma_start(k[r, s, h // 2, :], kd[:, 4 * s + h].rearrange("a r s -> (a r) s")).then_inc(in_loaded[s], 16)
                    sp.dma_start(v[:, s, :, :], vd.rearrange("a p (t f) -> (a p) t f", t=NT)[
                        :, :, s * 4 * VW:(s + 1) * 4 * VW]).then_inc(in_loaded[s], 16)

                def place(s, par):
                    for part in range(2):
                        for p in range(2):
                            sp.dma_start(q[AUG + part:AUG + part + ROWS + 1:ROWS, s, p, :],
                                         neg[2 * NT * p:2 * NT * p + 2 * NT, par, part, :]).then_inc(neg_placed[par], 16)

                sp.wait_ge(cleared, 3)
                for s in range(QUADS):
                    load(s, A["q0"][0:1], A["k0"][0:1], A["v0"][0:1])
                sp.wait_ge(max_read, len(units) + DELAY + 1)
                place(0, 0)
                for e in range(NE):
                    sp.dma_start(A["slot_x"][e * SLOTS:(e + 1) * SLOTS, :].rearrange("(t p) c -> p t c", p=P),
                                 zeros[:, :].rearrange("p (t c) -> p t c", c=D)).then_inc(slots_cleared, 16)
                sp.dma_start(A["slot_y"][NO_SLOT:NO_SLOT + P, :], zeros[:, 0:D]).then_inc(slots_cleared, 16)
                with sp.Fori(0, B) as it:
                    qd, kd, vd = (A[n][bass.ds((it + 1) % B, 1)] for n in ("q0", "k0", "v0"))
                    od = one(A["o0"], it)
                    kept = [sp.snap(it * 8 + 2 + e + 1) for e in range(8)]
                    used = [sp.snap(it * (SLOTS_B * QUADS) + 2 + SLOTS_B * (s + 1)) for s in range(QUADS)]
                    maxed = [sp.snap(it * PER_BATCH + FIRST + UNITS * s + TURN + 1) for s in range(QUADS)]

                    def store(s, c):
                        sp.wait_ge(out_kept, kept[2 * s + c])
                        for hq in range(4):
                            sp.dma_start(od[:, 4 * s + hq, :, c * HALF:(c + 1) * HALF].rearrange("a r s -> (a r) s"),
                                         out[VW * hq:VW * hq + 2 * DH, c, :]).then_inc(out_stored[c], 16)

                    for s in range(QUADS):
                        store(s, 0)
                        sp.wait_ge(max_read, maxed[s])
                        place((s + 1) % QUADS, (s + 1) % 2)
                        store(s, 1)
                        sp.wait_ge(pv_done, used[s])
                        load(s, qd, kd, vd)
                for s in range(QUADS):
                    sp.wait_ge(in_loaded[s], LOADS * (B + 1))
                for par in range(2):
                    sp.wait_ge(neg_placed[par], PLACED * (B * QUADS // 2 + 1 - par) + 1)
                for c in range(2):
                    sp.wait_ge(out_stored[c], 64 * B * QUADS + 1)
                sp.wait_ge(slots_cleared, 16 * (NE + 1))

            @block.vector
            def _(dve):
                nc.vector.memset(zeros[:, :], 0.0).then_inc(cleared, 1)
                nc.vector.memset(q[:, :, :, :], 0.0).then_inc(cleared, 1)
                dve.sem_inc(out_stored[0], 1)
                dve.sem_inc(out_stored[1], 1)
                dve.sem_inc(neg_placed[0], 1)
                dve.sem_inc(neg_placed[1], 1)

                def maximum(s, g, n, done, quads, placed):
                    par, bank = s % 2, mxb[bank_of(n)]
                    if g is None:
                        turned = bank[0:32, 0:P]
                        dve.wait_ge(neg_placed[par], placed * PLACED + 1)
                        dve.wait_ge(max_done, done + 1)
                        nc.vector.tensor_scalar(neg[:, par, 0, :], turned, -1.0, None, ALU.mult).then_inc(neg_hi, 1)
                        dve.wait_ge(neg_hi, quads + 1)
                        nc.vector.scalar_tensor_tensor(neg[:, par, 1, :], turned, -1.0, neg[:, par, 0, :], ALU.mult,
                                                       ALU.subtract).then_inc(max_read, 1)
                        return
                    hq, t, c = units[g]
                    dst = mx[:, par, hq, t:t + 1] if c == 0 else mx2[:, par, hq, t - 4:t - 3]
                    dve.wait_ge(max_done, done + 1)
                    nc.vector.tensor_reduce(dst, bank[:, 0:unit_width(g)], AX.X, ALU.max).then_inc(max_read, 1)
                    if g == len(units) - 1:
                        dve.wait_ge(max_read, done + 1)
                        nc.vector.tensor_tensor(mx[:, par, :, 4:8], mx[:, par, :, 4:8], mx2[:, par, :, :],
                                                ALU.max).then_inc(combined, 1)

                before = [(0, g) for g in range(AHEAD)] + stream(-1)
                for i, (s, g) in enumerate(before):
                    maximum(s, g, i - FIRST, i, 0, 0)
                with dve.Fori(0, B) as it:
                    for s in range(QUADS):
                        for i, (x, g) in enumerate(stream(s)):
                            n = UNITS * s + i
                            maximum(x, g, n, it * PER_BATCH + FIRST + n, it * QUADS + x, it * 2 + x // 2)

            @block.gpsimd
            def _(pool):
                nc.gpsimd.memset(k[:, :, :, :], 0.0).then_inc(cleared, 1)

            @block.scalar
            def _(act):
                act.sem_inc(pv_done, 2)
                act.sem_inc(out_kept, 2)
                with act.Fori(0, B) as it:
                    def keep(s, c):
                        last = SLOTS_B * s + (4 if c == 0 else SLOTS_B)
                        act.wait_ge(pv_done, it * (SLOTS_B * QUADS) + 2 + last)
                        act.wait_ge(out_stored[c], it * (64 * QUADS) + 64 * s + 1)
                        nc.scalar.copy(out[:, c, :], pv[c]).then_inc(out_kept, 1)

                    for s in range(QUADS):
                        for j, (c, jt) in enumerate(slots):
                            w = HALF * (c + 1) - max(HALF * c, P * jt)
                            act.wait_ge(pv_done, it * (SLOTS_B * QUADS) + SLOTS_B * s + j + 1)
                            for hq in range(4):
                                n = ITEMS * s + 4 * j + hq
                                act.wait_ge(st_done, it * (ITEMS * QUADS) + n + 1)
                                nc.scalar.activation(probs[:, n % 8, 0:w], st[n % 3][:, 0:w], ACT.Exp,
                                                     scale=DH ** -0.5).then_inc(exp_done, 1)
                            if j == 5:
                                keep(s, 0)
                            if j == 1 and s:
                                keep(s - 1, 1)
                    keep(QUADS - 1, 1)

            @block.tensor
            def _(pe):
                def unit(x, g, n, it):
                    bank, par, s = mxb[bank_of(n)], x % 2, x % QUADS
                    if it is not None:
                        pe.wait_ge(max_read, it * PER_BATCH + FIRST + bank_before(n) + 1)
                    elif FIRST + bank_before(n) >= 0:
                        pe.wait_ge(max_read, FIRST + bank_before(n) + 1)
                    if g is None:
                        pe.wait_ge(combined, it * QUADS + x + 1 if it is not None else x + 1)
                        nc.tensor.transpose(bank[0:32, 0:P], mx[:, par, :, :].rearrange("p h t -> p (h t)"),
                                            ident[:, :]).then_inc(max_done, 1)
                        return
                    if g == 0:
                        pe.wait_ge(in_loaded[s], it * LOADS + LOADS * (1 + x // QUADS) if it is not None else LOADS)
                    hq, t, c = units[g]
                    r = slice(ROWS * (hq % 2), ROWS * (hq % 2) + ROWS)
                    w = unit_width(g)
                    last = c == t // 4
                    ins = nc.tensor.matmul(bank[:, 0:w], q[r, s, hq // 2, t * P:t * P + P],
                                           k[r, s, hq // 2, HALF * c:HALF * c + w], start=True, stop=not last)
                    if last:
                        ins = nc.tensor.matmul(bank[:, w - P:w], identb[:, :], mask_ij[:, :], start=False, stop=True)
                    ins.then_inc(max_done, 1)

                plan = spread_units()
                pe.wait_ge(loaded, 64)
                for i, (x, g) in enumerate([(0, g) for g in range(AHEAD)] + stream(-1)):
                    unit(x, g, i - FIRST, None)
                with pe.Fori(0, B) as it:
                    def products(s, j):
                        c, jt = slots[j]
                        i0 = max(HALF * c, P * jt)
                        n = ITEMS * s + 4 * j
                        pe.wait_ge(exp_done, it * (ITEMS * QUADS) + n + 4)
                        if jt == 0:
                            pe.wait_ge(out_kept, it * 8 + 2 * s + c + 1)
                        for hq in range(4):
                            ins = nc.tensor.matmul(pv[c][VW * hq:VW * hq + VW, i0 - HALF * c:HALF],
                                                   v[:, s, jt, VW * hq:VW * hq + VW],
                                                   probs[:, (n + hq) % 8, 0:HALF * (c + 1) - i0],
                                                   start=(jt == 0), stop=(jt == 4 * c + 3), skip_group_check=True)
                        ins.then_inc(pv_done, 1)

                    before = None
                    for s in range(QUADS):
                        todo = list(enumerate(stream(s)))
                        pe.wait_ge(neg_placed[s % 2], it * (2 * PLACED) + PLACED * (s // 2 + 1) + 1)
                        for j, (c, jt) in enumerate(slots):
                            i0 = max(HALF * c, P * jt)
                            w = HALF * (c + 1) - i0
                            for hq in range(4):
                                n = ITEMS * s + 4 * j + hq
                                r = slice(ROWS * (hq % 2), ROWS * (hq % 2) + ROWS)
                                if n >= 3:
                                    pe.wait_ge(exp_done, it * (ITEMS * QUADS) + n - 2)
                                ins = nc.tensor.matmul(st[n % 3][:, 0:w], k[r, s, hq // 2, jt * P:jt * P + P],
                                                       q[r, s, hq // 2, i0:i0 + w], start=True, stop=(jt < 4 * c))
                                if jt >= 4 * c:
                                    ins = nc.tensor.matmul(st[n % 3][:, 0:P], identb[:, :], mask_ji[:, :],
                                                           start=False, stop=True)
                                ins.then_inc(st_done, 1)
                                for i, (x, g) in todo[:plan[4 * j + hq]]:
                                    unit(x, g, UNITS * s + i, it)
                                todo = todo[plan[4 * j + hq]:]
                            if before:
                                products(*before)
                            before = (s, j)
                    products(*before)


def between_layers(nc, A):
    with Space(nc) as m:
        ps = m.psum("psC")
        ident = m.sb("identC", [P, P])
        tables = m.sb("tablesC", [P, 4, S])
        w_out = m.sb("w_outC", [P, D])
        w_proj = m.sb("w_projC", [P, 4, P])
        w_vg = m.sb("w_vgC", [P, 2, P])
        w_router, b_router = m.sb("w_routerC", [P, NE]), m.sb("b_routerC", [P, NE])
        same_head = m.sb("same_headC", [P, P])
        eps, power = m.sb("epsC", [P, NT]), m.sb("powC", [P, NT])
        oT, den = m.sb("oTC", [P, S]), m.sb("denC", [P, S])
        x, u, gate = m.sb("xC", [P, NT, D]), m.sb("uC", [P, NT, D]), m.sb("gateC", [P, NT, D])
        rden, headT = m.sb("rdenC", [P, S]), m.sb("headTC", [P, S])
        x1 = m.sb("x1C", [P, NT, D])
        stat, mom = m.sb("statC", [P, NT, 6]), m.sb("momC", [P, NT, 2])
        held = m.sb("heldC", [P, 1])
        var, rstd = m.sb("varC", [P, NT]), m.sb("rstdC", [P, NT])
        xn, xnT = m.sb("xnC", [P, NT, D]), m.sb("xnTC", [P, S])
        terms = m.sb("termsC", [P, 2, 4, HALF])
        roped, rest = m.sb("ropedC", [P, 2, S]), m.sb("restC", [P, 2, S])
        hi, mid, lo = (m.sb(n, [P, 2, S], BF16) for n in ("hiC", "midC", "loC"))
        v, gate1 = m.sb("vC", [P, NT, D]), m.sb("gate1C", [P, NT, D])
        logits = m.sb("logitsC", [P, NT, NE])
        k_tok = m.sb("k_tokC", [P, NT, P])
        chunk_state = m.sb("chunk_stateC", [P, NT, P])
        state = m.sb("stateC", [P, NT, P])
        inter = m.sb("interC", [P, S])

        names = ("const init in_loaded u_loaded gated rden_ready head_ready s_done x1_half x1_ready stats moments var_ready "
                 "rstd_ready xn_ready turned xnT_ready projected vg_done v_kept g_kept router_done logits_ready terms_ready "
                 "roped_ready hi_ready rest_ready mid_ready lo_ready k_turned k_kept chunk_done chunk_ready state_ready "
                 "inter_done inter_kept stored").split()
        g = {n: m.sem(n + "C") for n in names}
        consts = [(ident, "ident"), (tables, "tables1"), (w_out, "w_outT"), (w_proj, "w_proj1"), (w_vg, "w_vg1"),
                  (w_router, "w_routerT"), (same_head, "same_head")]
        STORES = 12 + 6
        LOADS = 16 * 3

        with nc.Block() as block:
            @block.sync
            def _(sp):
                for dst, src in consts:
                    sp.dma_start(dst[:], A[src]).then_inc(g["const"], 16)
                sp.dma_start(b_router[:, :], A["b_router"].broadcast_to((P, NE))).then_inc(g["const"], 16)
                with sp.Fori(0, B) as it:
                    od = one(A["o0"], it).rearrange("a h r s -> (a h) r s")
                    xd = one(A["x"], it).rearrange("a (t p) c -> p (a t) c", p=P)
                    tok = {n: one(A[n][1:B + 1] if n == "u" else A[n], it).rearrange("a (t p) c -> p (a t) c", p=P)
                           for n in ("u", "x1", "xn1", "v1", "g1")}
                    ld = one(A["logits"], it).rearrange("a p f -> (a p) f")
                    nd = one(A["inter"], it).rearrange("a p s -> (a p) s")
                    q_rows = {n: split_rows(A["q1"], it, r) for n, r in Q_ROWS.items()}
                    k_rows = {n: split_rows(A["k1"], it, r) for n, r in K_ROWS.items()}
                    val = {n: sp.snap(it * c + c) for n, c in (("xn_ready", NT), ("v_kept", 2), ("g_kept", 2),
                                                                ("logits_ready", 1), ("lo_ready", 2), ("inter_kept", 2))}
                    free = sp.snap(it * 2 + 1)
                    sp.wait_ge(g["x1_ready"], free)
                    sp.dma_start(oT[:, :], od[:, 0:DH, :]).then_inc(g["in_loaded"], 16)
                    sp.dma_start(den[:, :], od[:, DH:2 * DH, :]).then_inc(g["in_loaded"], 16)
                    sp.dma_start(x[:, :, :], xd).then_inc(g["in_loaded"], 16)
                    sp.dma_start(u[:, :, :], tok["u"]).then_inc(g["u_loaded"], 16)
                    sp.wait_ge(g["xn_ready"], val["xn_ready"])
                    sp.dma_start(tok["x1"], x1[:, :, :]).then_inc(g["stored"], 16)
                    sp.dma_start(tok["xn1"], xn[:, :, :]).then_inc(g["stored"], 16)
                    sp.wait_ge(g["v_kept"], val["v_kept"])
                    sp.dma_start(tok["v1"], v[:, :, :]).then_inc(g["stored"], 16)
                    sp.wait_ge(g["g_kept"], val["g_kept"])
                    sp.dma_start(tok["g1"], gate1[:, :, :]).then_inc(g["stored"], 16)
                    sp.wait_ge(g["logits_ready"], val["logits_ready"])
                    sp.dma_start(ld, logits[:, :, :].rearrange("p t e -> p (t e)")).then_inc(g["stored"], 16)
                    sp.wait_ge(g["lo_ready"], val["lo_ready"])
                    for name, part in (("hi", hi), ("mid", mid), ("lo", lo)):
                        for i, rows in ((0, q_rows), (1, k_rows)):
                            for dst in rows[name]:
                                sp.dma_start(dst, part[:, i, :]).then_inc(g["stored"], 16)
                    sp.wait_ge(g["inter_kept"], val["inter_kept"])
                    sp.dma_start(nd, inter[:, :]).then_inc(g["stored"], 16)
                sp.wait_ge(g["stored"], 16 * STORES * B + 1)

            @block.vector
            def _(dve):
                nc.vector.memset(eps[:, :], LN_EPS).then_inc(g["init"], 1)
                nc.vector.memset(power[:, :], -0.5).then_inc(g["init"], 1)
                nc.vector.memset(state[:, 0, :], 0.0).then_inc(g["init"], 1)
                dve.sem_inc(g["stored"], 1)
                dve.sem_inc(g["x1_ready"], 1)
                dve.wait_ge(g["const"], 16 * (len(consts) + 1))
                with dve.Fori(0, B) as it:
                    def after(name, per, n):
                        dve.wait_ge(g[name], it * per + n)

                    after("in_loaded", LOADS, LOADS)
                    nc.vector.reciprocal(rden[:, :], den[:, :]).then_inc(g["rden_ready"], 1)
                    after("rden_ready", 1, 1)
                    for half in range(2):
                        c = slice(half * HALF, half * HALF + HALF)
                        nc.vector.tensor_tensor(headT[:, c], oT[:, c], rden[:, c], ALU.mult).then_inc(g["head_ready"], 1)
                    after("gated", 1, 1)
                    after("stored", 16 * STORES, 1)
                    for half in range(2):
                        t4 = slice(4 * half, 4 * half + 4)
                        after("s_done", 2, half + 1)
                        nc.vector.tensor_tensor(x1[:, t4, :], ps[:, half, :].rearrange("p (t c) -> p t c", c=D),
                                                gate[:, t4, :], ALU.mult).then_inc(g["x1_half"], 1)
                    for half in range(2):
                        t4 = slice(4 * half, 4 * half + 4)
                        after("x1_half", 2, half + 1)
                        nc.vector.tensor_tensor(x1[:, t4, :], x1[:, t4, :], x[:, t4, :], ALU.add).then_inc(g["x1_ready"], 1)
                    for t in range(NT):
                        if t % 4 == 0:
                            after("x1_ready", 2, t // 4 + 2)
                        nc.vector.bn_stats(stat[:, t, :], x1[:, t, :]).then_inc(g["stats"], 1)
                    after("stats", NT, NT)
                    nc.vector.memset(held[:, :], 0.0)
                    for t in range(NT):
                        nc.vector.bn_aggr(mom[:, t, :], stat[:, t, :]).then_inc(g["moments"], 1)
                    after("rstd_ready", 1, 1)
                    for t in range(NT):
                        nc.vector.tensor_scalar(xn[:, t, :], x1[:, t, :], mom[:, t, 0:1], rstd[:, t:t + 1],
                                                ALU.subtract, ALU.mult).then_inc(g["xn_ready"], 1)
                    for half in range(2):
                        c = slice(half * HALF, half * HALF + HALF)
                        after("projected", 2, half + 1)
                        for j in range(4):
                            ins = nc.vector.tensor_tensor(terms[:, half, j, :], ps[:, 2 + j, :], tables[:, j, c], ALU.mult)
                        ins.then_inc(g["terms_ready"], 1)
                    after("router_done", 1, 1)
                    nc.vector.tensor_tensor(logits[:, :, :], ps[:, 0, 0:NT * NE].rearrange("p (t e) -> p t e", e=NE),
                                            b_router[:, None, :].broadcast_to((P, NT, NE)),
                                            ALU.add).then_inc(g["logits_ready"], 1)
                    for half in range(2):
                        after("chunk_done", 2, half + 1)
                        nc.vector.tensor_tensor(chunk_state[:, 4 * half:4 * half + 4, :],
                                                ps[:, 6 + half, :].rearrange("p (t c) -> p t c", c=P),
                                                same_head[:, None, :].broadcast_to((P, 4, P)),
                                                ALU.mult).then_inc(g["chunk_ready"], 1)
                    after("chunk_ready", 2, 2)
                    for t in range(1, NT):
                        if t > 1:
                            after("state_ready", NT - 1, t - 1)
                        nc.vector.tensor_tensor(state[:, t, :], state[:, t - 1, :], chunk_state[:, t - 1, :],
                                                ALU.add).then_inc(g["state_ready"], 1)

            @block.gpsimd
            def _(pool):
                pool.wait_ge(g["init"], 3)
                with pool.Fori(0, B) as it:
                    pool.wait_ge(g["moments"], it * NT + NT)
                    nc.gpsimd.tensor_tensor(var[:, :], mom[:, :, 1], eps[:, :], ALU.add).then_inc(g["var_ready"], 1)
                    pool.wait_ge(g["var_ready"], it + 1)
                    nc.gpsimd.tensor_tensor(rstd[:, :], var[:, :], power[:, :], ALU.pow).then_inc(g["rstd_ready"], 1)
                    for half in range(2):
                        c = slice(half * HALF, half * HALF + HALF)
                        pool.wait_ge(g["terms_ready"], it * 2 + half + 1)
                        for i in range(2):
                            ins = nc.gpsimd.tensor_tensor(roped[:, i, c], terms[:, half, 2 * i, :],
                                                          terms[:, half, 2 * i + 1, :], ALU.add)
                        ins.then_inc(g["roped_ready"], 1)
                        pool.wait_ge(g["hi_ready"], it * 2 + half + 1)
                        for i in range(2):
                            ins = nc.gpsimd.tensor_tensor(rest[:, i, c], roped[:, i, c], hi[:, i, c], ALU.subtract)
                        ins.then_inc(g["rest_ready"], 1)
                        pool.wait_ge(g["mid_ready"], it * 2 + half + 1)
                        for i in range(2):
                            ins = nc.gpsimd.tensor_tensor(lo[:, i, c], rest[:, i, c], mid[:, i, c], ALU.subtract)
                        ins.then_inc(g["lo_ready"], 1)

            @block.scalar
            def _(act):
                act.wait_ge(g["init"], 3)
                with act.Fori(0, B) as it:
                    act.wait_ge(g["u_loaded"], it * 16 + 16)
                    nc.scalar.activation(gate[:, :, :], u[:, :, :], ACT.Silu).then_inc(g["gated"], 1)
                    for half in range(2):
                        act.wait_ge(g["turned"], it * 2 + half + 1)
                        nc.scalar.copy(xnT[:, half * HALF:half * HALF + HALF], ps[:, half, :]).then_inc(g["xnT_ready"], 1)
                    act.wait_ge(g["stored"], it * (16 * STORES) + 1)
                    for half in range(2):
                        t4 = slice(4 * half, 4 * half + 4)
                        act.wait_ge(g["vg_done"], it * 4 + half + 1)
                        nc.scalar.copy(v[:, t4, :], ps[:, 6 + half, :].rearrange("p (t c) -> p t c", c=D)
                                       ).then_inc(g["v_kept"], 1)
                    for half in range(2):
                        t4 = slice(4 * half, 4 * half + 4)
                        act.wait_ge(g["vg_done"], it * 4 + half + 3)
                        nc.scalar.activation(gate1[:, t4, :], ps[:, 6 + half, :].rearrange("p (t c) -> p t c", c=D),
                                             ACT.Silu).then_inc(g["g_kept"], 1)
                    for half in range(2):
                        c = slice(half * HALF, half * HALF + HALF)
                        act.wait_ge(g["roped_ready"], it * 2 + half + 1)
                        nc.scalar.copy(hi[:, :, c], roped[:, :, c]).then_inc(g["hi_ready"], 1)
                        act.wait_ge(g["rest_ready"], it * 2 + half + 1)
                        nc.scalar.copy(mid[:, :, c], rest[:, :, c]).then_inc(g["mid_ready"], 1)
                    for half in range(2):
                        act.wait_ge(g["k_turned"], it * 2 + half + 1)
                        nc.scalar.copy(k_tok[:, 4 * half:4 * half + 4, :],
                                       ps[:, 2 + half, :].rearrange("p (t c) -> p t c", c=P)).then_inc(g["k_kept"], 1)
                    for half in range(2):
                        act.wait_ge(g["inter_done"], it * 2 + half + 1)
                        nc.scalar.copy(inter[:, half * HALF:half * HALF + HALF], ps[:, 4 + half, :]
                                       ).then_inc(g["inter_kept"], 1)

            @block.tensor
            def _(pe):
                pe.wait_ge(g["const"], 16 * (len(consts) + 1))
                pe.wait_ge(g["init"], 3)
                with pe.Fori(0, B) as it:
                    def after(name, per, n):
                        pe.wait_ge(g[name], it * per + n)

                    for t in range(NT):
                        if t % 4 == 0:
                            after("head_ready", 2, t // 4 + 1)
                        ins = nc.tensor.matmul(ps[:, t // 4, (t % 4) * P:(t % 4) * P + P], headT[:, t * P:t * P + P],
                                               w_out[:, :], start=True, stop=True)
                        if t % 4 == 3:
                            ins.then_inc(g["s_done"], 1)
                    for t in range(NT):
                        after("xn_ready", NT, t + 1)
                        ins = nc.tensor.transpose(ps[:, t // 4, (t % 4) * P:(t % 4) * P + P], xn[:, t, :], ident[:, :])
                        if t % 4 == 3:
                            ins.then_inc(g["turned"], 1)

                    def project(half):
                        for j in range(4):
                            ins = nc.tensor.matmul(ps[:, 2 + j, :], w_proj[:, j, :],
                                                   xnT[:, half * HALF:half * HALF + HALF], start=True, stop=True)
                        ins.then_inc(g["projected"], 1)

                    def by_token(i):
                        for t in range(NT):
                            if i == 1 and t % 4 == 0:
                                after("v_kept", 2, t // 4 + 1)
                            ins = nc.tensor.matmul(ps[:, 6 + t // 4, (t % 4) * P:(t % 4) * P + P], xnT[:, t * P:t * P + P],
                                                   w_vg[:, i, :], start=True, stop=True)
                            if t % 4 == 3:
                                ins.then_inc(g["vg_done"], 1)

                    after("xnT_ready", 2, 1)
                    project(0)
                    after("xnT_ready", 2, 2)
                    by_token(0)
                    after("terms_ready", 2, 1)
                    project(1)
                    for t in range(NT):
                        ins = nc.tensor.matmul(ps[:, 0, t * NE:t * NE + NE], xnT[:, t * P:t * P + P], w_router[:, :],
                                               start=True, stop=True)
                    ins.then_inc(g["router_done"], 1)
                    by_token(1)
                    after("terms_ready", 2, 2)
                    for t in range(NT):
                        if t % 4 == 0:
                            after("roped_ready", 2, t // 4 + 1)
                        ins = nc.tensor.transpose(ps[:, 2 + t // 4, (t % 4) * P:(t % 4) * P + P],
                                                  roped[:, 1, t * P:t * P + P], ident[:, :])
                        if t % 4 == 3:
                            ins.then_inc(g["k_turned"], 1)
                    for t in range(NT):
                        if t % 4 == 0:
                            after("k_kept", 2, t // 4 + 1)
                            after("g_kept", 2, t // 4 + 1)
                        ins = nc.tensor.matmul(ps[:, 6 + t // 4, (t % 4) * P:(t % 4) * P + P], k_tok[:, t, :], v[:, t, :],
                                               start=True, stop=True)
                        if t % 4 == 3:
                            ins.then_inc(g["chunk_done"], 1)
                    for t in range(NT):
                        if t:
                            after("state_ready", NT - 1, t)
                        ins = nc.tensor.matmul(ps[:, 4 + t // 4, (t % 4) * P:(t % 4) * P + P], state[:, t, :],
                                               roped[:, 0, t * P:t * P + P], start=True, stop=True)
                        if t % 4 == 3:
                            ins.then_inc(g["inter_done"], 1)


def route(nc, A):
    TK = 2 * NTILES
    with Space(nc) as m:
        ps = m.psum("psR")
        before, ones_b = m.sb("beforeR", [P, P], BF16), m.sb("onesR", [P, P], BF16)
        rank = m.sb("rankR", [P, NE])
        ones = m.sb("ones_scanR", [P, TK])
        L = m.sb("logitsR", [P, NTILES, NE])
        top, z, e = m.sb("topR", [P, NTILES]), m.sb("zR", [P, NTILES, NE]), m.sb("eR", [P, NTILES, NE])
        total, inv = m.sb("totalR", [P, NTILES]), m.sb("invR", [P, NTILES])
        p = [m.sb(f"pR{i}", [P, NTILES, NE]) for i in range(2)]
        best = m.sb("bestR", [P, 2, NTILES])
        at = m.sb("atR", [P, 2, NTILES, NE])
        first = m.sb("firstR", [P, 2, NTILES])
        chosen = m.sb("chosenR", [P, 2, NTILES, NE])
        both, winv = m.sb("bothR", [P, NTILES]), m.sb("winvR", [P, NTILES])
        w, valid = m.sb("wR", [P, 2, NTILES]), m.sb("validR", [P, 2, NTILES])
        hot, hot_b = m.sb("hotR", [P, 2, NTILES, NE]), m.sb("hot_bR", [P, 2, NTILES, NE], BF16)
        upto = m.sb("uptoR", [P, TK, NE])
        pos = m.sb("posR", [P, TK, NE])
        own = m.sb("ownR", [P, TK])
        keep = m.sb("keepR", [P, TK])
        slot = m.sb("slotR", [P, TK])
        index = m.sb("indexR", [P, 2, NTILES], I32)
        weight = m.sb("weightR", [P, 2, NTILES])

        loaded, step, shifted, exped = m.sem("constR"), m.sem("stepR"), m.sem("shiftedR"), m.sem("expedR")
        hot_ready, counted, routed, stored = m.sem("hot_readyR"), m.sem("countedR"), m.sem("routedR"), m.sem("storedR")

        def spread(ap, n=NE):
            return ap[:, :, None].broadcast_to((P, ap.shape[1], n))

        def flat(ap):
            return ap[:, :, :, :].rearrange("p k t e -> p (k t) e")

        with nc.Block() as block:
            @block.sync
            def _(sp):
                for dst, src in ((before, A["before"]), (rank, A["rank"].broadcast_to((P, NE)))):
                    sp.dma_start(dst[:, :], src).then_inc(loaded, 16)
                sp.dma_start(L[:, :, :].rearrange("p (b t) e -> p b (t e)", b=B),
                             A["logits"].rearrange("b p f -> p b f")).then_inc(loaded, 16)
                sp.wait_ge(routed, 2)
                n = 0
                for b in range(B):
                    for kk in range(2):
                        sp.dma_start(A["index"][b, :, kk * NT:kk * NT + NT], index[:, kk, b * NT:b * NT + NT]).then_inc(stored, 16)
                        sp.dma_start(A["weight"][b, :, kk * NT:kk * NT + NT], weight[:, kk, b * NT:b * NT + NT]).then_inc(stored, 16)
                        n += 2
                sp.wait_ge(stored, 16 * n)

            @block.scalar
            def _(act):
                act.wait_ge(shifted, 1)
                nc.scalar.activation(e[:, :, :], z[:, :, :], ACT.Exp).then_inc(exped, 1)

            @block.tensor
            def _(pe):
                pe.wait_ge(loaded, 48)
                pe.wait_ge(hot_ready, 1)
                rhs = hot_b[:, :, :, :].rearrange("p k t e -> p (k t e)")
                nc.tensor.matmul(ps[:, 0, :], before[:, :], rhs, start=True, stop=True)
                nc.tensor.matmul(ps[:, 1, :], ones_b[:, :], rhs, start=True, stop=True).then_inc(counted, 1)

            @block.vector
            def _(dve):
                V = nc.vector
                link, _ = linker(dve, step, 0)
                link(V.memset(ones[:, :], 1.0))
                link(V.memset(ones_b[:, :], 1.0))
                dve.wait_ge(loaded, 48)
                link(V.tensor_reduce(top[:, :], L[:, :, :], AX.X, ALU.max))
                V.tensor_tensor(z[:, :, :], L[:, :, :], spread(top), ALU.subtract).then_inc(shifted, 1)
                dve.wait_ge(exped, 1)
                link(V.tensor_reduce(total[:, :], e[:, :, :], AX.X, ALU.add))
                link(V.reciprocal(inv[:, :], total[:, :]))
                link(V.tensor_tensor(p[0][:, :, :], e[:, :, :], spread(inv), ALU.mult))
                ranks = rank[:, None, :].broadcast_to((P, NTILES, NE))
                for kk in range(2):
                    link(V.tensor_reduce(best[:, kk, :], p[kk][:, :, :], AX.X, ALU.max))
                    link(V.tensor_tensor(at[:, kk], p[kk][:, :, :], spread(best[:, kk, :]), ALU.is_equal))
                    link(V.tensor_tensor(at[:, kk], at[:, kk], ranks, ALU.mult))
                    link(V.tensor_reduce(first[:, kk, :], at[:, kk], AX.X, ALU.max))
                    link(V.tensor_tensor(chosen[:, kk], at[:, kk], spread(first[:, kk, :]), ALU.is_equal))
                    if kk == 0:
                        link(V.scalar_tensor_tensor(p[1][:, :, :], chosen[:, 0], -2.0, p[0][:, :, :], ALU.mult, ALU.add))
                link(V.tensor_tensor(both[:, :], best[:, 0, :], best[:, 1, :], ALU.add))
                link(V.tensor_scalar(both[:, :], both[:, :], TOP_EPS, None, ALU.add))
                link(V.reciprocal(winv[:, :], both[:, :]))
                link(V.tensor_tensor(w[:, :, :], best[:, :, :], winv[:, None, :].broadcast_to((P, 2, NTILES)), ALU.mult))
                link(V.tensor_scalar(valid[:, :, :], w[:, :, :], TOP_EPS, None, ALU.is_gt))
                link(V.tensor_tensor(flat(hot), flat(chosen), spread(valid[:, :, :].rearrange("p k t -> p (k t)")), ALU.mult))
                V.tensor_copy(flat(hot_b), flat(hot)).then_inc(hot_ready, 1)
                dve.wait_ge(counted, 1)
                inside = ps[:, 0, :].rearrange("p (g e) -> p g e", e=NE)
                tile_n = ps[:, 1, :].rearrange("p (g e) -> p g e", e=NE)
                for x in range(NE):
                    ins = V.tensor_tensor_scan(upto[:, :, x], ones[:, :], tile_n[:, :, x], 0.0, ALU.mult, ALU.add)
                link(ins)
                link(V.tensor_tensor(pos[:, :, :], upto[:, :, :], tile_n, ALU.subtract))
                link(V.tensor_tensor(pos[:, :, :], pos[:, :, :], inside, ALU.add))
                link(V.tensor_tensor(pos[:, :, :], pos[:, :, :], flat(hot), ALU.mult))
                link(V.tensor_reduce(own[:, :], pos[:, :, :], AX.X, ALU.add))
                flat2 = [a[:, :, :].rearrange("p k t -> p (k t)") for a in (valid, first, w, weight, index)]
                link(V.scalar_tensor_tensor(keep[:, :], own[:, :], float(CAP), flat2[0], ALU.is_lt, ALU.mult))
                link(V.scalar_tensor_tensor(slot[:, :], flat2[1], -float(SLOTS), own[:, :], ALU.mult, ALU.add))
                link(V.tensor_scalar(slot[:, :], slot[:, :], float(NE * SLOTS - NO_SLOT), None, ALU.add))
                link(V.tensor_tensor(slot[:, :], slot[:, :], keep[:, :], ALU.mult))
                V.tensor_scalar(flat2[4], slot[:, :], float(NO_SLOT), None, ALU.add).then_inc(routed, 1)
                V.tensor_tensor(flat2[3], flat2[2], keep[:, :], ALU.mult).then_inc(routed, 1)


def retention(nc, A):
    units = [(hq, t, c) for t in range(1, NT) for c in range((t + 3) // 4) for hq in range(4)]
    PER_TILE = len(units) // NT
    MINE = len(units) // 2
    DEEP, DEEP_ABS = 4, 8
    LAG = 2
    VCOLS = 4 * DH + VW - DH
    with Space(nc) as m:
        ps = m.psum("psD")
        rows = {"act": [ps[:, 0, :], ps[:, 1, :]], "dve": [ps[:, 2, :], ps[:, 3, :]]}
        pt = [ps[:, 4:6, 2 * P * i:2 * P * i + 2 * P].rearrange("p b (a i) -> p a b i", a=2) for i in range(2)]
        po, pd = ps[:, 6, :], ps[:, 7, :]
        causal = m.sb("causalD", [P, P])
        ones = m.sb("onesD", [P, VW])
        q, k = m.sb("qD", [P, QUADS, 2, S], BF16), m.sb("kD", [P, QUADS, 2, S], BF16)
        v = m.sb("vD", [P, QUADS, NT, VCOLS])
        kept, absd = m.sb("keptD", [P, DEEP, 4 * P]), m.sb("absD", [P, DEEP_ABS, 4 * P])
        sums = m.sb("sumsD", [P, QUADS, len(units)])
        out, diag = m.sb("outD", [P, 2, HALF]), m.sb("diagD", [P, 2, HALF])

        x, index = m.sb("xD", [P, NT, D]), m.sb("indexD", [P, 2 * NT], I32)

        loaded, init = m.sem("constD"), m.sem("initD")
        x_loaded, scatter_step, scattered = m.sem("x_loadedD"), m.sem("scatter_stepD"), m.sem("scatteredD")
        in_loaded = [m.sem(f"in_loadedD{s}") for s in range(QUADS)]
        pt_done, masked, abs_done, pv_done = (m.sem(n) for n in ("pt_doneD", "maskedD", "abs_doneD", "pv_doneD"))
        out_kept, out_stored = m.sem("out_keptD"), [m.sem(f"out_storedD{p}") for p in range(2)]
        sums_stored = [m.sem(f"sums_storedD{s}") for s in range(QUADS)]
        unit_done = {e: m.sem("unit_doneD_" + e) for e in ("act", "dve")}
        unit_read = {e: m.sem("unit_readD_" + e) for e in ("act", "dve")}
        LOADS = 16 * 9

        def sum_unit(eng, name, it, s, g):
            i = g // 2
            eng.wait_ge(unit_done[name], it * (MINE * QUADS) + MINE * s + i + 1)
            hq, t, c = units[g]
            w = min(HALF, P * t - HALF * c)
            col = MINE * (g % 2) + i
            return rows[name][i % 2][:, 0:w], sums[:, s, col:col + 1]

        with nc.Block() as block:
            @block.sync
            def _(sp):
                sp.dma_start(causal[:, :], A["causal"]).then_inc(loaded, 16)
                sp.wait_ge(init, 4)

                def load(s, qd, kd, vd):
                    for h in range(4):
                        r = slice(ROWS * (h % 2), ROWS * (h % 2) + AUG)
                        sp.dma_start(q[r, s, h // 2, :], qd[:, 4 * s + h].rearrange("a r s -> (a r) s")).then_inc(in_loaded[s], 16)
                        sp.dma_start(k[r, s, h // 2, :], kd[:, 4 * s + h].rearrange("a r s -> (a r) s")).then_inc(in_loaded[s], 16)
                    n = min(VCOLS, D - 4 * DH * s)
                    sp.dma_start(v[:, s, :, 0:n], vd.rearrange("a (t p) c -> p (a t) c", p=P)[
                        :, :, 4 * DH * s:4 * DH * s + n]).then_inc(in_loaded[s], 16)

                for s in range(QUADS):
                    load(s, A["q1"][0:1], A["k1"][0:1], A["v1"][0:1])
                with sp.Fori(0, B) as it:
                    qd, kd, vd = (A[n][bass.ds((it + 1) % B, 1)] for n in ("q1", "k1", "v1"))
                    od, dd, sd = one(A["o1"], it), one(A["diag"], it), one(A["sums"], it)
                    kept_at = [sp.snap(it * 8 + 1 + e + 1) for e in range(8)]
                    units_read = [sp.snap(it * (MINE * QUADS) + MINE * (s + 1)) for s in range(QUADS)]
                    for s in range(QUADS):
                        for c in range(2):
                            sp.wait_ge(out_kept, kept_at[2 * s + c])
                            for hq in range(4):
                                sp.dma_start(od[:, 4 * s + hq, :, c * HALF:(c + 1) * HALF].rearrange("a r s -> (a r) s"),
                                             out[VW * hq:VW * hq + DH, c, :]).then_inc(out_stored[c], 16)
                            sp.dma_start(dd[:, s, 4 * c:4 * c + 4, :].rearrange("a t f -> (a t) f"),
                                         diag[0:P:VW, c, :]).then_inc(out_stored[c], 16)
                        for i, name in enumerate(("act", "dve")):
                            c = slice(MINE * i, MINE * i + MINE)
                            sp.wait_ge(unit_read[name], units_read[s])
                            sp.dma_start(sd[:, s, :, c].rearrange("a p u -> (a p) u"), sums[:, s, c]
                                         ).then_inc(sums_stored[s], 16)
                        load(s, qd, kd, vd)
                for s in range(QUADS):
                    sp.wait_ge(in_loaded[s], LOADS * (B + 1))
                    sp.wait_ge(sums_stored[s], 32 * B + 1)
                for c in range(2):
                    sp.wait_ge(out_stored[c], 80 * B * QUADS + 1)

            @block.vector
            def _(dve):
                nc.vector.memset(v[:, :, :, :], 0.0).then_inc(init, 1)
                nc.vector.memset(ones[:, :], 1.0).then_inc(init, 1)
                nc.vector.memset(q[:, :, :, :], 0.0).then_inc(init, 1)
                for c in range(2):
                    dve.sem_inc(out_stored[c], 1)
                for s in range(QUADS):
                    dve.sem_inc(sums_stored[s], 1)
                dve.wait_ge(loaded, 16)
                with dve.Fori(0, B) as it:
                    for s in range(QUADS):
                        for t in range(NT):
                            n = NT * s + t
                            dve.wait_ge(pt_done, it * (NT * QUADS) + n + 1)
                            dve.wait_ge(pv_done, it * (NT * QUADS) + n + 1)
                            nc.vector.tensor_tensor(kept[:, t % DEEP, :].rearrange("p (a b i) -> p a b i", a=2, b=2), pt[t % 2],
                                                    causal[:, None, None, :].broadcast_to((P, 2, 2, P)), ALU.mult).then_inc(masked, 1)
                            if t == 0:
                                dve.wait_ge(sums_stored[s], it * 32 + 1)
                            for g in range(PER_TILE * t, PER_TILE * t + PER_TILE):
                                if g % 2 == 1:
                                    src, dst = sum_unit(dve, "dve", it, s, g)
                                    nc.vector.tensor_reduce(dst, src, AX.X, ALU.add,
                                                            apply_absolute_value=True).then_inc(unit_read["dve"], 1)

            @block.gpsimd
            def _(pool):
                nc.gpsimd.memset(k[:, :, :, :], 0.0).then_inc(init, 1)
                with pool.Fori(0, B) as it:
                    xd = one(A["xn1"], it).rearrange("a (t p) c -> p (a t) c", p=P)
                    pool.dma_start(x[:, :, :], xd).then_inc(x_loaded, 16)
                    pool.dma_start(index[:, :], one(A["index"], it).rearrange("a p k -> (a p) k")).then_inc(x_loaded, 16)
                    all_rows = pool.snap(it * (16 * 2 * NT) + 16 * 2 * NT)
                    pool.wait_ge(x_loaded, it * 32 + 32)
                    pool.sem_inc(scatter_step, 1)
                    for kk in range(2):
                        for t in range(NT):
                            pool.indirect_dma_start(
                                A["slot_x"], bass.IndirectOffsetOnAxis(ap=index[:, kk * NT + t:kk * NT + t + 1], axis=0),
                                x[:, t, :], None, bounds_check=ALL_SLOTS - 1, oob_is_err=False).then_inc(scattered, 16)
                    pool.wait_ge(scattered, all_rows)
                    pool.sem_inc(scatter_step, 1)

            @block.scalar
            def _(act):
                act.sem_inc(pv_done, DEEP)
                act.sem_inc(out_kept, 1)
                with act.Fori(0, B) as it:
                    def keep(e):
                        act.wait_ge(pv_done, it * (NT * QUADS) + 4 * (e + 1) + DEEP)
                        act.wait_ge(out_stored[e % 2], it * (80 * QUADS) + 80 * (e // 2) + 1)
                        nc.scalar.copy(out[:, e % 2, :], po)
                        nc.scalar.copy(diag[:, e % 2, :], pd).then_inc(out_kept, 1)

                    for s in range(QUADS):
                        for t in range(NT):
                            n = NT * s + t
                            if t == 0:
                                act.wait_ge(sums_stored[s], it * 32 + 1)
                            for g in range(PER_TILE * t, PER_TILE * t + PER_TILE):
                                if g % 2 == 0:
                                    src, dst = sum_unit(act, "act", it, s, g)
                                    nc.scalar.activation(src, src, ACT.Abs, accum_out=dst).then_inc(unit_read["act"], 1)
                            act.wait_ge(masked, it * (NT * QUADS) + n + 1)
                            nc.scalar.activation(absd[:, t % DEEP_ABS, :], kept[:, t % DEEP, :], ACT.Abs).then_inc(abs_done, 1)
                            if t % 4 == 1 and n > 1:
                                keep(n // 4 - 1)
                    keep(2 * QUADS - 1)

            @block.tensor
            def _(pe):
                pe.wait_ge(init, 4)
                with pe.Fori(0, B) as it:
                    def inside(s, t):
                        n = NT * s + t
                        pe.wait_ge(abs_done, it * (NT * QUADS) + n + 1)
                        if t % 4 == 0:
                            pe.wait_ge(out_kept, it * 8 + n // 4 + 1)
                        c = slice((t % 4) * P, (t % 4) * P + P)
                        for hq in range(4):
                            ins = nc.tensor.matmul(po[VW * hq:VW * hq + VW, c], v[:, s, t, DH * hq:DH * hq + VW],
                                                   kept[:, t % DEEP, hq * P:hq * P + P], start=True, stop=True)
                        if t % 4 == 3:
                            for x in range(4):
                                ins = nc.tensor.matmul(pd[VW * x:VW * x + VW, :], ones[:, :], absd[:, t - 3 + x, :],
                                                       start=True, stop=True)
                        ins.then_inc(pv_done, 1)

                    def diagonal(s, t):
                        n = NT * s + t
                        if t == 0:
                            pe.wait_ge(in_loaded[s], it * LOADS + LOADS)
                        if n:
                            pe.wait_ge(masked, it * (NT * QUADS) + n)
                        ts = slice(t * P, t * P + P)
                        for hq in range(4):
                            r = slice(ROWS * (hq % 2), ROWS * (hq % 2) + ROWS)
                            ins = nc.tensor.matmul(pt[t % 2][:, hq // 2, hq % 2, :], k[r, s, hq // 2, ts],
                                                   q[r, s, hq // 2, ts], start=True, stop=True)
                        ins.then_inc(pt_done, 1)

                    waiting = []
                    diagonal(0, 0)
                    for s in range(QUADS):
                        for t in range(NT):
                            for g in range(PER_TILE * t, PER_TILE * t + PER_TILE):
                                hq, tq, c = units[g]
                                e, i = ("act", "dve")[g % 2], g // 2
                                r = slice(ROWS * (hq % 2), ROWS * (hq % 2) + ROWS)
                                w = min(HALF, P * tq - HALF * c)
                                done = MINE * s + i
                                if done >= 2:
                                    pe.wait_ge(unit_read[e], it * (MINE * QUADS) + done - 1)
                                nc.tensor.matmul(rows[e][i % 2][:, 0:w], q[r, s, hq // 2, tq * P:tq * P + P],
                                                 k[r, s, hq // 2, HALF * c:HALF * c + w], start=True,
                                                 stop=True).then_inc(unit_done[e], 1)
                                if g % PER_TILE == 2 and (s, t) != (QUADS - 1, NT - 1):
                                    diagonal(s + (t + 1) // NT, (t + 1) % NT)
                            waiting.append((s, t))
                            if len(waiting) > LAG:
                                inside(*waiting.pop(0))
                    for n in waiting:
                        inside(*n)
                    for e in ("act", "dve"):
                        pe.wait_ge(unit_read[e], it * (MINE * QUADS) + MINE * QUADS)


def experts(nc, A):
    PART = SLOTS // 2
    U = 10
    unit_of = {}
    for i, (t, c) in enumerate((t, c) for t in range(1, NT) for c in range((t + 3) // 4)):
        unit_of[t, c] = i
    with Space(nc) as m:
        ps = m.psum("psE")
        ident = m.sb("identE", [P, P])
        x = m.sb("xE", [P, 2, SLOT_TILES, D])
        fc1, fc2 = m.sb("fc1E", [P, 2, FF]), m.sb("fc2E", [P, 2, FC, D])
        b1, b2, ls = m.sb("b1E", [P, 2, FC]), m.sb("b2E", [P, 2, D]), m.sb("lsE", [P, 2, D])
        xT = m.sb("xTE", [P, SLOTS])
        hT = m.sb("hTE", [P, FC, SLOTS])
        y, z = m.sb("yE", [P, SLOT_TILES, D]), m.sb("zE", [P, SLOT_TILES, D])
        scaled = m.sb("scaledE", [P, SLOT_TILES, D])
        inter, intra = m.sb("interE", [P, S]), m.sb("intraE", [P, S])
        sums = m.sb("sumsE", [P, QUADS, 2, U, 2])
        diag = m.sb("diagE", [P, P])
        gate = m.sb("gateE", [P, NT, D])
        outT = m.sb("outTE", [P, S])
        den, rden = m.sb("denE", [P, NT, H]), m.sb("rdenE", [P, NT, H])
        ret, sq = m.sb("retE", [P, NT, D]), m.sb("sqE", [P, NT, D])
        gated = m.sb("gatedE", [P, NT, D])
        ms, rms = m.sb("msE", [P, NT * H]), m.sb("rmsE", [P, NT * H])
        root, square = m.sb("rootE", [P, NT * H]), m.sb("squareE", [P, NT * H])
        loaded = m.sem("constE")
        in_loaded = [m.sem(f"in_loadedE{i}") for i in range(2)]
        turned, xT_ready, h_done, gelu_done = (m.sem(n) for n in ("turnedE", "xT_readyE", "h_doneE", "gelu_doneE"))
        y_done, y_biased, y_scaled, z_ready, stored = (m.sem(n) for n in ("y_doneE", "y_biasedE", "y_scaledE", "z_readyE", "storedE"))
        ret_loaded, summed, by_token, step = (m.sem(n) for n in ("ret_loadedE", "summedE", "by_tokenE", "stepE"))
        ms_ready, root_ready, gated_ready, ret_stored = (m.sem(n) for n in ("ms_readyE", "root_readyE", "gated_readyE", "ret_storedE"))
        LOADS, RET_LOADS = 16 * 6, 16 * 5
        STEPS = 14
        with nc.Block() as block:
            @block.sync
            def _(sp):
                sp.dma_start(ident[:, :], A["ident"]).then_inc(loaded, 16)

                def load(i, src):
                    xd, f1, f2, c1, c2, l = src
                    for dst, s in ((x[:, i], xd), (fc1[:, i, :], f1), (fc2[:, i], f2), (b1[:, i, :], c1), (b2[:, i, :], c2),
                                   (ls[:, i, :], l)):
                        sp.dma_start(dst, s).then_inc(in_loaded[i], 16)

                def sources(sel):
                    return (sel(A["slot_x"].rearrange("(e t p) c -> e p t c", t=SLOT_TILES, p=P)).rearrange("a p t c -> (a p) t c"),
                            sel(A["fc1T"]).rearrange("a c h -> (a c) h"),
                            sel(A["fc2T"]).rearrange("a h q c -> (a h) q c"),
                            sel(A["fc1_b"]).rearrange("a p q -> (a p) q"),
                            sel(A["fc2_b"]).broadcast_to((P, D)), sel(A["ls"]).broadcast_to((P, D)))

                def load_retention(sel):
                    for dst, src in (
                            (inter[:, :], sel(A["inter"]).rearrange("a p s -> (a p) s")),
                            (intra[:, :], sel(A["o1"]).rearrange("a h r s -> (a h r) s")),
                            (sums[:, :, :, :, :].rearrange("p q a u b -> p q (a u b)"), sel(A["sums"]).rearrange("a q p u -> p (a q) u")),
                            (diag[:, :], sel(A["diag"]).rearrange("a q t (h i) -> (a q t h) i", h=4)),
                            (gate[:, :, :], sel(A["g1"]).rearrange("a (t p) c -> p (a t) c", p=P))):
                        sp.dma_start(dst, src).then_inc(ret_loaded, 16)

                load(0, sources(lambda a: a[0:1]))
                load_retention(lambda a: a[0:1])
                with sp.Fori(0, NE // 2) as it:
                    src1 = sources(lambda a: a[bass.ds(it * 2 + 1, 1)])
                    src0 = sources(lambda a: a[bass.ds((it * 2 + 2) % NE, 1)])
                    out = [A["slot_y"][0:ALL_SLOTS, :].rearrange("(e t p) c -> e p t c", t=SLOT_TILES, p=P)[
                        bass.ds(it * 2 + i, 1)].rearrange("a p t c -> (a p) t c") for i in range(2)]
                    ret_out = one(A["ret"], it).rearrange("a (t p) c -> p (a t) c", p=P)
                    z_at = [sp.snap(it * 2 + i + 1) for i in range(2)]
                    gated_at = sp.snap(it + 1)
                    load(1, src1)
                    sp.wait_ge(z_ready, z_at[0])
                    sp.dma_start(out[0], z[:, :, :]).then_inc(stored, 16)
                    load(0, src0)
                    sp.wait_ge(gated_ready, gated_at)
                    sp.dma_start(ret_out, gated[:, :, :]).then_inc(ret_stored, 16)
                    load_retention(lambda a: a[bass.ds((it + 1) % B, 1)])
                    sp.wait_ge(z_ready, z_at[1])
                    sp.dma_start(out[1], z[:, :, :]).then_inc(stored, 16)
                sp.wait_ge(in_loaded[0], LOADS * (NE // 2 + 1))
                sp.wait_ge(ret_loaded, RET_LOADS * (B + 1))
                sp.wait_ge(stored, 16 * NE + 1)
                sp.wait_ge(ret_stored, 16 * B + 1)

            @block.tensor
            def _(pe):
                pe.wait_ge(loaded, 16)
                with pe.Fori(0, NE // 2) as it:
                    for i in range(2):
                        pe.wait_ge(in_loaded[i], it * LOADS + LOADS)
                        for t in range(SLOT_TILES):
                            ins = nc.tensor.transpose(ps[:, t // 4, (t % 4) * P:(t % 4) * P + P], x[:, i, t, :], ident[:, :])
                        ins.then_inc(turned, 1)
                        pe.wait_ge(xT_ready, it * 2 + i + 1)
                        for c in range(FC):
                            for h in range(2):
                                n = 2 * c + h
                                if n >= 2:
                                    pe.wait_ge(gelu_done, it * (4 * FC) + 2 * FC * i + n - 1)
                                nc.tensor.matmul(ps[:, 2 + n % 2, 0:PART], fc1[:, i, c * P:c * P + P],
                                                 xT[:, h * PART:h * PART + PART], start=True, stop=True).then_inc(h_done, 1)
                        pe.wait_ge(gelu_done, it * (4 * FC) + 2 * FC * (i + 1))
                        pe.wait_ge(y_biased, it * 2 + i + 1)
                        for t in range(SLOT_TILES):
                            for c in range(FC):
                                ins = nc.tensor.matmul(ps[:, 6 + t // 4, (t % 4) * P:(t % 4) * P + P],
                                                       hT[:, c, t * P:t * P + P], fc2[:, i, c, :], start=(c == 0),
                                                       stop=(c == FC - 1))
                        if i == 0:
                            pe.wait_ge(summed, it + 1)
                            for t in range(NT):
                                nc.tensor.transpose(ps[:, 4 + t // 4, (t % 4) * P:(t % 4) * P + P], outT[:, t * P:t * P + P],
                                                    ident[:, :])
                            ins = nc.tensor.transpose(ps[:, 7, 3 * P:4 * P], diag[:, :], ident[:, :])
                        ins.then_inc(y_done, 1)

            @block.scalar
            def _(act):
                with act.Fori(0, NE // 2) as it:
                    for i in range(2):
                        act.wait_ge(turned, it * 2 + i + 1)
                        nc.scalar.copy(xT[:, :], ps[:, 0:2, :].rearrange("p b f -> p (b f)")[:, 0:SLOTS]).then_inc(xT_ready, 1)
                        for c in range(FC):
                            for h in range(2):
                                n = 2 * c + h
                                act.wait_ge(h_done, it * (4 * FC) + 2 * FC * i + n + 1)
                                nc.scalar.activation(hT[:, c, h * PART:h * PART + PART], ps[:, 2 + n % 2, 0:PART], ACT.Gelu,
                                                     bias=b1[:, i, c:c + 1]).then_inc(gelu_done, 1)
                    act.wait_ge(ms_ready, it + 1)
                    nc.scalar.activation(root[:, :], ms[:, :], ACT.Sqrt).then_inc(root_ready, 1)

            @block.vector
            def _(dve):
                V = nc.vector
                dve.sem_inc(stored, 1)
                dve.sem_inc(ret_stored, 1)
                dve.sem_inc(y_biased, 1)
                with dve.Fori(0, NE // 2) as it:
                    link, count = linker(dve, step, it * STEPS)

                    def expert(i):
                        V.tensor_tensor(y[:, :, :], ps[:, 6:8, :].rearrange("p b (t c) -> p (b t) c", c=D)[:, 0:SLOT_TILES, :],
                                        b2[:, i, None, :].broadcast_to((P, SLOT_TILES, D)), ALU.add).then_inc(y_biased, 1)
                        dve.wait_ge(y_biased, it * 2 + i + 2)
                        V.tensor_tensor(scaled[:, :, :], y[:, :, :], ls[:, i, None, :].broadcast_to((P, SLOT_TILES, D)),
                                        ALU.mult).then_inc(y_scaled, 1)
                        dve.wait_ge(stored, it * 32 + 16 * i + 1)
                        dve.wait_ge(y_scaled, it * 2 + i + 1)
                        V.tensor_tensor(z[:, :, :], scaled[:, :, :], x[:, i], ALU.add).then_inc(z_ready, 1)

                    dve.wait_ge(ret_loaded, it * RET_LOADS + RET_LOADS)
                    V.tensor_tensor(outT[:, :], inter[:, :], intra[:, :], ALU.add).then_inc(summed, 1)
                    dve.wait_ge(y_done, it * 2 + 1)
                    link(V.tensor_copy(den[:, :, :].rearrange("p t (q h) -> p q t h", h=4),
                                       ps[:, 7, 3 * P:4 * P].rearrange("p (q t h) -> p q t h", q=QUADS, h=4)))
                    expert(0)
                    for c in range(2):
                        for t in range(1 + 4 * c, NT):
                            d = den[:, t, :].rearrange("p (q b a) -> p q a b", b=2, a=2)
                            ins = V.tensor_tensor(d, d, sums[:, :, :, unit_of[t, c], :], ALU.add)
                        link(ins)
                    link(V.tensor_scalar(den[:, :, :], den[:, :, :], 1.0, 50000.0, ALU.max, ALU.min))
                    link(V.reciprocal(rden[:, :, :], den[:, :, :]))
                    for b in range(2):
                        t4 = slice(4 * b, 4 * b + 4)
                        ins = V.tensor_tensor(ret[:, t4, :].rearrange("p t (h d) -> p (t h) d", d=DH),
                                              ps[:, 4 + b, :].rearrange("p (g d) -> p g d", d=DH),
                                              rden[:, t4, :].rearrange("p t h -> p (t h)")[:, :, None].broadcast_to((P, 4 * H, DH)),
                                              ALU.mult)
                    link(ins)
                    link(V.tensor_tensor(sq[:, :, :], ret[:, :, :], ret[:, :, :], ALU.mult))
                    link(V.tensor_reduce(ms[:, :], sq[:, :, :].rearrange("p t (h d) -> p (t h) d", d=DH), AX.X, ALU.add))
                    V.tensor_scalar(ms[:, :], ms[:, :], 1.0 / DH, RMS_EPS, ALU.mult, ALU.add).then_inc(ms_ready, 1)
                    dve.wait_ge(root_ready, it + 1)
                    link(V.reciprocal(rms[:, :], root[:, :]))
                    link(V.tensor_tensor(square[:, :], rms[:, :], rms[:, :], ALU.mult))
                    link(V.tensor_tensor(square[:, :], square[:, :], ms[:, :], ALU.mult))
                    link(V.tensor_scalar(square[:, :], square[:, :], -0.5, 1.5, ALU.mult, ALU.add))
                    link(V.tensor_tensor(rms[:, :], rms[:, :], square[:, :], ALU.mult))
                    r3 = ret[:, :, :].rearrange("p t (h d) -> p (t h) d", d=DH)
                    link(V.tensor_tensor(r3, r3, rms[:, :, None].broadcast_to((P, NT * H, DH)), ALU.mult))
                    dve.wait_ge(ret_stored, it * 16 + 1)
                    V.tensor_tensor(gated[:, :, :], ret[:, :, :], gate[:, :, :], ALU.mult).then_inc(gated_ready, 1)
                    assert count[0] == STEPS
                    dve.wait_ge(y_done, it * 2 + 2)
                    expert(1)


def finish(nc, A):
    with Space(nc) as m:
        ret, x1 = m.sb("retF", [P, 2, NT, D]), m.sb("x1F", [P, 2, NT, D])
        index, weight = m.sb("indexF", [P, B, 2 * NT], I32), m.sb("weightF", [P, 2, 2 * NT])
        rows = m.sb("rowsF", [P, 2, 2, NT, D])
        first, moe, gate = (m.sb(n, [P, 2, NT, D]) for n in ("firstF", "moeF", "gateF"))
        prod, res = m.sb("prodF", [P, 2, NT, D]), m.sb("resF", [P, 2, NT, D])
        idx_loaded, first_ready, moe_ready, silued, prod_ready, done, stored = (
            m.sem(n) for n in ("idx_loadedF", "first_readyF", "moe_readyF", "siluedF", "prod_readyF", "doneF", "storedF"))
        in_loaded = [m.sem(f"in_loadedF{i}") for i in range(2)]
        gathered = [m.sem(f"gatheredF{i}") for i in range(2)]
        LOADS, ROWS_OF = 16 * 3, 16 * 2 * NT
        with nc.Block() as block:
            @block.sync
            def _(sp):
                def load(i, sel):
                    for dst, src in ((ret[:, i], sel(A["ret"]).rearrange("a (t p) c -> p (a t) c", p=P)),
                                     (x1[:, i], sel(A["x1"]).rearrange("a (t p) c -> p (a t) c", p=P)),
                                     (weight[:, i, :], sel(A["weight"]).rearrange("a p k -> (a p) k"))):
                        sp.dma_start(dst, src).then_inc(in_loaded[i], 16)

                sp.dma_start(index[:, :, :], A["index"].rearrange("b p k -> p b k")).then_inc(idx_loaded, 16)
                for i in range(2):
                    load(i, lambda a: a[i:i + 1])
                with sp.Fori(0, B // 2) as it:
                    out = [A["out"][bass.ds(it * 2 + i, 1)].rearrange("a (t p) c -> p (a t) c", p=P) for i in range(2)]
                    done_at = [sp.snap(it * 2 + i + 1) for i in range(2)]
                    for i in range(2):
                        sp.wait_ge(done, done_at[i])
                        sp.dma_start(out[i], res[:, i]).then_inc(stored, 16)
                        load(i, lambda a: a[bass.ds((it * 2 + 2 + i) % B, 1)])
                for i in range(2):
                    sp.wait_ge(in_loaded[i], LOADS * (B // 2 + 1))
                sp.wait_ge(stored, 16 * B + 1)

            @block.gpsimd
            def _(pool):
                pool.wait_ge(idx_loaded, 16)
                for b in range(B):
                    if b >= 2:
                        pool.wait_ge(moe_ready, b - 1)
                    for kk in range(2):
                        for t in range(NT):
                            pool.indirect_dma_start(
                                rows[:, b % 2, kk, t, :], None, A["slot_y"],
                                bass.IndirectOffsetOnAxis(ap=index[:, b, kk * NT + t:kk * NT + t + 1], axis=0)
                            ).then_inc(gathered[b % 2], 16)

            @block.scalar
            def _(act):
                with act.Fori(0, B // 2) as it:
                    for i in range(2):
                        act.wait_ge(moe_ready, it * 2 + i + 1)
                        nc.scalar.activation(gate[:, i], moe[:, i], ACT.Silu).then_inc(silued, 1)

            @block.vector
            def _(dve):
                V = nc.vector
                dve.sem_inc(stored, 1)
                with dve.Fori(0, B // 2) as it:
                    for i in range(2):
                        dve.wait_ge(in_loaded[i], it * LOADS + LOADS)
                        dve.wait_ge(gathered[i], it * ROWS_OF + ROWS_OF)
                        for t in range(NT):
                            V.tensor_scalar(first[:, i, t, :], rows[:, i, 0, t, :], weight[:, i, t:t + 1], None,
                                            ALU.mult).then_inc(first_ready, 1)
                        for t in range(NT):
                            dve.wait_ge(first_ready, it * (2 * NT) + NT * i + t + 1)
                            ins = V.scalar_tensor_tensor(moe[:, i, t, :], rows[:, i, 1, t, :], weight[:, i, NT + t:NT + t + 1],
                                                         first[:, i, t, :], ALU.mult, ALU.add)
                        ins.then_inc(moe_ready, 1)
                        dve.wait_ge(silued, it * 2 + i + 1)
                        V.tensor_tensor(prod[:, i], ret[:, i], gate[:, i], ALU.mult).then_inc(prod_ready, 1)
                        dve.wait_ge(prod_ready, it * 2 + i + 1)
                        dve.wait_ge(stored, it * 32 + 1)
                        V.tensor_tensor(res[:, i], prod[:, i], x1[:, i], ALU.add).then_inc(done, 1)


def program(nc, A):
    project_and_ffn(nc, A)
    attention(nc, A)
    between_layers(nc, A)
    route(nc, A)
    retention(nc, A)
    experts(nc, A)
    finish(nc, A)


def constants():
    bf16 = mybir.dt.np(BF16)
    f = np.float64
    i = np.arange(S, dtype=f)
    d = np.arange(DH)
    sign = np.where(d % 2 == 0, -1.0, 1.0)
    ang0 = np.minimum(i, 255)[:, None] * (10000.0 ** (-2.0 * (d // 2) / DH))[None, :]
    rows = lambda a: np.tile(a.T, (H, 1))
    ang1 = i[:, None] * np.repeat(1.0 / 10000.0 ** np.linspace(0.0, 1.0, DH // 2), 2)[None, :]
    decay = np.log(1.0 - 2.0 ** (-5.0 - np.arange(H, dtype=f)))
    norm = 1.0 / np.sqrt(np.cumsum(np.exp(decay[:, None] * i[None, :]), axis=1))
    qs = np.repeat(np.exp(decay[:, None] * i) * norm, DH, axis=0)
    ks = np.repeat(np.exp(-decay[:, None] * i) * D ** -0.5, DH, axis=0)
    cos1, sin1 = rows(np.cos(ang1)), rows(np.sin(ang1) * sign)
    p = np.arange(P)
    pick = np.zeros((P, 8, P))
    for j in range(8):
        pick[2 * j + 1, j, :] = 1.0
    behind = np.where(p[None, :] > p[:, None], MASKED, 0.0)
    return {
        "ident": np.eye(P, dtype=np.float32), "identb": np.eye(P).astype(bf16),
        "mask_ij": behind.astype(bf16), "mask_ji": behind.T.astype(bf16).copy(),
        "cos0": rows(np.cos(ang0)).astype(np.float32), "sin0": rows(np.sin(ang0) * sign).astype(np.float32),
        "tables1": np.stack([cos1 * qs, sin1 * qs, cos1 * ks, sin1 * ks], axis=1).astype(np.float32),
        "pick": pick.astype(np.float32),
        "same_head": (p[:, None] // DH == p[None, :] // DH).astype(np.float32),
        "causal": (p[None, :] >= p[:, None]).astype(np.float32),
        "before": (p[:, None] < p[None, :]).astype(bf16),
        "rank": (NE - np.arange(NE, dtype=np.float32))[None, :],
    }


def layouts(inp):
    t = {k: np.ascontiguousarray(np.asarray(v)) for k, v in inp.items()}
    swap = np.arange(D) ^ 1
    chunks = lambda w: np.ascontiguousarray(w.T.reshape(FC, P, -1).transpose(1, 0, 2))
    x = t["L0_attn_in_features"]
    wq, wk, wv = (t["L0_attn_W_" + n].T for n in "qkv")
    q1, k1, v1, g1 = (t["L1_attn_W" + n] for n in "qkvg")
    return {
        "x": x,
        "w_proj0": np.stack([wq, wq[:, swap], wk, wk[:, swap], wv], axis=1),
        "w1T": t["L0_ffn_W1"].T, "w2T": chunks(t["L0_ffn_W2"]),
        "b1c": t["L0_ffn_b1"].reshape(FC, P).T, "b2": t["L0_ffn_b2"][None, :],
        "scale": t["L0_ffn_scale"].reshape(1, 1),
        "w_outT": t["L0_attn_W_o"].T,
        "w_proj1": np.stack([q1, q1[:, swap], k1, k1[:, swap]], axis=1), "w_vg1": np.stack([v1, g1], axis=1),
        "w_routerT": t["L1_ffn_router_w"].T, "b_router": t["L1_ffn_router_b"][None, :],
        "fc1T": t["L1_ffn_fc1_w"].transpose(0, 2, 1),
        "fc2T": t["L1_ffn_fc2_w"].transpose(0, 2, 1).reshape(NE, FC, P, D).transpose(0, 2, 1, 3),
        "fc1_b": t["L1_ffn_fc1_b"].reshape(NE, FC, P).transpose(0, 2, 1),
        "fc2_b": t["L1_ffn_fc2_b"], "ls": t["L1_ffn_layer_scale"],
    }


SCRATCH = {
    "q0": ([B, H, ROWS0, S], BF16), "k0": ([B, H, ROWS0, S], BF16), "v0": ([B, P, NT * H * VW], F32),
    "u": ([B + 1, S, D], F32), "o0": ([B, H, 2 * DH, S], F32),
    "x1": ([B, S, D], F32), "xn1": ([B, S, D], F32), "v1": ([B, S, D], F32), "g1": ([B, S, D], F32),
    "logits": ([B, P, NT * NE], F32), "inter": ([B, P, S], F32),
    "q1": ([B, H, AUG, S], BF16), "k1": ([B, H, AUG, S], BF16),
    "o1": ([B, H, DH, S], F32), "diag": ([B, QUADS, NT, 4 * P], F32), "sums": ([B, QUADS, P, 40], F32), "ret": ([B, S, D], F32),
    "index": ([B, P, 2 * NT], I32), "weight": ([B, P, 2 * NT], F32),
    "slot_x": ([ALL_SLOTS, D], F32), "slot_y": ([ALL_SLOTS + P, D], F32),
}


def build(nc, arrays):
    A = {n: nc.dram_tensor(n, a.shape, mybir.dt.from_np(a.dtype), kind="ExternalInput").ap() for n, a in arrays.items()}
    for n, (shape, dt) in SCRATCH.items():
        A[n] = nc.dram_tensor(n, shape, dt).ap()
    A["out"] = nc.dram_tensor("out", (B, S, D), F32, kind="ExternalOutput").ap()
    program(nc, A)


def kernel(**inputs):
    import concourse.bacc as bacc
    from concourse.bass_utils import run_bass_kernel_spmd as run

    nc = bacc.Bacc("TRN2", target_bir_lowering=False, num_devices=1)
    arrays = {n: np.ascontiguousarray(a) for n, a in {**constants(), **layouts(inputs)}.items()}
    build(nc, arrays)
    r = run(nc, [arrays], core_ids=[0])
    return r.results[0]["out"]
```

```python
from contextlib import ExitStack

import numpy as np

import concourse.bass as bass
from concourse import mybir

F32 = mybir.dt.float32
BF16 = mybir.dt.bfloat16
I32 = mybir.dt.int32
ALU = mybir.AluOpType
ACT = mybir.ActivationFunctionType
AX = mybir.AxisListType

P = 128
B, S, D = 4, 1024, 128
H, DH = 16, 8
NT = S // P
NTILES = B * NT
HALF = 512
FF = 512
FC = FF // P
QUADS = H // 4
ROWS = 64
VW = 32
AUG = 48
ROWS0 = AUG + 2
Q_ROWS = {"hi": (0, 1, 2), "mid": (3, 4), "lo": (5,)}
K_ROWS = {"hi": (0, 3, 5), "mid": (1, 4), "lo": (2,)}
NE = 8
N = B * S
CAP = int(1.2 * (N // NE + 1))
SLOT_TILES = -(-CAP // P)
SLOTS = SLOT_TILES * P
ALL_SLOTS = NE * SLOTS
NO_SLOT = ALL_SLOTS
ROW = D + 1
FRONT = [(t, c) for t in range(1, NT) for c in range((t + 3) // 4)]
MASKED = -1.0e30
LN_EPS, RMS_EPS, TOP_EPS = 1e-5, 1e-6, 1e-9


def linker(engine, semaphore, base):
    count = [0]

    def link(ins):
        count[0] += 1
        ins.then_inc(semaphore, 1)
        engine.wait_ge(semaphore, base + count[0])

    return link, count


class Space:

    def __init__(self, nc):
        self.nc, self.stack = nc, ExitStack()

    def __enter__(self):
        self.stack.__enter__()
        return self

    def __exit__(self, *e):
        return self.stack.__exit__(*e)

    def sb(self, name, shape, dt=F32):
        return self.stack.enter_context(self.nc.sbuf_tensor(name, shape, dt))

    def psum(self, name):
        return self.stack.enter_context(self.nc.psum_tensor(name, [P, 8, HALF], F32))

    def sem(self, name):
        return self.stack.enter_context(self.nc.semaphore(name))


def one(ap, i):
    return ap[bass.ds(i, 1)]


def turn(it, i):
    return lambda per, n: (i * per + n if it is None else it * (2 * per) + i * per + n)


def in_register(engine, value):
    return value if isinstance(value, int) else engine.snap(value)


def split_rows(dst, it, rows):
    return [one(dst, it)[:, :, DH * r:DH * r + DH, :].rearrange("a h d s -> (a h) d s") for r in rows]


def project_and_ffn(nc, A):
    with Space(nc) as m:
        ps = m.psum("psA")
        ident = m.sb("identA", [P, P])
        cos, sin = m.sb("cosA", [P, S]), m.sb("sinA", [P, S])
        w_proj = m.sb("w_projA", [P, 5, P])
        w1 = m.sb("w1A", [P, FF])
        w2 = m.sb("w2A", [P, FC, P])
        b1 = m.sb("b1A", [P, FC])
        b2 = m.sb("b2A", [P, D])
        scale = m.sb("scaleA", [P, 1])
        pick = m.sb("pickA", [P, 8, P])
        eps, power = m.sb("epsA", [P, NT]), m.sb("powA", [P, NT])
        x = m.sb("xA", [P, NT, D])
        stat, mom = m.sb("statA", [P, NT, 6]), m.sb("momA", [P, NT, 2])
        held = m.sb("heldA", [P, 1])
        var, rstd = m.sb("varA", [P, NT]), m.sb("rstdA", [P, NT])
        xn = m.sb("xnA", [P, NT, D])
        xnT = m.sb("xnTA", [P, 2, S])
        terms = m.sb("termsA", [P, 2, 4, HALF])
        roped = m.sb("ropedA", [P, 2, S])
        rest = m.sb("restA", [P, 2, S])
        hi, mid, lo = (m.sb(n, [P, 2, 2, S], BF16) for n in ("hiA", "midA", "loA"))
        vaug = m.sb("vaugA", [P, 2, NT, H, VW])
        odd = m.sb("oddA", [P, 8])
        w1e = m.sb("w1eA", [P, FF])
        w2e = m.sb("w2eA", [P, FC, P])
        hT = m.sb("hTA", [P, FC, HALF])
        u = m.sb("uA", [P, 2, NT, D])
        aug = m.sb("augA", [B * H, 2, 2 * S], BF16)

        loaded, ready = m.sem("constA"), m.sem("initA")
        x_loaded, stats, moments = m.sem("x_loadedA"), m.sem("statsA"), m.sem("momentsA")
        var_ready, rstd_ready, xn_ready = m.sem("var_readyA"), m.sem("rstd_readyA"), m.sem("xn_readyA")
        turned, xnT_ready = m.sem("turnedA"), m.sem("xnT_readyA")
        projected, v_done, v_kept = m.sem("projectedA"), m.sem("v_doneA"), m.sem("v_keptA")
        outer_done, odd_ready, w_ready = m.sem("outer_doneA"), m.sem("odd_readyA"), m.sem("w_readyA")
        terms_ready, roped_ready = m.sem("terms_readyA"), m.sem("roped_readyA")
        hi_ready, rest_ready = m.sem("hi_readyA"), m.sem("rest_readyA")
        mid_ready, lo_ready = m.sem("mid_readyA"), m.sem("lo_readyA")
        h_done, gelu_done, u_done, u_ready = (m.sem(n) for n in ("h_doneA", "gelu_doneA", "u_doneA", "u_readyA"))
        stored, aug_stored = [m.sem(f"storedA{i}") for i in range(2)], m.sem("aug_storedA")
        STORES = 15
        consts = [(ident, A["ident"]), (cos, A["cos0"]), (sin, A["sin0"]), (w_proj, A["w_proj0"]), (w1, A["w1T"]),
                  (w2, A["w2T"]), (b1, A["b1c"]), (pick, A["pick"])]

        with nc.Block() as block:
            @block.sync
            def _(sp):
                def load(sel):
                    sp.dma_start(x[:, :, :], sel(A["x"]).rearrange("a (t p) c -> p (a t) c", p=P)).then_inc(x_loaded, 16)

                load(lambda a: a[0:1])
                for dst, src in consts:
                    sp.dma_start(dst[:], src).then_inc(loaded, 16)
                sp.dma_start(b2[:, :], A["b2"].broadcast_to((P, D))).then_inc(loaded, 16)
                sp.dma_start(scale[:, :], A["scale"].broadcast_to((P, 1))).then_inc(loaded, 16)
                sp.wait_ge(ready, 5)
                for i, n in enumerate(("q0", "k0")):
                    sp.dma_start(A[n].rearrange("b h r s -> (b h) r s")[:, AUG:ROWS0, :],
                                 aug[:, i, :].rearrange("p (r s) -> p r s", s=S)).then_inc(aug_stored, 16)
                sp.wait_ge(xn_ready, NT)
                load(lambda a: a[1:2])
                def pair(it, last):
                    if not last:
                        ahead = [A["x"][bass.ds(it * 2 + i + 2, 1)].rearrange("a (t p) c -> p (a t) c", p=P) for i in range(2)]
                    q_rows = [{k: split_rows(A["q0"], it * 2 + i, r) for k, r in Q_ROWS.items()} for i in range(2)]
                    k_rows = [{k: split_rows(A["k0"], it * 2 + i, r) for k, r in K_ROWS.items()} for i in range(2)]
                    ud = [A["u"][1:B + 1][bass.ds(it * 2 + i, 1)].rearrange("a (t p) c -> p (a t) c", p=P) for i in range(2)]
                    vd = [A["v0"][bass.ds(it * 2 + i, 1)].rearrange("a p f -> (a p) f") for i in range(2)]
                    count = [{n: in_register(sp, turn(it, i)(per, extra)) for n, per, extra in (
                        ("v", 2, 2), ("xn", NT, 2 * NT), ("hi", 2, 2), ("mid", 2, 2), ("lo", 2, 2), ("u", 2, 2), ("u_all", 2, 3))} for i in range(2)]
                    def store_parts(i, name, part):
                        for j, rows in ((0, q_rows[i]), (1, k_rows[i])):
                            for dst in rows[name]:
                                sp.dma_start(dst, part[:, i, j, :]).then_inc(stored[i], 16)

                    for i in range(2):
                        sp.wait_ge(v_kept, count[i]["v"])
                        sp.dma_start(vd[i], vaug[:, i].rearrange("p t h d -> p (t h d)")).then_inc(stored[i], 16)
                        if not last:
                            sp.wait_ge(xn_ready, count[i]["xn"])
                            sp.dma_start(x[:, :, :], ahead[i]).then_inc(x_loaded, 16)
                        sp.wait_ge(hi_ready, count[i]["hi"])
                        store_parts(i, "hi", hi)
                        sp.wait_ge(mid_ready, count[i]["mid"])
                        store_parts(i, "mid", mid)
                        sp.wait_ge(lo_ready, count[i]["lo"])
                        store_parts(i, "lo", lo)
                        for half, n in enumerate(("u", "u_all")):
                            sp.wait_ge(u_ready, count[i][n])
                            t4 = slice(4 * half, 4 * half + 4)
                            sp.dma_start(ud[i][:, t4, :], u[:, i, t4, :]).then_inc(stored[i], 16)

                with sp.Fori(0, B // 2 - 1) as it:
                    pair(it, False)
                pair(B // 2 - 1, True)
                sp.wait_ge(aug_stored, 32)
                for i in range(2):
                    sp.wait_ge(stored[i], 16 * STORES * (B // 2) + 1)

            @block.vector
            def _(dve):
                nc.vector.memset(eps[:, :], LN_EPS).then_inc(ready, 1)
                nc.vector.memset(power[:, :], -0.5).then_inc(ready, 1)
                for i in range(2):
                    nc.vector.memset(aug[:, i, :], float(i)).then_inc(ready, 1)
                    dve.sem_inc(stored[i], 1)
                dve.sem_inc(u_ready, 1)

                def statistics(at):
                    dve.wait_ge(x_loaded, at(16, 16))
                    for t in range(NT):
                        nc.vector.bn_stats(stat[:, t, :], x[:, t, :]).then_inc(stats, 1)
                    dve.wait_ge(stats, at(NT, NT))
                    nc.vector.memset(held[:, :], 0.0)
                    for t in range(NT):
                        nc.vector.bn_aggr(mom[:, t, :], stat[:, t, :]).then_inc(moments, 1)

                def normalise(at):
                    dve.wait_ge(rstd_ready, at(1, 1))
                    for t in range(NT):
                        nc.vector.tensor_scalar(xn[:, t, :], x[:, t, :], mom[:, t, 0:1], rstd[:, t:t + 1],
                                                ALU.subtract, ALU.mult).then_inc(xn_ready, 1)

                statistics(turn(None, 0))
                normalise(turn(None, 0))
                dve.wait_ge(loaded, 16 * (len(consts) + 2))
                def pair(it, last):
                    for i in range(2):
                        at, ahead = turn(it, i), turn(it, i + 1)

                        def rope(half):
                            c = slice(half * HALF, half * HALF + HALF)
                            dve.wait_ge(roped_ready, at(2, half + 1))
                            dve.wait_ge(projected, at(2, half + 1))
                            for j in range(4):
                                ins = nc.vector.tensor_tensor(terms[:, half, j, :], ps[:, 2 + j, :],
                                                              (cos if j % 2 == 0 else sin)[:, c], ALU.mult)
                            ins.then_inc(terms_ready, 1)

                        dve.wait_ge(xnT_ready, at(2, 1))
                        nc.vector.tensor_scalar(odd[:, :], xnT[:, i, 2:18:2], scale[:, 0:1], None,
                                                ALU.mult).then_inc(odd_ready, 1)
                        if not last or i == 0:
                            statistics(ahead)
                        rope(0)
                        dve.wait_ge(outer_done, at(1, 1))
                        dve.wait_ge(odd_ready, at(1, 1))
                        for j in range(4):
                            c = slice(j * P, j * P + P)
                            nc.vector.scalar_tensor_tensor(w1e[:, c], ps[:, 0, c], odd[:, j:j + 1], w1[:, c],
                                                           ALU.mult, ALU.add)
                        for j in range(4):
                            o = slice(j * 32, j * 32 + 32)
                            ins = nc.vector.scalar_tensor_tensor(
                                w2e[:, :, o], ps[:, 1, j * P:j * P + P].rearrange("p (r q) -> p q r", q=FC),
                                odd[:, 4 + j:5 + j], w2[:, :, o], ALU.mult, ALU.add)
                        ins.then_inc(w_ready, 1)
                        rope(1)
                        if not last or i == 0:
                            normalise(ahead)
                        dve.wait_ge(stored[i], it * (16 * STORES) + 1)
                        for half in range(2):
                            dve.wait_ge(u_done, at(2, half + 1))
                            nc.vector.tensor_tensor(
                                u[:, i, 4 * half:4 * half + 4, :], ps[:, 6 + half, :].rearrange("p (t c) -> p t c", c=D),
                                b2[:, None, :].broadcast_to((P, 4, D)), ALU.add).then_inc(u_ready, 1)

                with dve.Fori(0, B // 2 - 1) as it:
                    pair(it, False)
                pair(B // 2 - 1, True)

            @block.gpsimd
            def _(pool):
                nc.gpsimd.memset(vaug[:, :, :, :, :], 1.0).then_inc(ready, 1)
                pool.sem_inc(roped_ready, 2)

                def deviation(at):
                    pool.wait_ge(moments, at(NT, NT))
                    nc.gpsimd.tensor_tensor(var[:, :], mom[:, :, 1], eps[:, :], ALU.add).then_inc(var_ready, 1)
                    pool.wait_ge(var_ready, at(1, 1))
                    nc.gpsimd.tensor_tensor(rstd[:, :], var[:, :], power[:, :], ALU.pow).then_inc(rstd_ready, 1)

                pool.wait_ge(ready, 5)
                deviation(turn(None, 0))
                def pair(it, last):
                    for i in range(2):
                        at = turn(it, i)
                        if not last or i == 0:
                            deviation(turn(it, i + 1))
                        halves = [slice(half * HALF, half * HALF + HALF) for half in range(2)]
                        for half, c in enumerate(halves):
                            pool.wait_ge(terms_ready, at(2, half + 1))
                            for j in range(2):
                                ins = nc.gpsimd.tensor_tensor(roped[:, j, c], terms[:, half, 2 * j, :],
                                                              terms[:, half, 2 * j + 1, :], ALU.add)
                            ins.then_inc(roped_ready, 1)
                        for half, c in enumerate(halves):
                            pool.wait_ge(hi_ready, at(2, half + 1))
                            for j in range(2):
                                ins = nc.gpsimd.tensor_tensor(rest[:, j, c], roped[:, j, c], hi[:, i, j, c], ALU.subtract)
                            ins.then_inc(rest_ready, 1)
                        for half, c in enumerate(halves):
                            pool.wait_ge(mid_ready, at(2, half + 1))
                            for j in range(2):
                                ins = nc.gpsimd.tensor_tensor(lo[:, i, j, c], rest[:, j, c], mid[:, i, j, c], ALU.subtract)
                            ins.then_inc(lo_ready, 1)

                with pool.Fori(0, B // 2 - 1) as it:
                    pair(it, False)
                pair(B // 2 - 1, True)

            @block.scalar
            def _(act):
                def columns(at, i, half):
                    act.wait_ge(turned, at(2, half + 1))
                    nc.scalar.copy(xnT[:, i, half * HALF:half * HALF + HALF], ps[:, half, :]).then_inc(xnT_ready, 1)

                for half in range(2):
                    columns(turn(None, 0), 0, half)
                act.wait_ge(ready, 5)
                act.wait_ge(loaded, 16 * (len(consts) + 2))
                def pair(it, last):
                    for i in range(2):
                        at, ahead = turn(it, i), turn(it, i + 1)

                        def first_part(half):
                            c = slice(half * HALF, half * HALF + HALF)
                            act.wait_ge(roped_ready, at(2, half + 3))
                            nc.scalar.copy(hi[:, i, :, c], roped[:, :, c]).then_inc(hi_ready, 1)

                        def second_part(half):
                            c = slice(half * HALF, half * HALF + HALF)
                            act.wait_ge(rest_ready, at(2, half + 1))
                            nc.scalar.copy(mid[:, i, :, c], rest[:, :, c]).then_inc(mid_ready, 1)

                        def gelu(half):
                            for c in range(FC):
                                act.wait_ge(h_done, at(2 * FC, half * FC + c + 1))
                                if half == 1 and c == 0:
                                    act.wait_ge(u_done, at(2, 1))
                                nc.scalar.activation(hT[:, c, :], ps[:, 2 + c, :], ACT.Gelu,
                                                     bias=b1[:, c:c + 1]).then_inc(gelu_done, 1)

                        act.wait_ge(stored[i], it * (16 * STORES) + 1)
                        for half in range(2):
                            act.wait_ge(v_done, at(2, half + 1))
                            nc.scalar.copy(
                                vaug[:, i, 4 * half:4 * half + 4, :, 0:DH].rearrange("p t h d -> p (t h) d"),
                                ps[:, 6 + half, :].rearrange("p (g d) -> p g d", d=DH)).then_inc(v_kept, 1)
                        first_part(0)
                        gelu(0)
                        first_part(1)
                        second_part(0)
                        for half in range(2 if not last or i == 0 else 0):
                            columns(ahead, 1 - i, half)
                        second_part(1)
                        gelu(1)

                with act.Fori(0, B // 2 - 1) as it:
                    pair(it, False)
                pair(B // 2 - 1, True)

            @block.tensor
            def _(pe):
                def transposes(at):
                    for t in range(NT):
                        pe.wait_ge(xn_ready, at(NT, t + 1))
                        ins = nc.tensor.transpose(ps[:, t // 4, (t % 4) * P:(t % 4) * P + P], xn[:, t, :], ident[:, :])
                        if t % 4 == 3:
                            ins.then_inc(turned, 1)

                pe.wait_ge(loaded, 16 * (len(consts) + 2))
                transposes(turn(None, 0))
                def pair(it, last):
                    for i in range(2):
                        at, ahead = turn(it, i), turn(it, i + 1)

                        def project(half):
                            for j in range(4):
                                ins = nc.tensor.matmul(ps[:, 2 + j, :], w_proj[:, j, :],
                                                       xnT[:, i, half * HALF:half * HALF + HALF], start=True, stop=True)
                            ins.then_inc(projected, 1)

                        def feed_forward(half):
                            for c in range(FC):
                                nc.tensor.matmul(ps[:, 2 + c, :], w1e[:, c * P:c * P + P],
                                                 xnT[:, i, half * HALF:half * HALF + HALF], start=True,
                                                 stop=True).then_inc(h_done, 1)
                            for t in range(4):
                                for c in range(FC):
                                    if t == 0:
                                        pe.wait_ge(gelu_done, at(2 * FC, half * FC + c + 1))
                                    ins = nc.tensor.matmul(ps[:, 6 + half, t * P:t * P + P], hT[:, c, t * P:t * P + P],
                                                           w2e[:, c, :], start=(c == 0), stop=(c == FC - 1))
                            ins.then_inc(u_done, 1)

                        pe.wait_ge(xnT_ready, at(2, 1))
                        project(0)
                        pe.wait_ge(xnT_ready, at(2, 2))
                        for j in range(8):
                            ins = nc.tensor.matmul(ps[:, j // 4, (j % 4) * P:(j % 4) * P + P], pick[:, j, :], xn[:, 0, :],
                                                   start=True, stop=True)
                        ins.then_inc(outer_done, 1)
                        pe.wait_ge(u_ready, at(2, 1))
                        for t in range(NT):
                            ins = nc.tensor.matmul(ps[:, 6 + t // 4, (t % 4) * P:(t % 4) * P + P],
                                                   xnT[:, i, t * P:t * P + P], w_proj[:, 4, :], start=True, stop=True)
                            if t % 4 == 3:
                                ins.then_inc(v_done, 1)
                        pe.wait_ge(terms_ready, at(2, 1))
                        project(1)
                        pe.wait_ge(terms_ready, at(2, 2))
                        pe.wait_ge(w_ready, at(1, 1))
                        pe.wait_ge(v_kept, at(2, 2))
                        feed_forward(0)
                        if not last or i == 0:
                            transposes(ahead)
                        feed_forward(1)

                with pe.Fori(0, B // 2 - 1) as it:
                    pair(it, False)
                pair(B // 2 - 1, True)

def attention(nc, A):
    SLOTS_B, ITEMS = 12, 48
    units = [(hq, t, c) for t in range(NT) for c in range(t // 4 + 1) for hq in range(4)]
    UNITS = len(units) + 1
    slots = [(c, jt) for c in range(2) for jt in range(4 * c + 4)]
    PER_BATCH = UNITS * QUADS
    AHEAD = 12
    FIRST = UNITS + AHEAD
    DELAY = 4

    def unit_width(g):
        hq, t, c = units[g]
        return min(HALF, P * (t + 1) - HALF * c)

    def stream(s):
        first = [(s + 2, g) for g in range(AHEAD)]
        return [(s + 1, g) for g in range(AHEAD, len(units))] + first[:DELAY] + [(s + 1, None)] + first[DELAY:]

    def turned_at(s, last):
        return [g for _, (_, g) in units_with(s, last)].index(None) if not last or s < QUADS - 1 else 0

    def units_with(s, last):
        return list(enumerate(u for u in stream(s) if not last or u[0] < QUADS))

    def spread_units():
        cost = [64 + HALF * (c + 1) - max(HALF * c, P * jt) for c, jt in slots for _ in range(4)]
        work = [64 + (unit_width(g) if g is not None else HALF) for _, g in stream(0)]
        plan, done, spent, item = [], 0, 0.0, 0.0
        for n in range(ITEMS):
            item += cost[n]
            k = 0
            while done < UNITS and (n == ITEMS - 1 or (spent + work[done] / 2) / sum(work) <= item / sum(cost)):
                spent += work[done]
                done, k = done + 1, k + 1
            plan.append(k)
        return plan

    def bank_of(n):
        return (n % PER_BATCH) % 3

    def bank_before(n):
        return max(m for m in range(n - 5, n) if bank_of(m) == bank_of(n))

    with Space(nc) as m:
        ps = m.psum("psB")
        st = [ps[:, i, :] for i in range(3)]
        pv = [ps[:, 3 + c, :] for c in range(2)]
        mxb = [ps[:, 5 + i, :] for i in range(3)]
        ident, identb = m.sb("identB", [P, P]), m.sb("identbB", [P, P], BF16)
        mask_ij, mask_ji = m.sb("mask_ijB", [P, P], BF16), m.sb("mask_jiB", [P, P], BF16)
        empty = m.sb("emptyB", [P, SLOT_TILES, ROW])
        q, k = m.sb("qB", [P, QUADS, 2, S], BF16), m.sb("kB", [P, QUADS, 4, S], BF16)
        v = m.sb("vB", [P, QUADS, NT, 4 * VW])
        probs = m.sb("probsB", [P, 8, HALF])
        out = m.sb("outB", [P, 2, HALF])
        mx, mx2 = m.sb("mxB", [P, 2, 4, NT]), m.sb("mx2B", [P, 2, 4, NT // 2])
        neg = m.sb("negB", [32, 2, 2, P], BF16)

        loaded, cleared, q_cleared, k_cleared = m.sem("constB"), m.sem("clearedB"), m.sem("q_clearedB"), m.sem("k_clearedB")
        slots_cleared = m.sem("slots_clearedB")
        in_loaded = [m.sem(f"in_loadedB{s}") for s in range(QUADS)]
        st_done, exp_done, pv_done = m.sem("st_doneB"), m.sem("exp_doneB"), m.sem("pv_doneB")
        out_kept, out_stored = m.sem("out_keptB"), [m.sem(f"out_storedB{c}") for c in range(2)]
        max_done, max_read, combined, neg_hi = (m.sem(n) for n in ("max_doneB", "max_readB", "combinedB", "neg_hiB"))
        neg_placed = [m.sem(f"neg_placedB{p}") for p in range(2)]
        LOADS, PLACED = 16 * 9, 16 * 4

        with nc.Block() as block:
            @block.sync
            def _(sp):
                for dst, src in ((ident, "ident"), (identb, "identb"), (mask_ij, "mask_ij"), (mask_ji, "mask_ji")):
                    sp.dma_start(dst[:, :], A[src]).then_inc(loaded, 16)

                def load(s, qd, kd, vd):
                    for h in range(4):
                        r = slice(ROWS * (h % 2), ROWS * (h % 2) + ROWS0)
                        sp.dma_start(q[r, s, h // 2, :], qd[:, 4 * s + h].rearrange("a r s -> (a r) s")).then_inc(in_loaded[s], 16)
                        sp.dma_start(k[r, s, h, :], kd[:, 4 * s + h].rearrange("a r s -> (a r) s")).then_inc(in_loaded[s], 16)
                    sp.dma_start(v[:, s, :, :], vd.rearrange("a p (t f) -> (a p) t f", t=NT)[
                        :, :, s * 4 * VW:(s + 1) * 4 * VW]).then_inc(in_loaded[s], 16)

                def place(s, par):
                    for part in range(2):
                        for p in range(2):
                            sp.dma_start(q[AUG + part:AUG + part + ROWS + 1:ROWS, s, p, :],
                                         neg[2 * NT * p:2 * NT * p + 2 * NT, par, part, :]).then_inc(neg_placed[par], 16)

                for s in range(QUADS):
                    sp.wait_ge(k_cleared, s + 1)
                    sp.wait_ge(q_cleared, s + 1)
                    load(s, A["q0"][0:1], A["k0"][0:1], A["v0"][0:1])
                sp.wait_ge(max_read, len(units) + DELAY + 1)
                place(0, 0)
                sp.wait_ge(cleared, 2)
                for e in range(NE):
                    sp.dma_start(A["slot_x"][e * SLOTS:(e + 1) * SLOTS, :].rearrange("(t p) c -> p t c", p=P),
                                 empty[:, :, :]).then_inc(slots_cleared, 16)
                for g in range(2 * NTILES // 4):
                    sp.dma_start(A["back"][g * 4 * P:(g + 1) * 4 * P, :].rearrange("(t p) c -> p t c", p=P),
                                 empty[:, 0:4, 0:D]).then_inc(slots_cleared, 16)
                def batch(it, last):
                    if not last:
                        qd, kd, vd = (A[n][bass.ds(it + 1, 1)] for n in ("q0", "k0", "v0"))
                    od = one(A["o0"], it)
                    kept = [in_register(sp, it * 8 + 2 + e + 1) for e in range(8)]
                    used = [in_register(sp, it * (SLOTS_B * QUADS) + 2 + SLOTS_B * (s + 1)) for s in range(QUADS)]
                    maxed = [in_register(sp, it * PER_BATCH + FIRST + UNITS * s + 1 + turned_at(s, last)) for s in range(QUADS)]

                    def store(s, c):
                        sp.wait_ge(out_kept, kept[2 * s + c])
                        for hq in range(4):
                            sp.dma_start(od[:, 4 * s + hq, :, c * HALF:(c + 1) * HALF].rearrange("a r s -> (a r) s"),
                                         out[VW * hq:VW * hq + 2 * DH, c, :]).then_inc(out_stored[c], 16)

                    for s in range(QUADS):
                        store(s, 0)
                        if not last or s < QUADS - 1:
                            sp.wait_ge(max_read, maxed[s])
                            place((s + 1) % QUADS, (s + 1) % 2)
                        store(s, 1)
                        if not last:
                            sp.wait_ge(pv_done, used[s])
                            load(s, qd, kd, vd)

                with sp.Fori(0, B - 1) as it:
                    batch(it, False)
                batch(B - 1, True)
                for c in range(2):
                    sp.wait_ge(out_stored[c], 64 * B * QUADS + 1)
                sp.wait_ge(slots_cleared, 16 * (NE + 2 * NTILES // 4))

            @block.vector
            def _(dve):
                for s in range(QUADS):
                    nc.vector.memset(k[:, s], 0.0).then_inc(k_cleared, 1)
                nc.vector.memset(empty[:, :, 0:D], 0.0).then_inc(cleared, 1)
                nc.vector.memset(empty[:, :, D], float(2 * N)).then_inc(cleared, 1)
                dve.sem_inc(out_stored[0], 1)
                dve.sem_inc(out_stored[1], 1)
                dve.sem_inc(neg_placed[0], 1)
                dve.sem_inc(neg_placed[1], 1)

                def maximum(s, g, n, done, quads, placed):
                    par, bank = s % 2, mxb[bank_of(n)]
                    if g is None:
                        turned = bank[0:32, 0:P]
                        dve.wait_ge(neg_placed[par], placed * PLACED + 1)
                        dve.wait_ge(max_done, done + 1)
                        nc.vector.tensor_scalar(neg[:, par, 0, :], turned, -1.0, None, ALU.mult).then_inc(neg_hi, 1)
                        dve.wait_ge(neg_hi, quads + 1)
                        nc.vector.scalar_tensor_tensor(neg[:, par, 1, :], turned, -1.0, neg[:, par, 0, :], ALU.mult,
                                                       ALU.subtract).then_inc(max_read, 1)
                        return
                    hq, t, c = units[g]
                    dst = mx[:, par, hq, t:t + 1] if c == 0 else mx2[:, par, hq, t - 4:t - 3]
                    dve.wait_ge(max_done, done + 1)
                    nc.vector.tensor_reduce(dst, bank[:, 0:unit_width(g)], AX.X, ALU.max).then_inc(max_read, 1)
                    if g == len(units) - 1:
                        dve.wait_ge(max_read, done + 1)
                        nc.vector.tensor_tensor(mx[:, par, :, 4:8], mx[:, par, :, 4:8], mx2[:, par, :, :],
                                                ALU.max).then_inc(combined, 1)

                before = [(0, g) for g in range(AHEAD)] + stream(-1)
                for i, (s, g) in enumerate(before):
                    maximum(s, g, i - FIRST, i, 0, 0)

                def batch(it, last):
                    for s in range(QUADS):
                        for i, (x, g) in units_with(s, last):
                            n = UNITS * s + i
                            maximum(x, g, n, it * PER_BATCH + FIRST + n, it * QUADS + x, it * 2 + x // 2)

                with dve.Fori(0, B - 1) as it:
                    batch(it, False)
                batch(B - 1, True)

            @block.gpsimd
            def _(pool):
                for s in range(QUADS):
                    nc.gpsimd.memset(q[:, s], 0.0).then_inc(q_cleared, 1)

            @block.scalar
            def _(act):
                act.sem_inc(pv_done, 2)
                act.sem_inc(out_kept, 2)
                with act.Fori(0, B) as it:
                    def keep(s, c):
                        last = SLOTS_B * s + (4 if c == 0 else SLOTS_B)
                        act.wait_ge(pv_done, it * (SLOTS_B * QUADS) + 2 + last)
                        act.wait_ge(out_stored[c], it * (64 * QUADS) + 64 * s + 1)
                        nc.scalar.copy(out[:, c, :], pv[c]).then_inc(out_kept, 1)

                    for s in range(QUADS):
                        for j, (c, jt) in enumerate(slots):
                            w = HALF * (c + 1) - max(HALF * c, P * jt)
                            act.wait_ge(pv_done, it * (SLOTS_B * QUADS) + SLOTS_B * s + j + 1)
                            for hq in range(4):
                                n = ITEMS * s + 4 * j + hq
                                act.wait_ge(st_done, it * (ITEMS * QUADS) + n + 1)
                                nc.scalar.activation(probs[:, n % 8, 0:w], st[n % 3][:, 0:w], ACT.Exp,
                                                     scale=DH ** -0.5).then_inc(exp_done, 1)
                            if j == 5:
                                keep(s, 0)
                            if j == 1 and s:
                                keep(s - 1, 1)
                    keep(QUADS - 1, 1)

            @block.tensor
            def _(pe):
                def unit(x, g, n, it):
                    bank, par, s = mxb[bank_of(n)], x % 2, x % QUADS
                    if it is not None:
                        pe.wait_ge(max_read, it * PER_BATCH + FIRST + bank_before(n) + 1)
                    elif FIRST + bank_before(n) >= 0:
                        pe.wait_ge(max_read, FIRST + bank_before(n) + 1)
                    if g is None:
                        pe.wait_ge(combined, it * QUADS + x + 1 if it is not None else x + 1)
                        nc.tensor.transpose(bank[0:32, 0:P], mx[:, par, :, :].rearrange("p h t -> p (h t)"),
                                            ident[:, :]).then_inc(max_done, 1)
                        return
                    if g == 0:
                        pe.wait_ge(in_loaded[s], it * LOADS + LOADS * (1 + x // QUADS) if it is not None else LOADS)
                    hq, t, c = units[g]
                    w = unit_width(g)
                    last = c == t // 4
                    ins = nc.tensor.matmul(bank[:, 0:w], q[:, s, hq // 2, t * P:t * P + P],
                                           k[:, s, hq, HALF * c:HALF * c + w], start=True, stop=not last)
                    if last:
                        ins = nc.tensor.matmul(bank[:, w - P:w], identb[:, :], mask_ij[:, :], start=False, stop=True)
                    ins.then_inc(max_done, 1)

                plan = spread_units()
                pe.wait_ge(loaded, 64)
                for i, (x, g) in enumerate([(0, g) for g in range(AHEAD)] + stream(-1)):
                    unit(x, g, i - FIRST, None)
                def batch(it, last):
                    def products(s, j):
                        c, jt = slots[j]
                        i0 = max(HALF * c, P * jt)
                        n = ITEMS * s + 4 * j
                        pe.wait_ge(exp_done, it * (ITEMS * QUADS) + n + 4)
                        if jt == 0:
                            pe.wait_ge(out_kept, it * 8 + 2 * s + c + 1)
                        for hq in range(4):
                            ins = nc.tensor.matmul(pv[c][VW * hq:VW * hq + VW, i0 - HALF * c:HALF],
                                                   v[:, s, jt, VW * hq:VW * hq + VW],
                                                   probs[:, (n + hq) % 8, 0:HALF * (c + 1) - i0],
                                                   start=(jt == 0), stop=(jt == 4 * c + 3), skip_group_check=True)
                        ins.then_inc(pv_done, 1)

                    before = None
                    for s in range(QUADS):
                        todo = units_with(s, last)
                        pe.wait_ge(neg_placed[s % 2], it * (2 * PLACED) + PLACED * (s // 2 + 1) + 1)
                        for j, (c, jt) in enumerate(slots):
                            i0 = max(HALF * c, P * jt)
                            w = HALF * (c + 1) - i0
                            for hq in range(4):
                                n = ITEMS * s + 4 * j + hq
                                if n >= 3:
                                    pe.wait_ge(exp_done, it * (ITEMS * QUADS) + n - 2)
                                ins = nc.tensor.matmul(st[n % 3][:, 0:w], k[:, s, hq, jt * P:jt * P + P],
                                                       q[:, s, hq // 2, i0:i0 + w], start=True, stop=(jt < 4 * c))
                                if jt >= 4 * c:
                                    ins = nc.tensor.matmul(st[n % 3][:, 0:P], identb[:, :], mask_ji[:, :],
                                                           start=False, stop=True)
                                ins.then_inc(st_done, 1)
                                for i, (x, g) in todo[:plan[4 * j + hq]]:
                                    unit(x, g, UNITS * s + i, it)
                                todo = todo[plan[4 * j + hq]:]
                            if before:
                                products(*before)
                            before = (s, j)
                    products(*before)

                with pe.Fori(0, B - 1) as it:
                    batch(it, False)
                batch(B - 1, True)





def between_layers(nc, A):
    with Space(nc) as m:
        ps = m.psum("psC")
        ident = m.sb("identC", [P, P])
        tables = m.sb("tablesC", [P, 4, S])
        w_out = m.sb("w_outC", [P, D])
        w_proj = m.sb("w_projC", [P, 4, P])
        w_vg = m.sb("w_vgC", [P, 2, P])
        w_router, b_router = m.sb("w_routerC", [P, NE]), m.sb("b_routerC", [P, NE])
        same_head = m.sb("same_headC", [P, P])
        eps, power = m.sb("epsC", [P, NT]), m.sb("powC", [P, NT])
        den, rden = m.sb("denC", [P, B, P]), m.sb("rdenC", [P, B, P])
        oT, scale = m.sb("oTC", [P, S]), m.sb("scaleC", [P, S])
        x, u, gate = m.sb("xC", [P, NT, D]), m.sb("uC", [P, NT, D]), m.sb("gateC", [P, NT, D])
        headT = m.sb("headTC", [P, S])
        x1 = m.sb("x1C", [P, NT, D])
        stat, mom = m.sb("statC", [P, NT, 6]), m.sb("momC", [P, NT, 2])
        held = m.sb("heldC", [P, 1])
        var, rstd = m.sb("varC", [P, NT]), m.sb("rstdC", [P, NT])
        xn, xnT = m.sb("xnC", [P, NT, D]), m.sb("xnTC", [P, 2, S])
        terms = m.sb("termsC", [P, 2, 4, HALF])
        roped, rest = m.sb("ropedC", [P, 2, S]), m.sb("restC", [P, 2, S])
        hi, mid, lo = (m.sb(n, [P, 2, 2, S], BF16) for n in ("hiC", "midC", "loC"))
        v, gate1 = m.sb("vC", [P, 2, NT, D]), m.sb("gate1C", [P, 2, NT, D])
        logits = m.sb("logitsC", [P, 2, NT, NE])
        k_tok = m.sb("k_tokC", [P, NT, P])
        chunk_state = m.sb("chunk_stateC", [P, NT, P])
        state = m.sb("stateC", [P, NT, P])
        inter = m.sb("interC", [P, 2, S])

        names = ("const init den_loaded rden_ready rden_stored in_loaded gated head_ready s_done x1_half x1_ready stats "
                 "moments var_ready rstd_ready xn_ready turned xnT_ready projected vg_done v_kept g_kept router_done "
                 "logits_ready terms_ready roped_ready hi_ready rest_ready mid_ready lo_ready k_turned k_kept chunk_done "
                 "chunk_ready state_ready inter_done inter_kept x1_stored").split()
        g = {n: m.sem(n + "C") for n in names}
        stored = [m.sem(f"storedC{i}") for i in range(2)]
        consts = [(ident, "ident"), (tables, "tables1"), (w_out, "w_outT"), (w_proj, "w_proj1"), (w_vg, "w_vg1"),
                  (w_router, "w_routerT"), (same_head, "same_head")]
        STORES = 12 + 4
        LOADS = 16 * 4
        halves = [slice(half * HALF, half * HALF + HALF) for half in range(2)]
        fours = [slice(4 * half, 4 * half + 4) for half in range(2)]

        with nc.Block() as block:
            @block.sync
            def _(sp):
                by_token = lambda ap: ap.rearrange("a (t p) c -> p (a t) c", p=P)

                def sources(batch):
                    at = bass.ds(batch, 1)
                    return ((oT[:, :], A["o0"][at][:, :, 0:DH, :].rearrange("a h r s -> (a h) r s")),
                            (scale[:, :], A["rden"][at].rearrange("a h s -> (a h) s")[:, None, :].broadcast_to((H, DH, S))),
                            (x[:, :, :], by_token(A["x"][at])), (u[:, :, :], by_token(A["u"][1:B + 1][at])))

                def load(batch_sources):
                    for dst, src in batch_sources:
                        sp.dma_start(dst, src).then_inc(g["in_loaded"], 16)

                for b in range(B):
                    sp.dma_start(den[:, b, :], A["o0"][b, :, DH, :].rearrange("h (c i) -> h c i", i=P)).then_inc(g["den_loaded"], 16)
                for dst, src in consts:
                    sp.dma_start(dst[:], A[src]).then_inc(g["const"], 16)
                sp.dma_start(b_router[:, :], A["b_router"].broadcast_to((P, NE))).then_inc(g["const"], 16)
                sp.wait_ge(g["rden_ready"], 1)
                for b in range(B):
                    sp.dma_start(A["rden"][b].rearrange("h (c i) -> h c i", i=P), rden[:, b, :]).then_inc(g["rden_stored"], 16)
                sp.wait_ge(g["rden_stored"], 16 * B)
                load(sources(0))
                sp.wait_ge(g["x1_ready"], 2)
                load(sources(1))
                sp.wait_ge(g["xn_ready"], NT)
                sp.dma_start(by_token(A["x1"][0:1]), x1[:, :, :]).then_inc(g["x1_stored"], 16)
                sp.dma_start(by_token(A["xn1"][0:1]), xn[:, :, :]).then_inc(g["x1_stored"], 16)
                def pair(it, last):
                    if not last:
                        later = [sources(it * 2 + i + 2) for i in range(2)]
                    x1_out = [[by_token(A[n][bass.ds(it * 2 + i + 1, 1)]) for n in ("x1", "xn1")]
                              for i in range(1 if last else 2)]
                    here = [bass.ds(it * 2 + i, 1) for i in range(2)]
                    vd, gd = ([by_token(A[n][at]) for at in here] for n in ("v1", "g1"))
                    ld = [A["logits"][at].rearrange("a p f -> (a p) f") for at in here]
                    nd = [A["inter"][at].rearrange("a p s -> (a p) s") for at in here]
                    q_rows = [{n: split_rows(A["q1"], it * 2 + i, r) for n, r in Q_ROWS.items()} for i in range(2)]
                    k_rows = [{n: split_rows(A["k1"], it * 2 + i, r) for n, r in K_ROWS.items()} for i in range(2)]
                    count = [{n: in_register(sp, turn(it, i)(per, extra)) for n, per, extra in (
                        ("v_kept", 2, 2), ("logits_ready", 1, 2), ("x1_ready", 2, 4), ("g_kept", 2, 2),
                        ("xn_ready", NT, 2 * NT), ("hi_ready", 2, 2), ("mid_ready", 2, 2), ("lo_ready", 2, 2),
                        ("inter_kept", 2, 3))} for i in range(2)]
                    def store_parts(i, name, part):
                        for j, rows in ((0, q_rows[i]), (1, k_rows[i])):
                            for dst in rows[name]:
                                sp.dma_start(dst, part[:, i, j, :]).then_inc(stored[i], 16)

                    for i in range(2):
                        sp.wait_ge(g["v_kept"], count[i]["v_kept"])
                        sp.dma_start(vd[i], v[:, i]).then_inc(stored[i], 16)
                        sp.wait_ge(g["logits_ready"], count[i]["logits_ready"])
                        sp.dma_start(ld[i], logits[:, i].rearrange("p t e -> p (t e)")).then_inc(stored[i], 16)
                        if not last:
                            sp.wait_ge(g["x1_ready"], count[i]["x1_ready"])
                            load(later[i])
                        sp.wait_ge(g["g_kept"], count[i]["g_kept"])
                        sp.dma_start(gd[i], gate1[:, i]).then_inc(stored[i], 16)
                        sp.wait_ge(g["hi_ready"], count[i]["hi_ready"])
                        store_parts(i, "hi", hi)
                        if not last or i == 0:
                            sp.wait_ge(g["xn_ready"], count[i]["xn_ready"])
                            sp.dma_start(x1_out[i][0], x1[:, :, :]).then_inc(g["x1_stored"], 16)
                            sp.dma_start(x1_out[i][1], xn[:, :, :]).then_inc(g["x1_stored"], 16)
                        sp.wait_ge(g["mid_ready"], count[i]["mid_ready"])
                        store_parts(i, "mid", mid)
                        sp.wait_ge(g["lo_ready"], count[i]["lo_ready"])
                        store_parts(i, "lo", lo)
                        sp.wait_ge(g["inter_kept"], count[i]["inter_kept"])
                        sp.dma_start(nd[i], inter[:, i, :]).then_inc(stored[i], 16)

                with sp.Fori(0, B // 2 - 1) as it:
                    pair(it, False)
                pair(B // 2 - 1, True)
                sp.wait_ge(g["x1_stored"], 32 * B + 1)
                for i in range(2):
                    sp.wait_ge(stored[i], 16 * STORES * (B // 2) + 1)

            @block.vector
            def _(dve):
                nc.vector.memset(eps[:, :], LN_EPS).then_inc(g["init"], 1)
                nc.vector.memset(power[:, :], -0.5).then_inc(g["init"], 1)
                nc.vector.memset(state[:, 0, :], 0.0).then_inc(g["init"], 1)
                for i in range(2):
                    dve.sem_inc(stored[i], 1)
                dve.sem_inc(g["x1_stored"], 1)
                dve.sem_inc(g["logits_ready"], 1)
                dve.wait_ge(g["den_loaded"], 16 * B)
                nc.vector.reciprocal(rden[:, :, :], den[:, :, :]).then_inc(g["rden_ready"], 1)

                def heads(at):
                    dve.wait_ge(g["in_loaded"], at(LOADS, LOADS))
                    for half, c in enumerate(halves):
                        nc.vector.tensor_tensor(headT[:, c], oT[:, c], scale[:, c], ALU.mult).then_inc(g["head_ready"], 1)

                def residual(at):
                    dve.wait_ge(g["gated"], at(1, 1))
                    dve.wait_ge(g["x1_stored"], at(32, 1))
                    for half, t4 in enumerate(fours):
                        dve.wait_ge(g["s_done"], at(2, half + 1))
                        nc.vector.tensor_tensor(x1[:, t4, :], ps[:, half, :].rearrange("p (t c) -> p t c", c=D),
                                                gate[:, t4, :], ALU.mult).then_inc(g["x1_half"], 1)
                    for half, t4 in enumerate(fours):
                        dve.wait_ge(g["x1_half"], at(2, half + 1))
                        nc.vector.tensor_tensor(x1[:, t4, :], x1[:, t4, :], x[:, t4, :], ALU.add).then_inc(g["x1_ready"], 1)
                    for t in range(NT):
                        if t % 4 == 0:
                            dve.wait_ge(g["x1_ready"], at(2, t // 4 + 1))
                        nc.vector.bn_stats(stat[:, t, :], x1[:, t, :]).then_inc(g["stats"], 1)
                    dve.wait_ge(g["stats"], at(NT, NT))
                    nc.vector.memset(held[:, :], 0.0)
                    for t in range(NT):
                        nc.vector.bn_aggr(mom[:, t, :], stat[:, t, :]).then_inc(g["moments"], 1)

                def normalise(at):
                    dve.wait_ge(g["rstd_ready"], at(1, 1))
                    for t in range(NT):
                        nc.vector.tensor_scalar(xn[:, t, :], x1[:, t, :], mom[:, t, 0:1], rstd[:, t:t + 1],
                                                ALU.subtract, ALU.mult).then_inc(g["xn_ready"], 1)

                first = turn(None, 0)
                heads(first)
                residual(first)
                normalise(first)
                dve.wait_ge(g["const"], 16 * (len(consts) + 1))
                def pair(it, last):
                    for i in range(2):
                        at, ahead = turn(it, i), turn(it, i + 1)

                        def rope(half):
                            dve.wait_ge(g["roped_ready"], at(2, half + 1))
                            dve.wait_ge(g["projected"], at(2, half + 1))
                            for j in range(4):
                                ins = nc.vector.tensor_tensor(terms[:, half, j, :], ps[:, 2 + j, :], tables[:, j, halves[half]],
                                                              ALU.mult)
                            ins.then_inc(g["terms_ready"], 1)

                        if not last or i == 0:
                            heads(ahead)
                        rope(0)
                        dve.wait_ge(stored[i], it * (16 * STORES) + 1)
                        dve.wait_ge(g["router_done"], at(1, 1))
                        nc.vector.tensor_tensor(logits[:, i], ps[:, 0, 0:NT * NE].rearrange("p (t e) -> p t e", e=NE),
                                                b_router[:, None, :].broadcast_to((P, NT, NE)),
                                                ALU.add).then_inc(g["logits_ready"], 1)
                        rope(1)
                        if not last or i == 0:
                            residual(ahead)
                        for half, t4 in enumerate(fours):
                            dve.wait_ge(g["chunk_done"], at(2, half + 1))
                            nc.vector.tensor_tensor(chunk_state[:, t4, :], ps[:, 6 + half, :].rearrange("p (t c) -> p t c", c=P),
                                                    same_head[:, None, :].broadcast_to((P, 4, P)),
                                                    ALU.mult).then_inc(g["chunk_ready"], 1)
                        if not last or i == 0:
                            normalise(ahead)
                        dve.wait_ge(g["chunk_ready"], at(2, 2))
                        for t in range(1, NT):
                            if t > 1:
                                dve.wait_ge(g["state_ready"], at(NT - 1, t - 1))
                            nc.vector.tensor_tensor(state[:, t, :], state[:, t - 1, :], chunk_state[:, t - 1, :],
                                                    ALU.add).then_inc(g["state_ready"], 1)

                with dve.Fori(0, B // 2 - 1) as it:
                    pair(it, False)
                pair(B // 2 - 1, True)

            @block.gpsimd
            def _(pool):
                pool.sem_inc(g["roped_ready"], 2)

                def deviation(at):
                    pool.wait_ge(g["moments"], at(NT, NT))
                    nc.gpsimd.tensor_tensor(var[:, :], mom[:, :, 1], eps[:, :], ALU.add).then_inc(g["var_ready"], 1)
                    pool.wait_ge(g["var_ready"], at(1, 1))
                    nc.gpsimd.tensor_tensor(rstd[:, :], var[:, :], power[:, :], ALU.pow).then_inc(g["rstd_ready"], 1)

                pool.wait_ge(g["init"], 3)
                deviation(turn(None, 0))
                def pair(it, last):
                    for i in range(2):
                        at = turn(it, i)

                        def rope(half):
                            pool.wait_ge(g["terms_ready"], at(2, half + 1))
                            for j in (1, 0):
                                ins = nc.gpsimd.tensor_tensor(roped[:, j, halves[half]], terms[:, half, 2 * j, :],
                                                              terms[:, half, 2 * j + 1, :], ALU.add)
                            ins.then_inc(g["roped_ready"], 1)

                        rope(0)
                        rope(1)
                        for half, c in enumerate(halves):
                            pool.wait_ge(g["hi_ready"], at(2, half + 1))
                            for j in range(2):
                                ins = nc.gpsimd.tensor_tensor(rest[:, j, c], roped[:, j, c], hi[:, i, j, c], ALU.subtract)
                            ins.then_inc(g["rest_ready"], 1)
                            if half == 0 and (not last or i == 0):
                                deviation(turn(it, i + 1))
                        for half, c in enumerate(halves):
                            pool.wait_ge(g["mid_ready"], at(2, half + 1))
                            for j in range(2):
                                ins = nc.gpsimd.tensor_tensor(lo[:, i, j, c], rest[:, j, c], mid[:, i, j, c], ALU.subtract)
                            ins.then_inc(g["lo_ready"], 1)

                with pool.Fori(0, B // 2 - 1) as it:
                    pair(it, False)
                pair(B // 2 - 1, True)

            @block.scalar
            def _(act):
                act.sem_inc(g["inter_kept"], 1)

                def columns(at, i, half):
                    act.wait_ge(g["turned"], at(2, half + 1))
                    nc.scalar.copy(xnT[:, i, halves[half]], ps[:, half, :]).then_inc(g["xnT_ready"], 1)

                act.wait_ge(g["in_loaded"], LOADS)
                nc.scalar.activation(gate[:, :, :], u[:, :, :], ACT.Silu).then_inc(g["gated"], 1)
                for half in range(2):
                    columns(turn(None, 0), 0, half)
                def pair(it, last):
                    for i in range(2):
                        at, ahead = turn(it, i), turn(it, i + 1)

                        def first_part(half):
                            act.wait_ge(g["roped_ready"], at(2, half + 3))
                            nc.scalar.copy(hi[:, i, :, halves[half]], roped[:, :, halves[half]]).then_inc(g["hi_ready"], 1)

                        def second_part(half):
                            act.wait_ge(g["rest_ready"], at(2, half + 1))
                            nc.scalar.copy(mid[:, i, :, halves[half]], rest[:, :, halves[half]]).then_inc(g["mid_ready"], 1)

                        if not last or i == 0:
                            act.wait_ge(g["in_loaded"], ahead(LOADS, LOADS))
                            act.wait_ge(g["x1_half"], at(2, 2))
                            nc.scalar.activation(gate[:, :, :], u[:, :, :], ACT.Silu).then_inc(g["gated"], 1)
                        act.wait_ge(stored[i], it * (16 * STORES) + 1)
                        for half, t4 in enumerate(fours):
                            act.wait_ge(g["vg_done"], at(4, half + 1))
                            nc.scalar.copy(v[:, i, t4, :], ps[:, 6 + half, :].rearrange("p (t c) -> p t c", c=D)
                                           ).then_inc(g["v_kept"], 1)
                        first_part(0)
                        for half, t4 in enumerate(fours):
                            act.wait_ge(g["vg_done"], at(4, half + 3))
                            nc.scalar.activation(gate1[:, i, t4, :], ps[:, 6 + half, :].rearrange("p (t c) -> p t c", c=D),
                                                 ACT.Silu).then_inc(g["g_kept"], 1)
                        first_part(1)
                        for half in range(2):
                            act.wait_ge(g["k_turned"], at(2, half + 1))
                            nc.scalar.copy(k_tok[:, fours[half], :],
                                           ps[:, 2 + half, :].rearrange("p (t c) -> p t c", c=P)).then_inc(g["k_kept"], 1)
                        second_part(0)
                        for half in range(2 if not last or i == 0 else 0):
                            columns(ahead, 1 - i, half)
                        second_part(1)
                        for half in range(2):
                            act.wait_ge(g["inter_done"], at(2, half + 1))
                            nc.scalar.copy(inter[:, i, halves[half]], ps[:, 4 + half, :]).then_inc(g["inter_kept"], 1)

                with act.Fori(0, B // 2 - 1) as it:
                    pair(it, False)
                pair(B // 2 - 1, True)

            @block.tensor
            def _(pe):
                def place(bank, t):
                    return ps[:, bank + t // 4, (t % 4) * P:(t % 4) * P + P]

                def output_projection(at):
                    for t in range(NT):
                        if t % 4 == 0:
                            pe.wait_ge(g["head_ready"], at(2, t // 4 + 1))
                        ins = nc.tensor.matmul(place(0, t), headT[:, t * P:t * P + P], w_out[:, :], start=True, stop=True)
                        if t % 4 == 3:
                            ins.then_inc(g["s_done"], 1)

                def transposes(at):
                    for t in range(NT):
                        pe.wait_ge(g["xn_ready"], at(NT, t + 1))
                        ins = nc.tensor.transpose(place(0, t), xn[:, t, :], ident[:, :])
                        if t % 4 == 3:
                            ins.then_inc(g["turned"], 1)

                pe.wait_ge(g["const"], 16 * (len(consts) + 1))
                pe.wait_ge(g["init"], 3)
                output_projection(turn(None, 0))
                transposes(turn(None, 0))
                def pair(it, last):
                    for i in range(2):
                        at, ahead = turn(it, i), turn(it, i + 1)

                        def project(half):
                            for j in range(4):
                                ins = nc.tensor.matmul(ps[:, 2 + j, :], w_proj[:, j, :], xnT[:, i, halves[half]],
                                                       start=True, stop=True)
                            ins.then_inc(g["projected"], 1)

                        def by_token(j):
                            for t in range(NT):
                                if j == 1 and t % 4 == 0:
                                    pe.wait_ge(g["v_kept"], at(2, t // 4 + 1))
                                ins = nc.tensor.matmul(place(6, t), xnT[:, i, t * P:t * P + P], w_vg[:, j, :],
                                                       start=True, stop=True)
                                if t % 4 == 3:
                                    ins.then_inc(g["vg_done"], 1)

                        pe.wait_ge(g["inter_kept"], at(2, 1))
                        pe.wait_ge(g["xnT_ready"], at(2, 1))
                        project(0)
                        pe.wait_ge(g["xnT_ready"], at(2, 2))
                        for t in range(NT):
                            ins = nc.tensor.matmul(ps[:, 0, t * NE:t * NE + NE], xnT[:, i, t * P:t * P + P], w_router[:, :],
                                                   start=True, stop=True)
                        ins.then_inc(g["router_done"], 1)
                        by_token(0)
                        pe.wait_ge(g["terms_ready"], at(2, 1))
                        project(1)
                        pe.wait_ge(g["logits_ready"], at(1, 2))
                        if not last or i == 0:
                            output_projection(ahead)
                        by_token(1)
                        pe.wait_ge(g["terms_ready"], at(2, 2))
                        for t in range(NT):
                            if t % 4 == 0:
                                pe.wait_ge(g["roped_ready"], at(2, t // 4 + 3))
                            ins = nc.tensor.transpose(place(2, t), roped[:, 1, t * P:t * P + P], ident[:, :])
                            if t % 4 == 3:
                                ins.then_inc(g["k_turned"], 1)
                        for t in range(NT):
                            if t % 4 == 0:
                                pe.wait_ge(g["k_kept"], at(2, t // 4 + 1))
                                pe.wait_ge(g["g_kept"], at(2, t // 4 + 1))
                            ins = nc.tensor.matmul(place(6, t), k_tok[:, t, :], v[:, i, t, :], start=True, stop=True)
                            if t % 4 == 3:
                                ins.then_inc(g["chunk_done"], 1)
                        if not last or i == 0:
                            transposes(ahead)
                        for t in range(NT):
                            if t:
                                pe.wait_ge(g["state_ready"], at(NT - 1, t))
                            ins = nc.tensor.matmul(place(4, t), state[:, t, :], roped[:, 0, t * P:t * P + P],
                                                   start=True, stop=True)
                            if t % 4 == 3:
                                ins.then_inc(g["inter_done"], 1)

                with pe.Fori(0, B // 2 - 1) as it:
                    pair(it, False)
                pair(B // 2 - 1, True)

def routing(nc, A, m, counts):
    TK = 2 * NTILES
    before, ones_b = m.sb("beforeR", [P, P], BF16), m.sb("onesR", [P, P], BF16)
    rank = m.sb("rankR", [P, NE])
    ones = m.sb("ones_scanR", [P, TK])
    L = m.sb("logitsR", [P, NTILES, NE])
    top, z, e = m.sb("topR", [P, NTILES]), m.sb("zR", [P, NTILES, NE]), m.sb("eR", [P, NTILES, NE])
    total, inv = m.sb("totalR", [P, NTILES]), m.sb("invR", [P, NTILES])
    p = [m.sb(f"pR{i}", [P, NTILES, NE]) for i in range(2)]
    best = m.sb("bestR", [P, 2, NTILES])
    at = m.sb("atR", [P, 2, NTILES, NE])
    first = m.sb("firstR", [P, 2, NTILES])
    chosen = m.sb("chosenR", [P, 2, NTILES, NE])
    both, winv = m.sb("bothR", [P, NTILES]), m.sb("winvR", [P, NTILES])
    w, valid = m.sb("wR", [P, 2, NTILES]), m.sb("validR", [P, 2, NTILES])
    hot, hot_b = m.sb("hotR", [P, 2, NTILES, NE]), m.sb("hot_bR", [P, 2, NTILES, NE], BF16)
    upto = m.sb("uptoR", [P, TK, NE])
    pos = m.sb("posR", [P, TK, NE])
    own = m.sb("ownR", [P, TK])
    keep = m.sb("keepR", [P, TK])
    slot = m.sb("slotR", [P, TK])
    index = m.sb("indexR", [P, 2, NTILES], I32)
    weight = m.sb("weightR", [P, 2, NTILES])

    loaded, step, shifted, exped = m.sem("constR"), m.sem("stepR"), m.sem("shiftedR"), m.sem("expedR")
    hot_ready, counted, routed, stored = m.sem("hot_readyR"), m.sem("countedR"), m.sem("routedR"), m.sem("storedR")

    def spread(ap, n=NE):
        return ap[:, :, None].broadcast_to((P, ap.shape[1], n))

    def flat(ap):
        return ap[:, :, :, :].rearrange("p k t e -> p (k t) e")

    def load(sp):
        for dst, src in ((before, A["before"]), (rank, A["rank"].broadcast_to((P, NE)))):
            sp.dma_start(dst[:, :], src).then_inc(loaded, 16)
        sp.dma_start(L[:, :, :].rearrange("p (b t) e -> p b (t e)", b=B),
                     A["logits"].rearrange("b p f -> p b f")).then_inc(loaded, 16)

    def store(sp):
        sp.wait_ge(routed, 2)
        for b in range(B):
            for kk in range(2):
                sp.dma_start(A["index"][b, :, kk * NT:kk * NT + NT], index[:, kk, b * NT:b * NT + NT]).then_inc(stored, 16)
                sp.dma_start(A["weight"][b, :, kk * NT:kk * NT + NT], weight[:, kk, b * NT:b * NT + NT]).then_inc(stored, 16)

    def exponentials(act):
        act.wait_ge(shifted, 1)
        nc.scalar.activation(e[:, :, :], z[:, :, :], ACT.Exp).then_inc(exped, 1)

    def count_tokens(pe):
        pe.wait_ge(loaded, 48)
        pe.wait_ge(hot_ready, 1)
        rhs = hot_b[:, :, :, :].rearrange("p k t e -> p (k t e)")
        nc.tensor.matmul(counts[0], before[:, :], rhs, start=True, stop=True)
        nc.tensor.matmul(counts[1], ones_b[:, :], rhs, start=True, stop=True).then_inc(counted, 1)

    def choose(dve):
        V = nc.vector
        link, _ = linker(dve, step, 0)
        link(V.memset(ones[:, :], 1.0))
        link(V.memset(ones_b[:, :], 1.0))
        dve.wait_ge(loaded, 48)
        link(V.tensor_reduce(top[:, :], L[:, :, :], AX.X, ALU.max))
        V.tensor_tensor(z[:, :, :], L[:, :, :], spread(top), ALU.subtract).then_inc(shifted, 1)
        dve.wait_ge(exped, 1)
        link(V.tensor_reduce(total[:, :], e[:, :, :], AX.X, ALU.add))
        link(V.reciprocal(inv[:, :], total[:, :]))
        link(V.tensor_tensor(p[0][:, :, :], e[:, :, :], spread(inv), ALU.mult))
        ranks = rank[:, None, :].broadcast_to((P, NTILES, NE))
        for kk in range(2):
            link(V.tensor_reduce(best[:, kk, :], p[kk][:, :, :], AX.X, ALU.max))
            link(V.tensor_tensor(at[:, kk], p[kk][:, :, :], spread(best[:, kk, :]), ALU.is_equal))
            link(V.tensor_tensor(at[:, kk], at[:, kk], ranks, ALU.mult))
            link(V.tensor_reduce(first[:, kk, :], at[:, kk], AX.X, ALU.max))
            link(V.tensor_tensor(chosen[:, kk], at[:, kk], spread(first[:, kk, :]), ALU.is_equal))
            if kk == 0:
                link(V.scalar_tensor_tensor(p[1][:, :, :], chosen[:, 0], -2.0, p[0][:, :, :], ALU.mult, ALU.add))
        link(V.tensor_tensor(both[:, :], best[:, 0, :], best[:, 1, :], ALU.add))
        link(V.tensor_scalar(both[:, :], both[:, :], TOP_EPS, None, ALU.add))
        link(V.reciprocal(winv[:, :], both[:, :]))
        link(V.tensor_tensor(w[:, :, :], best[:, :, :], winv[:, None, :].broadcast_to((P, 2, NTILES)), ALU.mult))
        link(V.tensor_scalar(valid[:, :, :], w[:, :, :], TOP_EPS, None, ALU.is_gt))
        link(V.tensor_tensor(flat(hot), flat(chosen), spread(valid[:, :, :].rearrange("p k t -> p (k t)")), ALU.mult))
        V.tensor_copy(flat(hot_b), flat(hot)).then_inc(hot_ready, 1)
        dve.wait_ge(counted, 1)
        inside = counts[0].rearrange("p (g e) -> p g e", e=NE)
        tile_n = counts[1].rearrange("p (g e) -> p g e", e=NE)
        for x in range(NE):
            ins = V.tensor_tensor_scan(upto[:, :, x], ones[:, :], tile_n[:, :, x], 0.0, ALU.mult, ALU.add)
        link(ins)
        link(V.tensor_tensor(pos[:, :, :], upto[:, :, :], tile_n, ALU.subtract))
        link(V.tensor_tensor(pos[:, :, :], pos[:, :, :], inside, ALU.add))
        link(V.tensor_tensor(pos[:, :, :], pos[:, :, :], flat(hot), ALU.mult))
        link(V.tensor_reduce(own[:, :], pos[:, :, :], AX.X, ALU.add))
        flat2 = [a[:, :, :].rearrange("p k t -> p (k t)") for a in (valid, first, w, weight, index)]
        link(V.scalar_tensor_tensor(keep[:, :], own[:, :], float(CAP), flat2[0], ALU.is_lt, ALU.mult))
        link(V.scalar_tensor_tensor(slot[:, :], flat2[1], -float(SLOTS), own[:, :], ALU.mult, ALU.add))
        link(V.tensor_scalar(slot[:, :], slot[:, :], float(NE * SLOTS - NO_SLOT), None, ALU.add))
        link(V.tensor_tensor(slot[:, :], slot[:, :], keep[:, :], ALU.mult))
        V.tensor_scalar(flat2[4], slot[:, :], float(NO_SLOT), None, ALU.add).then_inc(routed, 1)
        V.tensor_tensor(flat2[3], flat2[2], keep[:, :], ALU.mult).then_inc(routed, 1)

    return load, store, exponentials, count_tokens, choose, stored


def retention(nc, A):
    units = [(hq, t, c) for t, c in FRONT for hq in range(4)]
    PER_TILE = len(units) // NT
    of_width = {w: [g for g, (hq, t, c) in enumerate(units) if min(HALF, P * t - HALF * c) == w] for w in range(P, HALF + 1, P)}
    plan = [("dve", 2 * P), ("act", 3 * P), ("dve", HALF), ("act", HALF), ("dve", P)]
    order, engine_of = [], []
    for _ in range(NT):
        for e, w in plan:
            order.append(of_width[w].pop(0))
            engine_of.append(e)
    place_of = [engine_of[:n].count(engine_of[n]) for n in range(len(units))]
    MINE = {e: engine_of.count(e) for e in ("act", "dve")}
    DEEP, DEEP_ABS = 4, 16
    LAG = 2
    VCOLS = 4 * DH + VW - DH
    with Space(nc) as m:
        ps = m.psum("psD")
        rows = {"act": [ps[:, 0, :], ps[:, 1, :]], "dve": [ps[:, 2, :], ps[:, 3, :]]}
        pt = [ps[:, 4:6, 2 * P * i:2 * P * i + 2 * P].rearrange("p b (a i) -> p a b i", a=2) for i in range(2)]
        po, pd = ps[:, 6, :], ps[:, 7, :]
        causal = m.sb("causalD", [P, P])
        ones = m.sb("onesD", [P, VW])
        q, k = m.sb("qD", [P, QUADS, 4, S], BF16), m.sb("kD", [P, QUADS, 2, S], BF16)
        v = m.sb("vD", [P, QUADS, NT, VCOLS])
        kept, absd = m.sb("keptD", [P, DEEP, 4 * P]), m.sb("absD", [P, DEEP_ABS, 4 * P])
        sums = m.sb("sumsD", [P, QUADS, len(units)])
        out, diag = m.sb("outD", [P, 2, HALF]), m.sb("diagD", [P, 2, HALF])

        x, index = m.sb("xD", [P, 2, NT, ROW]), m.sb("indexD", [P, 2 * NT], I32)
        token = m.sb("tokenD", [P, 2 * NT])

        load_logits, store_routes, exponentials, count_tokens, choose, routes_stored = routing(nc, A, m, (po, pd))
        loaded, q_cleared, k_cleared = m.sem("constD"), m.sem("q_clearedD"), m.sem("k_clearedD")
        x_loaded, scatter_step, scattered = m.sem("x_loadedD"), m.sem("scatter_stepD"), m.sem("scatteredD")
        in_loaded = [m.sem(f"in_loadedD{s}") for s in range(QUADS)]
        pt_done, sums_done, masked, abs_done, pv_done = (m.sem(n) for n in ("pt_doneD", "sums_doneD", "maskedD", "abs_doneD", "pv_doneD"))
        out_kept, sums_kept, out_stored = m.sem("out_keptD"), m.sem("sums_keptD"), [m.sem(f"out_storedD{p}") for p in range(2)]
        sums_stored = [m.sem(f"sums_storedD{s}") for s in range(QUADS)]
        unit_step = m.sem("unit_stepD")
        unit_done = {e: m.sem("unit_doneD_" + e) for e in ("act", "dve")}
        unit_read = {e: m.sem("unit_readD_" + e) for e in ("act", "dve")}
        LOADS = 16 * 9

        def sum_unit(eng, name, it, s, i):
            g, n = order[i], MINE[name] * s + place_of[i]
            eng.wait_ge(unit_done[name], it * (MINE[name] * QUADS) + n + 1)
            hq, t, c = units[g]
            w = min(HALF, P * t - HALF * c)
            return rows[name][n % 2][:, 0:w], sums[:, s, g:g + 1]

        with nc.Block() as block:
            @block.sync
            def _(sp):
                load_logits(sp)
                sp.dma_start(causal[:, :], A["causal"]).then_inc(loaded, 16)

                def load(s, qd, kd, vd):
                    for h in range(4):
                        r = slice(ROWS * (h % 2), ROWS * (h % 2) + AUG)
                        sp.dma_start(q[r, s, h, :], qd[:, 4 * s + h].rearrange("a r s -> (a r) s")).then_inc(in_loaded[s], 16)
                        sp.dma_start(k[r, s, h // 2, :], kd[:, 4 * s + h].rearrange("a r s -> (a r) s")).then_inc(in_loaded[s], 16)
                    n = min(VCOLS, D - 4 * DH * s)
                    sp.dma_start(v[:, s, :, 0:n], vd.rearrange("a (t p) c -> p (a t) c", p=P)[
                        :, :, 4 * DH * s:4 * DH * s + n]).then_inc(in_loaded[s], 16)

                for s in range(QUADS):
                    if s == 0:
                        sp.wait_ge(q_cleared, 3)
                    sp.wait_ge(k_cleared, s + 1)
                    load(s, A["q1"][0:1], A["k1"][0:1], A["v1"][0:1])
                store_routes(sp)
                def batch(it, ahead):
                    if ahead:
                        qd, kd, vd = (A[n][bass.ds(it + 1, 1)] for n in ("q1", "k1", "v1"))
                    od, dd, sd = one(A["o1"], it), one(A["diag"], it), one(A["sums"], it)
                    kept_at = [in_register(sp, it * 8 + 1 + e + 1) for e in range(8)]
                    units_read = [{e: in_register(sp, it * (n * QUADS) + n * (s + 1)) for e, n in MINE.items()} for s in range(QUADS)]
                    for s in range(QUADS):
                        for c in range(2):
                            sp.wait_ge(out_kept, kept_at[2 * s + c])
                            for hq in range(4):
                                sp.dma_start(od[:, 4 * s + hq, :, c * HALF:(c + 1) * HALF].rearrange("a r s -> (a r) s"),
                                             out[VW * hq:VW * hq + DH, c, :]).then_inc(out_stored[c], 16)
                            sp.wait_ge(sums_kept, kept_at[2 * s + c])
                            sp.dma_start(dd[:, s, 4 * c:4 * c + 4, :].rearrange("a t f -> (a t) f"),
                                         diag[0:P:VW, c, :]).then_inc(out_stored[c], 16)
                        sp.wait_ge(unit_read["dve"], units_read[s]["dve"])
                        sp.sem_inc(unit_step, 1)
                        sp.wait_ge(unit_read["act"], units_read[s]["act"])
                        sp.dma_start(sd[:, s, :, :].rearrange("a p u -> (a p) u"), sums[:, s, :]).then_inc(sums_stored[s], 16)
                        if ahead:
                            load(s, qd, kd, vd)

                with sp.Fori(0, B - 1) as it:
                    batch(it, True)
                batch(B - 1, False)
                for s in range(QUADS):
                    sp.wait_ge(sums_stored[s], 16 * B + 1)
                for c in range(2):
                    sp.wait_ge(out_stored[c], 80 * B * QUADS + 1)

            @block.vector
            def _(dve):
                nc.vector.memset(v[:, :, :, :], 0.0).then_inc(q_cleared, 1)
                nc.vector.memset(ones[:, :], 1.0).then_inc(q_cleared, 1)
                nc.vector.memset(q[:, 0], 0.0).then_inc(q_cleared, 1)
                choose(dve)
                for c in range(2):
                    dve.sem_inc(out_stored[c], 1)
                for s in range(QUADS):
                    dve.sem_inc(sums_stored[s], 1)
                dve.wait_ge(loaded, 16)
                with dve.Fori(0, B) as it:
                    for s in range(QUADS):
                        for t in range(NT):
                            n = NT * s + t
                            if t == 0:
                                dve.wait_ge(sums_stored[s], it * 16 + 1)
                            for i in range(PER_TILE * t, PER_TILE * t + PER_TILE):
                                if i == PER_TILE * t + 0:
                                    dve.wait_ge(pt_done, it * (NT * QUADS) + n + 1)
                                    dve.wait_ge(pv_done, it * (NT * QUADS) + n + 1)
                                    nc.vector.tensor_tensor(kept[:, t % DEEP, :].rearrange("p (a b i) -> p a b i", a=2, b=2), pt[t % 2],
                                                            causal[:, None, None, :].broadcast_to((P, 2, 2, P)), ALU.mult).then_inc(masked, 1)
                                if engine_of[i] == "dve":
                                    src, dst = sum_unit(dve, "dve", it, s, i)
                                    nc.vector.tensor_reduce(dst, src, AX.X, ALU.add,
                                                            apply_absolute_value=True).then_inc(unit_read["dve"], 1)

            @block.gpsimd
            def _(pool):
                for s in range(QUADS):
                    if s:
                        nc.gpsimd.memset(q[:, s], 0.0)
                    nc.gpsimd.memset(k[:, s], 0.0).then_inc(k_cleared, 1)
                pool.wait_ge(routes_stored, 16 * 4 * B)
                pool.sem_inc(scatter_step, 1)
                with pool.Fori(0, B) as it:
                    xd = one(A["xn1"], it).rearrange("a (t p) c -> p (a t) c", p=P)
                    for kk in range(2):
                        pool.dma_start(x[:, kk, :, 0:D], xd).then_inc(x_loaded, 16)
                    for dst, src in ((index, "index"), (token, "token")):
                        pool.dma_start(dst[:, :], one(A[src], it).rearrange("a p k -> (a p) k")).then_inc(x_loaded, 16)
                    all_rows = pool.snap(it * (16 * 2 * NT) + 16 * 2 * NT)
                    pool.wait_ge(x_loaded, it * 64 + 64)
                    pool.sem_inc(scatter_step, 1)
                    nc.gpsimd.tensor_copy(x[:, :, :, D], token[:, :].rearrange("p (k t) -> p k t", k=2)).then_inc(scatter_step, 1)
                    pool.wait_ge(scatter_step, it * 4 + 3)
                    pool.sem_inc(scatter_step, 1)
                    for kk in range(2):
                        for t in range(NT):
                            pool.indirect_dma_start(
                                A["slot_x"], bass.IndirectOffsetOnAxis(ap=index[:, kk * NT + t:kk * NT + t + 1], axis=0),
                                x[:, kk, t, :], None, bounds_check=ALL_SLOTS - 1, oob_is_err=False).then_inc(scattered, 16)
                    pool.wait_ge(scattered, all_rows)
                    pool.sem_inc(scatter_step, 1)

            @block.scalar
            def _(act):
                exponentials(act)
                act.sem_inc(pv_done, DEEP)
                act.sem_inc(out_kept, 1)
                act.sem_inc(sums_kept, 1)
                with act.Fori(0, B) as it:
                    def absolute(n):
                        act.wait_ge(masked, it * (NT * QUADS) + n + 1)
                        nc.scalar.activation(absd[:, n % DEEP_ABS, :], kept[:, n % DEEP, :], ACT.Abs).then_inc(abs_done, 1)

                    def keep_outputs(e):
                        act.wait_ge(pv_done, it * (NT * QUADS) + 4 * (e + 1) + DEEP)
                        act.wait_ge(out_stored[e % 2], it * (80 * QUADS) + 80 * (e // 2) + 1)
                        nc.scalar.copy(out[:, e % 2, :], po).then_inc(out_kept, 1)

                    def keep_sums(e):
                        act.wait_ge(sums_done, it * (2 * QUADS) + e + 1)
                        act.wait_ge(out_stored[e % 2], it * (80 * QUADS) + 80 * (e // 2) + 1)
                        nc.scalar.copy(diag[:, e % 2, :], pd).then_inc(sums_kept, 1)

                    for s in range(QUADS):
                        for t in range(NT):
                            n = NT * s + t
                            if t == 0:
                                act.wait_ge(sums_stored[s], it * 16 + 1)
                            for i in range(PER_TILE * t, PER_TILE * t + PER_TILE):
                                if engine_of[i] == "act":
                                    src, dst = sum_unit(act, "act", it, s, i)
                                    nc.scalar.activation(src, src, ACT.Abs, accum_out=dst).then_inc(unit_read["act"], 1)
                                if i == PER_TILE * t + 2 and n:
                                    absolute(n - 1)
                                if i == PER_TILE * t and n > 4:
                                    if t % 4 == 2:
                                        keep_outputs(n // 4 - 1)
                                    if t % 4 == 1 and n > 8:
                                        keep_sums(n // 4 - 2)
                    absolute(QUADS * NT - 1)
                    keep_sums(2 * QUADS - 2)
                    keep_outputs(2 * QUADS - 1)
                    keep_sums(2 * QUADS - 1)

            @block.tensor
            def _(pe):
                pe.wait_ge(q_cleared, 2)
                count_tokens(pe)
                with pe.Fori(0, B) as it:
                    def inside(s, t):
                        n = NT * s + t
                        pe.wait_ge(abs_done, it * (NT * QUADS) + n + 1)
                        if t % 4 == 0:
                            pe.wait_ge(out_kept, it * 8 + n // 4 + 1)
                        c = slice((t % 4) * P, (t % 4) * P + P)
                        for hq in range(4):
                            ins = nc.tensor.matmul(po[VW * hq:VW * hq + VW, c], v[:, s, t, DH * hq:DH * hq + VW],
                                                   kept[:, t % DEEP, hq * P:hq * P + P], start=True, stop=True)
                        ins.then_inc(pv_done, 1)
                        if n >= 3:
                            sums_inside((n - 3) // 4, (n - 3) % 4)

                    def sums_inside(e, hq):
                        if hq == 0:
                            pe.wait_ge(sums_kept, it * 8 + e + 1)
                        c = slice(hq * P, hq * P + P)
                        for x in range(4):
                            ins = nc.tensor.matmul(pd[VW * x:VW * x + VW, c], ones[:, :], absd[:, (4 * e + x) % DEEP_ABS, c],
                                                   start=True, stop=True)
                        if hq == 3:
                            ins.then_inc(sums_done, 1)

                    def diagonal(s, t):
                        n = NT * s + t
                        if t == 0:
                            pe.wait_ge(in_loaded[s], it * LOADS + LOADS)
                        if n:
                            pe.wait_ge(masked, it * (NT * QUADS) + n)
                        ts = slice(t * P, t * P + P)
                        for hq in range(4):
                            ins = nc.tensor.matmul(pt[t % 2][:, hq // 2, hq % 2, :], k[:, s, hq // 2, ts],
                                                   q[:, s, hq, ts], start=True, stop=True)
                        ins.then_inc(pt_done, 1)

                    waiting = []
                    diagonal(0, 0)
                    for s in range(QUADS):
                        for t in range(NT):
                            for i in range(PER_TILE * t, PER_TILE * t + PER_TILE):
                                hq, tq, c = units[order[i]]
                                e = engine_of[i]
                                w = min(HALF, P * tq - HALF * c)
                                n = MINE[e] * s + place_of[i]
                                if n >= 2:
                                    pe.wait_ge(unit_read[e], it * (MINE[e] * QUADS) + n - 1)
                                nc.tensor.matmul(rows[e][n % 2][:, 0:w], q[:, s, hq, tq * P:tq * P + P],
                                                 k[:, s, hq // 2, HALF * c:HALF * c + w], start=True,
                                                 stop=True).then_inc(unit_done[e], 1)
                                if i % PER_TILE == 2 and (s, t) != (QUADS - 1, NT - 1):
                                    diagonal(s + (t + 1) // NT, (t + 1) % NT)
                            waiting.append((s, t))
                            if len(waiting) > LAG:
                                inside(*waiting.pop(0))
                    for n in waiting:
                        inside(*n)
                    for hq in range(1, 4):
                        sums_inside(2 * QUADS - 1, hq)
                    for e in ("act", "dve"):
                        pe.wait_ge(unit_read[e], it * (MINE[e] * QUADS) + MINE[e] * QUADS)


def experts(nc, A):
    PART = SLOTS // 2
    U = 10
    with Space(nc) as m:
        ps = m.psum("psE")
        ident = m.sb("identE", [P, P])
        x, to = m.sb("xE", [P, 2, SLOT_TILES, ROW]), m.sb("toE", [P, 2, SLOT_TILES], I32)
        fc1, fc2 = m.sb("fc1E", [P, 2, FF]), m.sb("fc2E", [P, 2, FC, D])
        b1, b2, ls = m.sb("b1E", [P, 2, FC]), m.sb("b2E", [P, 2, D]), m.sb("lsE", [P, 2, D])
        xT = m.sb("xTE", [P, SLOTS])
        hT = m.sb("hTE", [P, FC, SLOTS])
        y, z = m.sb("yE", [P, SLOT_TILES, D]), m.sb("zE", [P, 2, SLOT_TILES, D])
        scaled = m.sb("scaledE", [P, SLOT_TILES, D])
        inter, intra = m.sb("interE", [P, S]), m.sb("intraE", [P, S])
        sums = m.sb("sumsE", [P, QUADS, U, 4])
        diag = m.sb("diagE", [P, P])
        gate = m.sb("gateE", [P, NT, D])
        outT = m.sb("outTE", [P, S])
        den, rden = m.sb("denE", [P, NT, H]), m.sb("rdenE", [P, NT, H])
        ret, sq = m.sb("retE", [P, NT, D]), m.sb("sqE", [P, NT, D])
        gated = m.sb("gatedE", [P, NT, D])
        ms, rms = m.sb("msE", [P, NT * H]), m.sb("rmsE", [P, NT * H])
        root, square = m.sb("rootE", [P, NT * H]), m.sb("squareE", [P, NT * H])
        loaded = m.sem("constE")
        in_loaded = [m.sem(f"in_loadedE{i}") for i in range(2)]
        turned, xT_ready, h_done, gelu_done = (m.sem(n) for n in ("turnedE", "xT_readyE", "h_doneE", "gelu_doneE"))
        y_done, y_biased, y_scaled, z_ready, step_pool = (m.sem(n) for n in ("y_doneE", "y_biasedE", "y_scaledE", "z_readyE", "step_poolE"))
        sent, z_free = ([m.sem(f"{n}E{i}") for i in range(2)] for n in ("sent", "z_free"))
        ret_loaded, summed, step = (m.sem(n) for n in ("ret_loadedE", "summedE", "stepE"))
        ms_ready, root_ready, gated_ready, ret_stored = (m.sem(n) for n in ("ms_readyE", "root_readyE", "gated_readyE", "ret_storedE"))
        LOADS, RET_LOADS, SENT = 16 * 6, 16 * 5, 16 * SLOT_TILES
        STEPS = 14
        with nc.Block() as block:
            @block.sync
            def _(sp):
                sp.dma_start(ident[:, :], A["ident"]).then_inc(loaded, 16)

                def load(i, src):
                    xd, f1, f2, c1, c2, l = src
                    for dst, s in ((x[:, i], xd), (fc1[:, i, :], f1), (fc2[:, i], f2), (b1[:, i, :], c1), (b2[:, i, :], c2),
                                   (ls[:, i, :], l)):
                        sp.dma_start(dst, s).then_inc(in_loaded[i], 16)

                def sources(sel):
                    return (sel(A["slot_x"].rearrange("(e t p) c -> e p t c", t=SLOT_TILES, p=P)).rearrange("a p t c -> (a p) t c"),
                            sel(A["fc1T"]).rearrange("a c h -> (a c) h"),
                            sel(A["fc2T"]).rearrange("a h q c -> (a h) q c"),
                            sel(A["fc1_b"]).rearrange("a p q -> (a p) q"),
                            sel(A["fc2_b"]).broadcast_to((P, D)), sel(A["ls"]).broadcast_to((P, D)))

                def load_retention(sel):
                    for dst, src in (
                            (inter[:, :], sel(A["inter"]).rearrange("a p s -> (a p) s")),
                            (intra[:, :], sel(A["o1"]).rearrange("a h r s -> (a h r) s")),
                            (sums[:, :, :, :].rearrange("p q u h -> p q (u h)"), sel(A["sums"]).rearrange("a q p u -> p (a q) u")),
                            (diag[:, :], sel(A["diag"]).rearrange("a q t (h i) -> (a q t h) i", h=4)),
                            (gate[:, :, :], sel(A["g1"]).rearrange("a (t p) c -> p (a t) c", p=P))):
                        sp.dma_start(dst, src).then_inc(ret_loaded, 16)

                for i in range(2):
                    load(i, sources(lambda a: a[i:i + 1]))
                load_retention(lambda a: a[0:1])
                def pair(it, ahead):
                    if ahead:
                        later = [sources(lambda a: a[bass.ds(it * 2 + i + 2, 1)]) for i in range(2)]
                    ret_out = one(A["ret"], it).rearrange("a (t p) c -> p (a t) c", p=P)
                    z_at, z_at2 = in_register(sp, it * 2 + 1), in_register(sp, it * 2 + 2)
                    gated_at = in_register(sp, it + 1)
                    if ahead:
                        sp.wait_ge(z_ready, z_at)
                        load(0, later[0])
                    sp.wait_ge(gated_ready, gated_at)
                    sp.dma_start(ret_out, gated[:, :, :]).then_inc(ret_stored, 16)
                    if ahead:
                        load_retention(lambda a: a[bass.ds(it + 1, 1)])
                        sp.wait_ge(z_ready, z_at2)
                        load(1, later[1])

                with sp.Fori(0, NE // 2 - 1) as it:
                    pair(it, True)
                pair(NE // 2 - 1, False)
                sp.wait_ge(ret_stored, 16 * B + 1)

            @block.gpsimd
            def _(pool):
                with pool.Fori(0, NE // 2) as it:
                    all_sent = pool.snap(it * SENT + SENT)
                    for i in range(2):
                        pool.wait_ge(z_ready, it * 2 + i + 1)
                        pool.sem_inc(step_pool, 1)
                        for t in range(SLOT_TILES):
                            pool.indirect_dma_start(A["back"], bass.IndirectOffsetOnAxis(ap=to[:, i, t:t + 1], axis=0),
                                                    z[:, i, t, :], None, bounds_check=2 * N - 1,
                                                    oob_is_err=False).then_inc(sent[i], 16)
                        pool.wait_ge(sent[i], all_sent)
                        pool.sem_inc(z_free[i], 1)

            @block.tensor
            def _(pe):
                pe.wait_ge(loaded, 16)
                with pe.Fori(0, NE // 2) as it:
                    for i in range(2):
                        pe.wait_ge(in_loaded[i], it * LOADS + LOADS)
                        for t in range(SLOT_TILES):
                            ins = nc.tensor.transpose(ps[:, t // 4, (t % 4) * P:(t % 4) * P + P], x[:, i, t, 0:D], ident[:, :])
                        ins.then_inc(turned, 1)
                        pe.wait_ge(xT_ready, it * 2 + i + 1)
                        for c in range(FC):
                            for h in range(2):
                                n = 2 * c + h
                                if n >= 2:
                                    pe.wait_ge(gelu_done, it * (4 * FC) + 2 * FC * i + n - 1)
                                nc.tensor.matmul(ps[:, 2 + n % 2, 0:PART], fc1[:, i, c * P:c * P + P],
                                                 xT[:, h * PART:h * PART + PART], start=True, stop=True).then_inc(h_done, 1)
                        pe.wait_ge(gelu_done, it * (4 * FC) + 2 * FC * (i + 1))
                        pe.wait_ge(y_biased, it * 2 + i + 1)
                        for t in range(SLOT_TILES):
                            for c in range(FC):
                                ins = nc.tensor.matmul(ps[:, 6 + t // 4, (t % 4) * P:(t % 4) * P + P],
                                                       hT[:, c, t * P:t * P + P], fc2[:, i, c, :], start=(c == 0),
                                                       stop=(c == FC - 1))
                        if i == 0:
                            pe.wait_ge(summed, it + 1)
                            for t in range(NT):
                                nc.tensor.transpose(ps[:, 4 + t // 4, (t % 4) * P:(t % 4) * P + P], outT[:, t * P:t * P + P],
                                                    ident[:, :])
                            ins = nc.tensor.transpose(ps[:, 7, 3 * P:4 * P], diag[:, :], ident[:, :])
                        ins.then_inc(y_done, 1)

            @block.scalar
            def _(act):
                with act.Fori(0, NE // 2) as it:
                    for i in range(2):
                        act.wait_ge(turned, it * 2 + i + 1)
                        nc.scalar.copy(xT[:, :], ps[:, 0:2, :].rearrange("p b f -> p (b f)")[:, 0:SLOTS]).then_inc(xT_ready, 1)
                        for c in range(FC):
                            for h in range(2):
                                n = 2 * c + h
                                act.wait_ge(h_done, it * (4 * FC) + 2 * FC * i + n + 1)
                                nc.scalar.activation(hT[:, c, h * PART:h * PART + PART], ps[:, 2 + n % 2, 0:PART], ACT.Gelu,
                                                     bias=b1[:, i, c:c + 1]).then_inc(gelu_done, 1)
                    act.wait_ge(ms_ready, it + 1)
                    nc.scalar.activation(root[:, :], ms[:, :], ACT.Sqrt).then_inc(root_ready, 1)

            @block.vector
            def _(dve):
                V = nc.vector
                for i in range(2):
                    dve.sem_inc(z_free[i], 1)
                dve.sem_inc(ret_stored, 1)
                dve.sem_inc(y_biased, 1)
                with dve.Fori(0, NE // 2) as it:
                    link, count = linker(dve, step, it * STEPS)

                    def expert(i):
                        V.tensor_tensor(y[:, :, :], ps[:, 6:8, :].rearrange("p b (t c) -> p (b t) c", c=D)[:, 0:SLOT_TILES, :],
                                        b2[:, i, None, :].broadcast_to((P, SLOT_TILES, D)), ALU.add).then_inc(y_biased, 1)
                        dve.wait_ge(y_biased, it * 2 + i + 2)
                        V.tensor_tensor(scaled[:, :, :], y[:, :, :], ls[:, i, None, :].broadcast_to((P, SLOT_TILES, D)),
                                        ALU.mult).then_inc(y_scaled, 1)
                        dve.wait_ge(z_free[i], it + 1)
                        V.tensor_copy(to[:, i, :], x[:, i, :, D])
                        dve.wait_ge(y_scaled, it * 2 + i + 1)
                        V.tensor_tensor(z[:, i], scaled[:, :, :], x[:, i, :, 0:D], ALU.add).then_inc(z_ready, 1)

                    dve.wait_ge(ret_loaded, it * RET_LOADS + RET_LOADS)
                    V.tensor_tensor(outT[:, :], inter[:, :], intra[:, :], ALU.add).then_inc(summed, 1)
                    dve.wait_ge(y_done, it * 2 + 1)
                    link(V.tensor_copy(den[:, :, :].rearrange("p t (q h) -> p q t h", h=4),
                                       ps[:, 7, 3 * P:4 * P].rearrange("p (q t h) -> p q t h", q=QUADS, h=4)))
                    expert(0)
                    for c in range(2):
                        for t in range(1 + 4 * c, NT):
                            u = FRONT.index((t, c))
                            d = den[:, t, :].rearrange("p (q h) -> p q h", h=4)
                            ins = V.tensor_tensor(d, d, sums[:, :, u, :], ALU.add)
                        link(ins)
                    link(V.tensor_scalar(den[:, :, :], den[:, :, :], 1.0, 50000.0, ALU.max, ALU.min))
                    link(V.reciprocal(rden[:, :, :], den[:, :, :]))
                    for b in range(2):
                        t4 = slice(4 * b, 4 * b + 4)
                        ins = V.tensor_tensor(ret[:, t4, :].rearrange("p t (h d) -> p (t h) d", d=DH),
                                              ps[:, 4 + b, :].rearrange("p (g d) -> p g d", d=DH),
                                              rden[:, t4, :].rearrange("p t h -> p (t h)")[:, :, None].broadcast_to((P, 4 * H, DH)),
                                              ALU.mult)
                    link(ins)
                    link(V.tensor_tensor(sq[:, :, :], ret[:, :, :], ret[:, :, :], ALU.mult))
                    link(V.tensor_reduce(ms[:, :], sq[:, :, :].rearrange("p t (h d) -> p (t h) d", d=DH), AX.X, ALU.add))
                    V.tensor_scalar(ms[:, :], ms[:, :], 1.0 / DH, RMS_EPS, ALU.mult, ALU.add).then_inc(ms_ready, 1)
                    dve.wait_ge(root_ready, it + 1)
                    link(V.reciprocal(rms[:, :], root[:, :]))
                    link(V.tensor_tensor(square[:, :], rms[:, :], rms[:, :], ALU.mult))
                    link(V.tensor_tensor(square[:, :], square[:, :], ms[:, :], ALU.mult))
                    link(V.tensor_scalar(square[:, :], square[:, :], -0.5, 1.5, ALU.mult, ALU.add))
                    link(V.tensor_tensor(rms[:, :], rms[:, :], square[:, :], ALU.mult))
                    r3 = ret[:, :, :].rearrange("p t (h d) -> p (t h) d", d=DH)
                    link(V.tensor_tensor(r3, r3, rms[:, :, None].broadcast_to((P, NT * H, DH)), ALU.mult))
                    dve.wait_ge(ret_stored, it * 16 + 1)
                    V.tensor_tensor(gated[:, :, :], ret[:, :, :], gate[:, :, :], ALU.mult).then_inc(gated_ready, 1)
                    assert count[0] == STEPS
                    dve.wait_ge(y_done, it * 2 + 2)
                    expert(1)


def finish(nc, A):
    with Space(nc) as m:
        ret, x1 = m.sb("retF", [P, 2, NT, D]), m.sb("x1F", [P, 2, NT, D])
        weight = m.sb("weightF", [P, 2, 2 * NT])
        rows = m.sb("rowsF", [P, 2, 2, NT, D])
        first, moe, gate = (m.sb(n, [P, 2, NT, D]) for n in ("firstF", "moeF", "gateF"))
        prod, res = m.sb("prodF", [P, 2, NT, D]), m.sb("resF", [P, 2, NT, D])
        first_ready, moe_ready, silued, prod_ready, done, stored = (
            m.sem(n) for n in ("first_readyF", "moe_readyF", "siluedF", "prod_readyF", "doneF", "storedF"))
        in_loaded = [m.sem(f"in_loadedF{i}") for i in range(2)]
        LOADS = 16 * 5
        with nc.Block() as block:
            @block.sync
            def _(sp):
                def load(i, sel):
                    for kk in range(2):
                        back = sel(A["back"][kk * N:(kk + 1) * N, :].rearrange("(b t p) c -> b p t c", t=NT, p=P))
                        sp.dma_start(rows[:, i, kk], back.rearrange("a p t c -> (a p) t c")).then_inc(in_loaded[i], 16)
                    for dst, src in ((ret[:, i], sel(A["ret"]).rearrange("a (t p) c -> p (a t) c", p=P)),
                                     (x1[:, i], sel(A["x1"]).rearrange("a (t p) c -> p (a t) c", p=P)),
                                     (weight[:, i, :], sel(A["weight"]).rearrange("a p k -> (a p) k"))):
                        sp.dma_start(dst, src).then_inc(in_loaded[i], 16)

                for i in range(2):
                    load(i, lambda a: a[i:i + 1])
                def pair(it, ahead):
                    out = [A["out"][bass.ds(it * 2 + i, 1)].rearrange("a (t p) c -> p (a t) c", p=P) for i in range(2)]
                    done_at = [in_register(sp, it * 2 + i + 1) for i in range(2)]
                    for i in range(2):
                        sp.wait_ge(done, done_at[i])
                        sp.dma_start(out[i], res[:, i]).then_inc(stored, 16)
                        if ahead:
                            load(i, lambda a: a[bass.ds(it * 2 + 2 + i, 1)])

                with sp.Fori(0, B // 2 - 1) as it:
                    pair(it, True)
                pair(B // 2 - 1, False)
                sp.wait_ge(stored, 16 * B + 1)

            @block.scalar
            def _(act):
                with act.Fori(0, B // 2) as it:
                    for i in range(2):
                        act.wait_ge(moe_ready, it * 2 + i + 1)
                        nc.scalar.activation(gate[:, i], moe[:, i], ACT.Silu).then_inc(silued, 1)

            @block.vector
            def _(dve):
                V = nc.vector
                dve.sem_inc(stored, 1)
                with dve.Fori(0, B // 2) as it:
                    for i in range(2):
                        dve.wait_ge(in_loaded[i], it * LOADS + LOADS)
                        for t in range(NT):
                            V.tensor_scalar(first[:, i, t, :], rows[:, i, 0, t, :], weight[:, i, t:t + 1], None,
                                            ALU.mult).then_inc(first_ready, 1)
                        for t in range(NT):
                            dve.wait_ge(first_ready, it * (2 * NT) + NT * i + t + 1)
                            ins = V.scalar_tensor_tensor(moe[:, i, t, :], rows[:, i, 1, t, :], weight[:, i, NT + t:NT + t + 1],
                                                         first[:, i, t, :], ALU.mult, ALU.add)
                        ins.then_inc(moe_ready, 1)
                        dve.wait_ge(silued, it * 2 + i + 1)
                        V.tensor_tensor(prod[:, i], ret[:, i], gate[:, i], ALU.mult).then_inc(prod_ready, 1)
                        dve.wait_ge(prod_ready, it * 2 + i + 1)
                        dve.wait_ge(stored, it * 32 + 1)
                        V.tensor_tensor(res[:, i], prod[:, i], x1[:, i], ALU.add).then_inc(done, 1)


def program(nc, A):
    project_and_ffn(nc, A)
    attention(nc, A)
    between_layers(nc, A)
    retention(nc, A)
    experts(nc, A)
    finish(nc, A)


def constants():
    bf16 = mybir.dt.np(BF16)
    f = np.float64
    i = np.arange(S, dtype=f)
    d = np.arange(DH)
    sign = np.where(d % 2 == 0, -1.0, 1.0)
    ang0 = np.minimum(i, 255)[:, None] * (10000.0 ** (-2.0 * (d // 2) / DH))[None, :]
    rows = lambda a: np.tile(a.T, (H, 1))
    ang1 = i[:, None] * np.repeat(1.0 / 10000.0 ** np.linspace(0.0, 1.0, DH // 2), 2)[None, :]
    decay = np.log(1.0 - 2.0 ** (-5.0 - np.arange(H, dtype=f)))
    norm = 1.0 / np.sqrt(np.cumsum(np.exp(decay[:, None] * i[None, :]), axis=1))
    qs = np.repeat(np.exp(decay[:, None] * i) * norm, DH, axis=0)
    ks = np.repeat(np.exp(-decay[:, None] * i) * D ** -0.5, DH, axis=0)
    cos1, sin1 = rows(np.cos(ang1)), rows(np.sin(ang1) * sign)
    p = np.arange(P)
    pick = np.zeros((P, 8, P))
    for j in range(8):
        pick[2 * j + 1, j, :] = 1.0
    behind = np.where(p[None, :] > p[:, None], MASKED, 0.0)
    return {
        "ident": np.eye(P, dtype=np.float32), "identb": np.eye(P).astype(bf16),
        "mask_ij": behind.astype(bf16), "mask_ji": behind.T.astype(bf16).copy(),
        "cos0": rows(np.cos(ang0)).astype(np.float32), "sin0": rows(np.sin(ang0) * sign).astype(np.float32),
        "tables1": np.stack([cos1 * qs, sin1 * qs, cos1 * ks, sin1 * ks], axis=1).astype(np.float32),
        "pick": pick.astype(np.float32),
        "same_head": (p[:, None] // DH == p[None, :] // DH).astype(np.float32),
        "causal": (p[None, :] >= p[:, None]).astype(np.float32),
        "before": (p[:, None] < p[None, :]).astype(bf16),
        "token": (np.arange(2)[None, None, :, None] * N + np.arange(B)[:, None, None, None] * S
                  + np.arange(NT)[None, None, None, :] * P + p[None, :, None, None]).reshape(B, P, 2 * NT).astype(np.float32),
        "rank": (NE - np.arange(NE, dtype=np.float32))[None, :],
    }


def layouts(inp):
    t = {k: np.ascontiguousarray(np.asarray(v)) for k, v in inp.items()}
    swap = np.arange(D) ^ 1
    chunks = lambda w: np.ascontiguousarray(w.T.reshape(FC, P, -1).transpose(1, 0, 2))
    x = t["L0_attn_in_features"]
    wq, wk, wv = (t["L0_attn_W_" + n].T for n in "qkv")
    q1, k1, v1, g1 = (t["L1_attn_W" + n] for n in "qkvg")
    return {
        "x": x,
        "w_proj0": np.stack([wq, wq[:, swap], wk, wk[:, swap], wv], axis=1),
        "w1T": t["L0_ffn_W1"].T, "w2T": chunks(t["L0_ffn_W2"]),
        "b1c": t["L0_ffn_b1"].reshape(FC, P).T, "b2": t["L0_ffn_b2"][None, :],
        "scale": t["L0_ffn_scale"].reshape(1, 1),
        "w_outT": t["L0_attn_W_o"].T,
        "w_proj1": np.stack([q1, q1[:, swap], k1, k1[:, swap]], axis=1), "w_vg1": np.stack([v1, g1], axis=1),
        "w_routerT": t["L1_ffn_router_w"].T, "b_router": t["L1_ffn_router_b"][None, :],
        "fc1T": t["L1_ffn_fc1_w"].transpose(0, 2, 1),
        "fc2T": t["L1_ffn_fc2_w"].transpose(0, 2, 1).reshape(NE, FC, P, D).transpose(0, 2, 1, 3),
        "fc1_b": t["L1_ffn_fc1_b"].reshape(NE, FC, P).transpose(0, 2, 1),
        "fc2_b": t["L1_ffn_fc2_b"], "ls": t["L1_ffn_layer_scale"],
    }


SCRATCH = {
    "q0": ([B, H, ROWS0, S], BF16), "k0": ([B, H, ROWS0, S], BF16), "v0": ([B, P, NT * H * VW], F32),
    "u": ([B + 1, S, D], F32), "o0": ([B, H, 2 * DH, S], F32), "rden": ([B, H, S], F32),
    "x1": ([B, S, D], F32), "xn1": ([B, S, D], F32), "v1": ([B, S, D], F32), "g1": ([B, S, D], F32),
    "logits": ([B, P, NT * NE], F32), "inter": ([B, P, S], F32),
    "q1": ([B, H, AUG, S], BF16), "k1": ([B, H, AUG, S], BF16),
    "o1": ([B, H, DH, S], F32), "diag": ([B, QUADS, NT, 4 * P], F32), "sums": ([B, QUADS, P, 40], F32), "ret": ([B, S, D], F32),
    "index": ([B, P, 2 * NT], I32), "weight": ([B, P, 2 * NT], F32),
    "slot_x": ([ALL_SLOTS, ROW], F32), "back": ([2 * N, D], F32),
}


def build(nc, arrays):
    A = {n: nc.dram_tensor(n, a.shape, mybir.dt.from_np(a.dtype), kind="ExternalInput").ap() for n, a in arrays.items()}
    for n, (shape, dt) in SCRATCH.items():
        A[n] = nc.dram_tensor(n, shape, dt).ap()
    A["out"] = nc.dram_tensor("out", (B, S, D), F32, kind="ExternalOutput").ap()
    program(nc, A)


def kernel(**inputs):
    import concourse.bacc as bacc
    from concourse.bass_utils import run_bass_kernel_spmd as run

    nc = bacc.Bacc("TRN2", target_bir_lowering=False, num_devices=1)
    arrays = {n: np.ascontiguousarray(a) for n, a in {**constants(), **layouts(inputs)}.items()}
    build(nc, arrays)
    r = run(nc, [arrays], core_ids=[0])
    return r.results[0]["out"]
```
